# Optimizing a Trainium2 kernel written in Bass

```python
import numpy as np
import jax
import jax.numpy as jnp

def _softmax(x, axis=-1):
    return jax.nn.softmax(x, axis=axis)

def _gelu(x):
    return jax.nn.gelu(x, approximate=True)

def _silu(x):
    return jax.nn.silu(x)

def _sigmoid(x):
    return jax.nn.sigmoid(x)

def _layernorm(x, axis=-1, eps=1e-05):
    m = jnp.mean(x, axis=axis, keepdims=True)
    v = jnp.var(x, axis=axis, keepdims=True)
    return (x - m) / jnp.sqrt(v + eps)

def _scatter_add(tgt, idx, src, axis=0):
    return tgt.at[idx].add(src)

def _segment_sum(src, seg, n):
    return jax.ops.segment_sum(src, seg, n)
kernel_name = 'mk_seq_preln_d2_jaxref_r8_f43075'

def setup_inputs(seed: int=0):
    np.random.seed(seed)
    _w = jnp.asarray

    def _L0_attn_setup():
        import jax, jax.numpy as jnp
        import numpy as np
        B, L, D = (2, 256, 128)
        H = 16
        DH = D // H

        def rope_tables(seq_len, dim):
            inv_freq = 1.0 / 10000.0 ** (jnp.arange(0, dim, 2, dtype=jnp.float32) / dim)
            t = jnp.arange(seq_len, dtype=jnp.float32)
            freqs = jnp.outer(t, inv_freq)
            emb = jnp.concatenate([freqs, freqs], -1)
            return (jnp.cos(emb), jnp.sin(emb))

        def rotate_half(x):
            x1, x2 = (x[..., :x.shape[-1] // 2], x[..., x.shape[-1] // 2:])
            return jnp.concatenate([-x2, x1], axis=-1)
        key = jax.random.key(seed)
        k1, k2, k3 = jax.random.split(key, 3)
        x = jax.random.normal(k1, (B, L, D), dtype=jnp.float32)
        Wqkv = jax.random.normal(k2, (D, 3 * D), dtype=jnp.float32) / np.sqrt(D)
        Wo = jax.random.normal(k3, (D, D), dtype=jnp.float32) / np.sqrt(D)
        return {'x': x, 'Wqkv': Wqkv, 'Wo': Wo}
    _L0_attn_in = _L0_attn_setup()

    def _L0_ffn_setup():
        import jax, jax.numpy as jnp
        import numpy as np
        H, I, E_ROUTED, TOP_K = (128, 352, 7, 2)
        B, S = (4, 256)

        def _expert(h, g, u, d):
            return jnp.einsum('...i,hi->...h', jax.nn.silu(h @ g.T) * (h @ u.T), d)
        key = jax.random.key(seed)
        ks = jax.random.split(key, 10)
        sc = 0.02
        return {'x': jax.random.normal(ks[0], (B, S, H), dtype=jnp.float32), 'sg': jax.random.normal(ks[1], (I, H), dtype=jnp.float32) * sc, 'su': jax.random.normal(ks[2], (I, H), dtype=jnp.float32) * sc, 'sd': jax.random.normal(ks[3], (H, I), dtype=jnp.float32) * sc, 'rg': jax.random.normal(ks[4], (E_ROUTED, I, H), dtype=jnp.float32) * sc, 'ru': jax.random.normal(ks[5], (E_ROUTED, I, H), dtype=jnp.float32) * sc, 'rd': jax.random.normal(ks[6], (E_ROUTED, H, I), dtype=jnp.float32) * sc, 'wr': jax.random.normal(ks[7], (E_ROUTED, H), dtype=jnp.float32) * sc, 'rb': jnp.zeros((E_ROUTED,), dtype=jnp.float32)}
    _L0_ffn_in = _L0_ffn_setup()

    def _L1_attn_setup():
        import jax, jax.numpy as jnp
        import numpy as np
        H = 128
        NH = 16
        HD = H // NH
        EPS = 1e-05

        def _attn_block(x, ln_gamma, ln_beta, W_qkv, b_qkv, W_out, b_out):
            B, S, _ = x.shape
            mu = jnp.mean(x, axis=-1, keepdims=True)
            var = jnp.mean(jnp.square(x - mu), axis=-1, keepdims=True)
            xn = (x - mu) / jnp.sqrt(var + EPS) * ln_gamma + ln_beta
            qkv = jnp.einsum('bsh,oh->bso', xn, W_qkv) + b_qkv
            qkv = qkv.reshape(B, S, 3, NH, HD).transpose(2, 0, 3, 1, 4)
            q, k, v = (qkv[0], qkv[1], qkv[2])
            scores = jnp.einsum('bhqd,bhkd->bhqk', q, k) / jnp.sqrt(jnp.asarray(HD, x.dtype))
            probs = jax.nn.softmax(scores, axis=-1)
            ctx = jnp.einsum('bhqk,bhkd->bhqd', probs, v)
            ctx = ctx.transpose(0, 2, 1, 3).reshape(B, S, H)
            out = jnp.einsum('bsh,oh->bso', ctx, W_out) + b_out
            return x + out
        key = jax.random.key(seed)
        ks = jax.random.split(key, 5)
        b_qkv = float(np.sqrt(6.0 / (H + 3 * H)))
        b_out = float(np.sqrt(6.0 / (H + H)))
        return {'hidden_states': jax.random.normal(ks[0], (2, 256, H), dtype=jnp.float32), 'ln_gamma': jnp.ones((H,), jnp.float32), 'ln_beta': jnp.zeros((H,), jnp.float32), 'W_qkv': jax.random.uniform(ks[1], (3 * H, H), jnp.float32, -b_qkv, b_qkv), 'b_qkv': jnp.zeros((3 * H,), jnp.float32), 'W_out': jax.random.uniform(ks[2], (H, H), jnp.float32, -b_out, b_out), 'b_out': jnp.zeros((H,), jnp.float32)}
    _L1_attn_in = _L1_attn_setup()

    def _L1_ffn_setup():
        import jax, jax.numpy as jnp
        import numpy as np
        D = 128
        H = 16
        HD = D // H
        E = 32
        ES = 128
        K = 4
        B, S = (2, 128)
        ROPE_BASE = 10000.0

        def _layernorm(x, g, b):
            m = x.mean(-1, keepdims=True)
            v = ((x - m) ** 2).mean(-1, keepdims=True)
            return (x - m) * jax.lax.rsqrt(v + 1e-05) * g + b

        def _forward(src, wq, wk, wv, wp, wo, ln1_g, ln1_b, ln2_g, ln2_b, sel_w, keys, values):
            Bs, Ss, Ds = src.shape
            scale = 1.0 / jnp.sqrt(jnp.array(HD, dtype=src.dtype))
            x = _layernorm(src, ln1_g, ln1_b)
            q = (x @ wq).reshape(Bs, Ss, H, HD)
            k = (x @ wk).reshape(Bs, Ss, H, HD)
            v = (x @ wv).reshape(Bs, Ss, H, HD)
            pos = jnp.arange(Ss - 1, -Ss, -1, dtype=src.dtype)
            inv_freq = 1.0 / ROPE_BASE ** (jnp.arange(0, Ds, 2, dtype=src.dtype) / Ds)
            ang = pos[:, None] * inv_freq[None, :]
            pe = jnp.concatenate([jnp.sin(ang), jnp.cos(ang)], axis=-1)
            p = (pe @ wp).reshape(2 * Ss - 1, H, HD)
            ac = jnp.einsum('bihd,bjhd->bhij', q, k)
            bd_full = jnp.einsum('bihd,phd->bhip', q, p)
            rel = jnp.arange(Ss)[:, None] - jnp.arange(Ss)[None, :] + (Ss - 1)
            bd = bd_full[:, :, jnp.arange(Ss)[:, None], rel]
            att = jax.nn.softmax((ac + bd) * scale, axis=-1)
            attn_out = jnp.einsum('bhij,bjhd->bihd', att, v).reshape(Bs, Ss, Ds) @ wo
            src = src + attn_out
            x2 = _layernorm(src, ln2_g, ln2_b)
            sel = jax.nn.sigmoid(x2 @ sel_w)
            scores, idx = jax.lax.top_k(sel, K)
            gate = (jax.nn.one_hot(idx, E, dtype=sel.dtype) * scores[..., None]).sum(-2)
            h = jax.nn.relu(jnp.einsum('bsd,edh->bseh', x2, keys))
            moe_out = jnp.einsum('bseh,ehd,bse->bsd', h, values, gate)
            return src + moe_out
        key = jax.random.key(seed)
        ks = jax.random.split(key, 10)
        std_scale = np.sqrt(2.0 / 18)
        w_std = std_scale / np.sqrt(D)
        return {'src': jax.random.normal(ks[0], (B, S, D), jnp.float32), 'wq': jax.random.normal(ks[1], (D, H * HD), jnp.float32) * w_std, 'wk': jax.random.normal(ks[2], (D, H * HD), jnp.float32) * w_std, 'wv': jax.random.normal(ks[3], (D, H * HD), jnp.float32) * w_std, 'wp': jax.random.normal(ks[4], (D, H * HD), jnp.float32) * w_std, 'wo': jax.random.normal(ks[5], (H * HD, D), jnp.float32) * w_std, 'ln1_g': jnp.ones((D,), jnp.float32), 'ln1_b': jnp.zeros((D,), jnp.float32), 'ln2_g': jnp.ones((D,), jnp.float32), 'ln2_b': jnp.zeros((D,), jnp.float32), 'sel_w': jax.random.normal(ks[6], (D, E), jnp.float32) / np.sqrt(D), 'keys': jax.random.normal(ks[7], (E, D, ES), jnp.float32) * w_std, 'values': jax.random.normal(ks[8], (E, ES, D), jnp.float32) * (std_scale / np.sqrt(ES))}
    _L1_ffn_in = _L1_ffn_setup()
    _d = {'L0_attn_x': _L0_attn_in['x'], 'L0_attn_Wqkv': _L0_attn_in['Wqkv'], 'L0_attn_Wo': _L0_attn_in['Wo'], 'L0_ffn_sg': _L0_ffn_in['sg'], 'L0_ffn_su': _L0_ffn_in['su'], 'L0_ffn_sd': _L0_ffn_in['sd'], 'L0_ffn_rg': _L0_ffn_in['rg'], 'L0_ffn_ru': _L0_ffn_in['ru'], 'L0_ffn_rd': _L0_ffn_in['rd'], 'L0_ffn_wr': _L0_ffn_in['wr'], 'L0_ffn_rb': _L0_ffn_in['rb'], 'L1_attn_ln_gamma': _L1_attn_in['ln_gamma'], 'L1_attn_ln_beta': _L1_attn_in['ln_beta'], 'L1_attn_W_qkv': _L1_attn_in['W_qkv'], 'L1_attn_b_qkv': _L1_attn_in['b_qkv'], 'L1_attn_W_out': _L1_attn_in['W_out'], 'L1_attn_b_out': _L1_attn_in['b_out'], 'L1_ffn_wq': _L1_ffn_in['wq'], 'L1_ffn_wk': _L1_ffn_in['wk'], 'L1_ffn_wv': _L1_ffn_in['wv'], 'L1_ffn_wp': _L1_ffn_in['wp'], 'L1_ffn_wo': _L1_ffn_in['wo'], 'L1_ffn_ln1_g': _L1_ffn_in['ln1_g'], 'L1_ffn_ln1_b': _L1_ffn_in['ln1_b'], 'L1_ffn_ln2_g': _L1_ffn_in['ln2_g'], 'L1_ffn_ln2_b': _L1_ffn_in['ln2_b'], 'L1_ffn_sel_w': _L1_ffn_in['sel_w'], 'L1_ffn_keys': _L1_ffn_in['keys'], 'L1_ffn_values': _L1_ffn_in['values']}
    _x0 = _d['L0_attn_x']
    _d['L0_attn_x'] = jax.random.normal(jax.random.fold_in(jax.random.key(seed), 1), (2, 1024, 128), dtype=_x0.dtype)
    del _x0
    return _d

def reference(L0_attn_x, L0_attn_Wqkv, L0_attn_Wo, L0_ffn_sg, L0_ffn_su, L0_ffn_sd, L0_ffn_rg, L0_ffn_ru, L0_ffn_rd, L0_ffn_wr, L0_ffn_rb, L1_attn_ln_gamma, L1_attn_ln_beta, L1_attn_W_qkv, L1_attn_b_qkv, L1_attn_W_out, L1_attn_b_out, L1_ffn_wq, L1_ffn_wk, L1_ffn_wv, L1_ffn_wp, L1_ffn_wo, L1_ffn_ln1_g, L1_ffn_ln1_b, L1_ffn_ln2_g, L1_ffn_ln2_b, L1_ffn_sel_w, L1_ffn_keys, L1_ffn_values):

    def _L0_attn_ref(x, Wqkv, Wo):
        import jax, jax.numpy as jnp
        import numpy as np
        B, L, D = (2, 256, 128)
        H = 16
        DH = D // H

        def rope_tables(seq_len, dim):
            inv_freq = 1.0 / 10000.0 ** (jnp.arange(0, dim, 2, dtype=jnp.float32) / dim)
            t = jnp.arange(seq_len, dtype=jnp.float32)
            freqs = jnp.outer(t, inv_freq)
            emb = jnp.concatenate([freqs, freqs], -1)
            return (jnp.cos(emb), jnp.sin(emb))

        def rotate_half(x):
            x1, x2 = (x[..., :x.shape[-1] // 2], x[..., x.shape[-1] // 2:])
            return jnp.concatenate([-x2, x1], axis=-1)
        b, l, d = x.shape
        qkv = (x @ Wqkv).reshape(b, l, 3, H, DH)
        q, k, v = (qkv[:, :, 0], qkv[:, :, 1], qkv[:, :, 2])
        cos, sin = rope_tables(l, DH)
        cos = cos[:, None, :]
        sin = sin[:, None, :]
        q = q * cos + rotate_half(q) * sin
        k = k * cos + rotate_half(k) * sin
        scale = DH ** (-0.5)
        scores = jnp.einsum('bqhd,bkhd->bhqk', q, k) * scale
        attn = jax.nn.softmax(scores, axis=-1)
        out = jnp.einsum('bhqk,bkhd->bqhd', attn, v)
        out = out.reshape(b, l, d)
        return out @ Wo

    def _L0_ffn_ref(x, sg, su, sd, rg, ru, rd, wr, rb):
        import jax, jax.numpy as jnp
        import numpy as np
        H, I, E_ROUTED, TOP_K = (128, 352, 7, 2)
        B, S = (4, 256)

        def _expert(h, g, u, d):
            return jnp.einsum('...i,hi->...h', jax.nn.silu(h @ g.T) * (h @ u.T), d)
        shared_out = _expert(x, sg, su, sd)
        logits = x @ wr.T + rb
        probs = jax.nn.softmax(logits, axis=-1)
        scores, idx = jax.lax.top_k(probs, TOP_K)
        scores = scores / scores.sum(axis=-1, keepdims=True)
        w = jnp.sum(scores[..., None] * jax.nn.one_hot(idx, E_ROUTED, dtype=x.dtype), axis=-2)
        out = shared_out
        for e in range(E_ROUTED):
            out = out + w[..., e:e + 1] * _expert(x, rg[e], ru[e], rd[e])
        return out

    def _L1_attn_ref(hidden_states, ln_gamma, ln_beta, W_qkv, b_qkv, W_out, b_out):
        import jax, jax.numpy as jnp
        import numpy as np
        H = 128
        NH = 16
        HD = H // NH
        EPS = 1e-05

        def _attn_block(x, ln_gamma, ln_beta, W_qkv, b_qkv, W_out, b_out):
            B, S, _ = x.shape
            mu = jnp.mean(x, axis=-1, keepdims=True)
            var = jnp.mean(jnp.square(x - mu), axis=-1, keepdims=True)
            xn = (x - mu) / jnp.sqrt(var + EPS) * ln_gamma + ln_beta
            qkv = jnp.einsum('bsh,oh->bso', xn, W_qkv) + b_qkv
            qkv = qkv.reshape(B, S, 3, NH, HD).transpose(2, 0, 3, 1, 4)
            q, k, v = (qkv[0], qkv[1], qkv[2])
            scores = jnp.einsum('bhqd,bhkd->bhqk', q, k) / jnp.sqrt(jnp.asarray(HD, x.dtype))
            probs = jax.nn.softmax(scores, axis=-1)
            ctx = jnp.einsum('bhqk,bhkd->bhqd', probs, v)
            ctx = ctx.transpose(0, 2, 1, 3).reshape(B, S, H)
            out = jnp.einsum('bsh,oh->bso', ctx, W_out) + b_out
            return x + out
        return _attn_block(hidden_states, ln_gamma, ln_beta, W_qkv, b_qkv, W_out, b_out)

    def _L1_ffn_ref(src, wq, wk, wv, wp, wo, ln1_g, ln1_b, ln2_g, ln2_b, sel_w, keys, values):
        import jax, jax.numpy as jnp
        import numpy as np
        D = 128
        H = 16
        HD = D // H
        E = 32
        ES = 128
        K = 4
        B, S = (2, 128)
        ROPE_BASE = 10000.0

        def _layernorm(x, g, b):
            m = x.mean(-1, keepdims=True)
            v = ((x - m) ** 2).mean(-1, keepdims=True)
            return (x - m) * jax.lax.rsqrt(v + 1e-05) * g + b

        def _forward(src, wq, wk, wv, wp, wo, ln1_g, ln1_b, ln2_g, ln2_b, sel_w, keys, values):
            Bs, Ss, Ds = src.shape
            scale = 1.0 / jnp.sqrt(jnp.array(HD, dtype=src.dtype))
            x = _layernorm(src, ln1_g, ln1_b)
            q = (x @ wq).reshape(Bs, Ss, H, HD)
            k = (x @ wk).reshape(Bs, Ss, H, HD)
            v = (x @ wv).reshape(Bs, Ss, H, HD)
            pos = jnp.arange(Ss - 1, -Ss, -1, dtype=src.dtype)
            inv_freq = 1.0 / ROPE_BASE ** (jnp.arange(0, Ds, 2, dtype=src.dtype) / Ds)
            ang = pos[:, None] * inv_freq[None, :]
            pe = jnp.concatenate([jnp.sin(ang), jnp.cos(ang)], axis=-1)
            p = (pe @ wp).reshape(2 * Ss - 1, H, HD)
            ac = jnp.einsum('bihd,bjhd->bhij', q, k)
            bd_full = jnp.einsum('bihd,phd->bhip', q, p)
            rel = jnp.arange(Ss)[:, None] - jnp.arange(Ss)[None, :] + (Ss - 1)
            bd = bd_full[:, :, jnp.arange(Ss)[:, None], rel]
            att = jax.nn.softmax((ac + bd) * scale, axis=-1)
            attn_out = jnp.einsum('bhij,bjhd->bihd', att, v).reshape(Bs, Ss, Ds) @ wo
            src = src + attn_out
            x2 = _layernorm(src, ln2_g, ln2_b)
            sel = jax.nn.sigmoid(x2 @ sel_w)
            scores, idx = jax.lax.top_k(sel, K)
            gate = (jax.nn.one_hot(idx, E, dtype=sel.dtype) * scores[..., None]).sum(-2)
            h = jax.nn.relu(jnp.einsum('bsd,edh->bseh', x2, keys))
            moe_out = jnp.einsum('bseh,ehd,bse->bsd', h, values, gate)
            return src + moe_out
        return _forward(src, wq, wk, wv, wp, wo, ln1_g, ln1_b, ln2_g, ln2_b, sel_w, keys, values)
    x = L0_attn_x
    x = x + _L0_attn_ref(_layernorm(x, axis=-1), L0_attn_Wqkv, L0_attn_Wo)
    x = x + _L0_ffn_ref(_layernorm(x, axis=-1), L0_ffn_sg, L0_ffn_su, L0_ffn_sd, L0_ffn_rg, L0_ffn_ru, L0_ffn_rd, L0_ffn_wr, L0_ffn_rb)
    x = x + _L1_attn_ref(_layernorm(x, axis=-1), L1_attn_ln_gamma, L1_attn_ln_beta, L1_attn_W_qkv, L1_attn_b_qkv, L1_attn_W_out, L1_attn_b_out)
    x = x + _L1_ffn_ref(_layernorm(x, axis=-1), L1_ffn_wq, L1_ffn_wk, L1_ffn_wv, L1_ffn_wp, L1_ffn_wo, L1_ffn_ln1_g, L1_ffn_ln1_b, L1_ffn_ln2_g, L1_ffn_ln2_b, L1_ffn_sel_w, L1_ffn_keys, L1_ffn_values)
    return x

_drawn_inputs = setup_inputs


def setup_inputs(seed=0):
    import zlib

    import numpy as np

    out = dict(_drawn_inputs(seed))
    spreads = {'L0_ffn_rb': (0.0, 0.8),
     'L1_attn_ln_gamma': (1.0, 0.6),
     'L1_attn_ln_beta': (0.0, 0.1),
     'L1_attn_b_qkv': (0.0, 0.1),
     'L1_attn_b_out': (0.0, 0.1),
     'L1_ffn_ln1_g': (1.0, 0.6),
     'L1_ffn_ln1_b': (0.0, 0.8),
     'L1_ffn_ln2_g': (1.0, 0.6),
     'L1_ffn_ln2_b': (0.0, 2.0)}
    factors = {'L0_ffn_sg': 5.008,
     'L0_ffn_su': 4.804,
     'L0_ffn_sd': 4.828,
     'L0_ffn_rg': 7.212,
     'L0_ffn_ru': 7.262,
     'L0_ffn_rd': 7.285,
     'L0_ffn_wr': 8.0,
     'L1_ffn_wq': 8.0,
     'L1_ffn_wk': 8.0,
     'L1_ffn_wv': 7.713,
     'L1_ffn_wp': 8.0,
     'L1_ffn_wo': 6.72,
     'L1_ffn_sel_w': 3.405,
     'L1_ffn_keys': 3.794,
     'L1_ffn_values': 3.166}
    for name, (base, spread) in spreads.items():
        noise = np.random.default_rng([zlib.crc32(name.encode()), seed]).standard_normal(out[name].shape)
        drawn = base * np.exp(spread * noise) if base else spread * noise
        out[name] = jnp.asarray(drawn.astype(out[name].dtype))
    for name, factor in factors.items():
        out[name] = (out[name] * factor).astype(out[name].dtype)
    return out
```

```python
from contextlib import ExitStack, contextmanager

import numpy as np

import concourse.bass as bass
from concourse import mybir
from concourse.alu_op_type import AluOpType as ALU

F32 = mybir.dt.float32
BF16 = mybir.dt.bfloat16
ACT = mybir.ActivationFunctionType
AX = mybir.AxisListType

P = 128
NB, L = 2, 1024
H, DH = 16, 8
NH = NB * H
TT = NB * L // P
GT, GW = 4, 512
NG = TT // GT
QT = L // P
EPS = 1e-5
SCALE = DH ** -0.5
PARTS = 3
STACK = PARTS * PARTS * DH
ROWS = 96
VC = 32
NE0, FI = 8, 352
FCH = [(0, 128), (128, 128), (256, 96)]
NE1 = 32
SLOTS = 4


def tables():
    t = np.arange(L, dtype=np.float32)
    inv = (1.0 / 10000.0 ** (np.arange(0, DH, 2, dtype=np.float32) / DH)).astype(np.float32)
    ang = (t[:, None] * inv[None, :]).astype(np.float32)
    ang = np.tile(np.concatenate([ang, ang], 1), (1, H)).T.astype(np.float64)
    sign = np.where(np.arange(P) % DH < DH // 2, -1.0, 1.0)[:, None]
    rope = np.stack([np.cos(ang), np.sin(ang) * sign], 1).astype(np.float32)
    finv = (1.0 / 10000.0 ** (np.arange(0, P, 2, dtype=np.float32) / P)).astype(np.float32)
    fang = finv.astype(np.float64)[:, None] * t.astype(np.float64)[None, :]
    s, c = np.sin(fang), np.cos(fang)
    rel = np.stack([np.concatenate([s, c]), np.concatenate([c, c]), np.concatenate([s, -s])], 1)
    return rope, rel.astype(np.float32)


class Steps:

    def __init__(self, eng, sem):
        self.eng, self.sem, self.base, self.k, self.i, self.per = eng, sem, 0, 0, None, 0

    def now(self):
        return self.base + self.k if self.i is None else self.base + self.i * self.per + self.k

    def __call__(self, ins):
        ins.then_inc(self.sem, 1)
        self.k += 1

    def settle(self):
        self.eng.wait_ge(self.sem, self.now())

    def settle_by(self, cell):
        self.settle()
        self(self.eng.memset(cell, 0.0))

    @contextmanager
    def loop(self, trips, per):
        self.base, self.k, self.per = self.base + self.k, 0, per
        with self.eng.Fori(0, trips) as i:
            self.i = i
            yield i
        assert self.k == per, (self.k, per)
        self.base, self.k, self.i = self.base + trips * per, 0, None


def two_layers(nc, A, out, upto=99):
    with ExitStack() as ctx:
        def sb(name, shape, dt=F32):
            return ctx.enter_context(nc.sbuf_tensor(name, shape, dt))

        def sem(name):
            return ctx.enter_context(nc.semaphore(name))

        PS = ctx.enter_context(nc.psum_tensor("PS", [P, 8, GW], F32))

        def bank(b, dt=F32):
            return PS[:, b, :] if dt == F32 else PS[:, b, :].bitcast(dt)

        q_stack = nc.dram_tensor("q_stack", [9, NB * P, L], BF16)
        k_stack = nc.dram_tensor("k_stack", [9, NB * P, L], BF16)
        w_stack = nc.dram_tensor("w_stack", [9, NB * P, 2 * P], BF16)
        o_dram = nc.dram_tensor("o_dram", [NH + 1, 4, 32, 256], F32)

        X = sb("X", [P, TT, P])
        SRC = sb("SRC", [P, TT, P])
        XT = sb("XT", [P, TT * P])
        ident = sb("ident", [P, P])
        identb = sb("identb", [P, P], BF16)
        w_qkv = sb("w_qkv", [P, 3, 5 * P])
        w_out = sb("w_out", [P, 3, P])
        rope = sb("rope", [P, 2, L])
        rel = sb("rel", [P, 3, L])
        cols = sb("cols", [P, 8])
        rows = sb("rows", [P, 3, P])
        w_rt0 = sb("w_rt0", [P, 8])
        w_rt1 = sb("w_rt1", [P, NE1])
        Qs = sb("Qs", [P, SLOTS, L], BF16)
        Ks = sb("Ks", [P, SLOTS, L], BF16)
        zrow = sb("zrow", [PARTS, L], BF16)
        Vt = sb("Vt", [P, NH, QT, DH])
        Va = sb("Va", [P, SLOTS, QT, VC])
        M = sb("M", [P, SLOTS, QT])
        Mr = sb("Mr", [P, 2, QT])
        Ms = sb("Ms", [P, SLOTS, PARTS, QT], BF16)
        MT = sb("MT", [PARTS * QT, SLOTS, P], BF16)
        PR = sb("PR", [P, 4, L])
        Ob = sb("Ob", [P, 2, 256])
        Ws = sb("Ws", [P, 2, 2 * P], BF16)
        At = sb("At", [P, 2, L])
        tA = sb("tA", [P, 2, GW])
        BIG = sb("BIG", [P, 2 * QT * 4 * P])
        PT = BIG[:].rearrange("p (a k g q) -> p a k g q", a=2, k=QT, g=4)
        st = sb("st", [P, GT, 6])
        mv = sb("mv", [P, GT, 2])
        sd = sb("sd", [P, 2, GT])
        xn = sb("xn", [P, GT, P])
        xTs = sb("xTs", [P, GW])
        qk = sb("qk", [P, 2, GW])
        rt = sb("rt", [P, 2, GW])
        sp = sb("sp", [P, 2, PARTS, GW], BF16)
        atu = sb("atu", [P, 2, GW])
        atn = sb("atn", [P, GW])
        lg = sb("lg", [P, GT, NE1 + 8])
        lg2 = sb("lg2", [P, GT, NE1 + 8])
        m8 = sb("m8", [P, GT, 8])
        rp = sb("rp", [P, GT, 8])
        sm = sb("sm", [P, 2, GT])
        spare = sb("spare", [1, 1])
        nil = sb("nil", [P, 1])
        gate = sb("gate", [P, GT, NE1])
        gres = sb("gres", [P, 2, GT, NE1])
        gsp = sb("gsp", [P, GT, PARTS, NE1], BF16)
        GTs = sb("GTs", [P, TT * P], BF16)
        sel0 = sb("sel0", [ROWS, NE1])
        sel = sb("sel", [P, NE1, P], BF16)
        wg = sb("wg", [P, 2, 2, FI])
        wd = sb("wd", [P, 2, 3, P])
        hh = BIG[:, 0:6 * GW].rearrange("p (a c t) -> p a c t", a=2, c=3)
        sg = BIG[:, 6 * GW:9 * GW].rearrange("p (c t) -> p c t", c=3)
        xw = BIG[:, 9 * GW:11 * GW].rearrange("p (a t) -> p a t", a=2)
        we = sb("we", [P, 2, 2, P])
        acc = PR[:].rearrange("p a (b t) -> p (a b) t", b=2)[:, 0:NG, :]

        x_in, c_in = sem("x_in"), sem("c_in")
        stage = {e: sem(f"stage_{e}") for e in ("sp", "act", "pool", "pe", "dve")}
        own_dve, own_pool, own_act = sem("own_dve"), sem("own_pool"), sem("own_act")
        at_in, atn_ok, wo_ok, var_ok, sd_ok, xn_ok, xT_ok, xs_ok, xs_used = map(
            sem, "at_in atn_ok wo_ok var_ok sd_ok xn_ok xT_ok xs_ok xs_used".split())
        proj_ok, split_k, stk_out, v_ok, xres = map(sem, "proj_ok split_k stk_out v_ok xres".split())
        kin_ok, split_q, lgt_ok, ex_in, ex_ok, gsp_ok, gtp_ok, gt_ok = map(
            sem, "kin_ok split_q lgt_ok ex_in ex_ok gsp_ok gtp_ok gt_ok".split())
        w_out_ok = sem("w_out_ok")
        wp_in, wsplit = sem("wp_in"), sem("wsplit")
        qk_in = [sem(f"qk_in{s}") for s in range(SLOTS)]
        m_in = [sem(f"m_in{s}") for s in range(SLOTS)]
        o_out = [sem(f"o_out{s}") for s in range(2)]
        v_ready, s_done, max_done, m_split, mt_done, mt_copied = map(
            sem, "v_ready s_done max_done m_split mt_done mt_copied".split())
        st_done, exp_done, pv_done, o_copied, o_zero = map(
            sem, "st_done exp_done pv_done o_copied o_zero".split())
        ws_in = [sem(f"ws_in{s}") for s in range(2)]
        prep_ps, prep_mul, prep_add = map(sem, "prep_ps prep_mul prep_add".split())
        rs_done, rmax, rexp, rt_done, rev_a, rev_d, rpv = map(
            sem, "rs_done rmax rexp rt_done rev_a rev_d rpv".split())
        ro_copied = sem("ro_copied")
        rv_ready = sem("rv_ready")
        ew_in = [sem(f"ew_in{s}") for s in range(2)]
        acc_zero = sem("acc_zero")
        b_ps, g_ps, u_ps, xw_ok, sg_ok, h_ok, dn_ok, acc_ok = map(
            sem, "b_ps g_ps u_ps xw_ok sg_ok h_ok dn_ok acc_ok".split())
        y_out = sem("y_out")

        block = ctx.enter_context(nc.Block())

        N_CONST = 10

        def meet(eng, me, k):
            eng.sem_inc(stage[me], 1)
            for other in stage:
                if other != me:
                    eng.wait_ge(stage[other], k)

        KEEP = {0: "qkv0", 1: "moe0", 2: "qkv1", 3: "qkv2", 4: "moe1"}

        @block.sync
        def _(e):
            for g in range(NG):
                e.dma_start(X[:, GT * g:GT * g + GT, :],
                            A["x"].rearrange("(t p) d -> p t d", p=P)[:, GT * g:GT * g + GT, :]).then_inc(x_in, 16)
            loads = [(ident[:], A["ident"]), (w_qkv[:], A["w_qkv"]), (rope[:], A["rope"]),
                     (w_out[:], A["w_out"]), (cols[:], A["cols"]), (rows[:], A["rows"]),
                     (rel[:], A["rel"]), (w_rt0[:], A["w_rt0"]), (w_rt1[:], A["w_rt1"]),
                     (sel0[:], A["sel0"])]
            for dst, src in loads:
                e.dma_start(dst, src).then_inc(c_in, 16)
            assert len(loads) == N_CONST

            def stacks_out(f, b, half):
                u = 4 * f + 2 * b + half
                for which, ready, dst in ((0, split_q, q_stack), (1, split_k, k_stack)):
                    e.wait_ge(ready, 4 * QKV.index(f) + 2 * b + half + 1)
                    d = dst[:, bass.ts(b, P), half * GW:(half + 1) * GW]
                    if which == 0:
                        for i in range(PARTS):
                            e.dma_start(d[PARTS * i:PARTS * i + PARTS].rearrange("j p t -> p j t"),
                                        sp[:, 0, i, :].unsqueeze(1).broadcast_to([P, PARTS, GW])).then_inc(stk_out, 16)
                    else:
                        for j in range(PARTS):
                            dj = d.rearrange("(i j) p t -> j p i t", j=PARTS)[j]
                            e.dma_start(dj, sp[:, 1, j, :].unsqueeze(1).broadcast_to([P, PARTS, GW]))\
                                .then_inc(stk_out, 16)

            def attention_in(k, b, half, relative):
                u = 4 * k + 2 * b + half
                e.wait_ge(atn_ok, u)
                heads = o_dram[1:NH + 1].rearrange("(b h) g c q -> b h g c q", b=NB)[bass.ds(b, 1)]
                heads = heads.rearrange("b h g c q -> (b h) g c q")
                if relative:
                    pieces = [(g, slice(half * P, half * P + P)) for g in range(4)]
                else:
                    pieces = [(2 * half + g, slice(0, 256)) for g in range(2)]
                w = GW // len(pieces)
                for n, (g, q) in enumerate(pieces):
                    src = heads[:, g, :, q]
                    e.dma_start(atu[:, 0, n * w:(n + 1) * w], src[:, 0:DH, :]).then_inc(at_in, 16)
                    e.dma_start(atu[:, 1, n * w:(n + 1) * w],
                                src[:, DH:DH + 1, :].broadcast_to([H, DH, w])).then_inc(at_in, 16)

            def load_qk(a, n, s):
                e.dma_start(Qs[0:STACK, s, :], q_stack[:, bass.ts(n, DH), :]).then_inc(qk_in[s], 16)
                e.dma_start(Qs[STACK:STACK + PARTS, s, :], zrow[:, :]).then_inc(qk_in[s], 16)
                e.dma_start(Ks[0:STACK, s, :], k_stack[:, bass.ts(n, DH), :]).then_inc(qk_in[s], 16)

            def attention(a):
                def max_rows(n, s):
                    e.wait_ge(mt_copied, NH * a + n + 1)
                    e.dma_start(Qs[STACK:STACK + PARTS, s, :], MT[:, s, :]).then_inc(m_in[s], 16)

                def store(k):
                    e.wait_ge(o_copied, (NH + 1) * a + k + 1)
                    e.dma_start(o_dram[bass.ds(k, 1)].rearrange("n g c q -> (n g c) q"),
                                Ob[:, (k % 2) if isinstance(k, int) else None, :])

                def position(i, s, last):
                    n = SLOTS * i + s
                    if not (last and s >= 1):
                        e.wait_ge(st_done, 16 * (NH * a + n))
                        load_qk(a, n + 3, (s + 3) % SLOTS)
                    e.wait_ge(o_copied, (NH + 1) * a + n + 1)
                    e.dma_start(o_dram[bass.ds(n, 1)].rearrange("n g c q -> (n g c) q"), Ob[:, s % 2, :])\
                        .then_inc(o_out[s % 2], 16)
                    if not (last and s == 3):
                        max_rows(n + 1, (s + 1) % SLOTS)

                for n in range(3):
                    load_qk(a, n, n)
                max_rows(0, 0)
                with e.Fori(0, NH // SLOTS - 1) as i:
                    for s in range(SLOTS):
                        position(i, s, False)
                for s in range(SLOTS):
                    position(NH // SLOTS - 1, s, True)
                e.wait_ge(o_copied, (NH + 1) * (a + 1))
                e.dma_start(o_dram[NH:NH + 1].rearrange("n g c q -> (n g c) q"), Ob[:, 0, :]).then_inc(o_out[0], 16)
                e.wait_ge(o_out[0], 16 * 17 * (a + 1))
                e.wait_ge(o_out[1], 16 * 16 * (a + 1))

            def relative_attention():
                def load(n, s):
                    load_qk(2, n, s)
                    e.dma_start(Ws[0:STACK, s, :], w_stack[:, bass.ts(n, DH), :]).then_inc(ws_in[s], 16)

                def position(i, s, last):
                    n = 2 * i + s
                    e.wait_ge(ro_copied, n + 1)
                    e.dma_start(o_dram[bass.ds(n + 1, 1)].rearrange("n g c q -> (n g c) q"), Ob[:, s, :])\
                        .then_inc(o_out[s], 16)
                    if not last:
                        load(n + 2, s)

                load(0, 0)
                load(1, 1)
                with e.Fori(0, NH // 2 - 1) as i:
                    for s in range(2):
                        position(i, s, False)
                for s in range(2):
                    position(NH // 2 - 1, s, True)
                e.wait_ge(o_out[0], 16 * (17 * 2 + NH // 2))
                e.wait_ge(o_out[1], 16 * (16 * 2 + NH // 2))

            def experts0():
                def load(x, s):
                    e.dma_start(wg[:, s, :, :], A["gu"][bass.ds(x, 1)].rearrange("x p a f -> (x p) a f"))\
                        .then_inc(ew_in[s], 16)
                    e.dma_start(wd[:, s, :, :], A["dn"][bass.ds(x, 1)].rearrange("x p c f -> (x p) c f"))\
                        .then_inc(ew_in[s], 16)
                for s in range(2):
                    load(s, s)
                with e.Fori(0, NE0 // 2 - 1) as i:
                    for s in range(2):
                        e.wait_ge(dn_ok, NG * (2 * i + s + 1))
                        load(2 * i + s + 2, s)

            def experts1():
                def load(x, s):
                    e.dma_start(we[:, s, :, :], A["kv"][bass.ds(x, 1)].rearrange("x p a f -> (x p) a f"))\
                        .then_inc(ew_in[s], 16)
                for s in range(2):
                    load(s, s)
                with e.Fori(0, NE1 // 2 - 1) as i:
                    for s in range(2):
                        e.wait_ge(dn_ok, NG * (NE0 + 2 * i + s + 1))
                        load(2 * i + s + 2, s)

            QKV = [0, 2, 3]
            k = 0

            def front(f):
                nonlocal k
                with e.Fori(0, NB) as b:
                    for half in range(2):
                        if f in (1, 3, 4):
                            attention_in({1: 0, 3: 1, 4: 2}[f], b, half, f == 4)
                        if f in QKV:
                            stacks_out(f, b, half)
                if f in QKV:
                    e.wait_ge(stk_out, 16 * 6 * 4 * (QKV.index(f) + 1))
                if f == 3:
                    e.wait_ge(wsplit, 1)
                    for b in range(NB):
                        d = w_stack[:, b * P:(b + 1) * P, :].rearrange("(i j) p t -> j p i t", j=PARTS)
                        for j in range(PARTS):
                            src = PT[:, 1, j, 0:2, :].rearrange("p a f -> p (a f)").bitcast(BF16)[:, 0:2 * P]
                            e.dma_start(d[j], src.unsqueeze(1).broadcast_to([P, PARTS, 2 * P])).then_inc(stk_out, 16)
                    e.wait_ge(stk_out, 16 * (6 * 4 * 3 + 6))

            def attention1():
                e.dma_start(PT[:, 0, 0:2, 0, :], A["wpT"].rearrange("p (a f) -> p a f", a=2)).then_inc(wp_in, 16)
                attention(1)

            plan = [lambda: front(0), lambda: attention(0), lambda: front(1), experts0, lambda: front(2),
                    attention1, lambda: front(3), relative_attention, lambda: front(4), experts1]
            for k, run in enumerate(plan[:upto]):
                run()
                meet(e, "sp", k + 1)
            if upto > len(plan):
                e.wait_ge(xres, 8)
            o_t = out.rearrange("(t p) d -> p t d", p=P)
            for g in range(NG):
                e.dma_start(o_t[:, GT * g:GT * g + GT, :], X[:, GT * g:GT * g + GT, :]).then_inc(y_out, 16)
            e.wait_ge(y_out, 16 * NG)

        @block.tensor
        def _(e):
            e.wait_ge(c_in, 16 * N_CONST)

            def front(f):
                a = {1: 0, 3: 1, 4: 2}.get(f)
                with e.Fori(0, NB) as b:
                    for half in range(2):
                        g = 2 * b + half
                        u = 4 * f + g
                        if a is not None:
                            e.wait_ge(atn_ok, 4 * a + g + 1)
                            for t in range(GT):
                                m = e.matmul(PS[:, 6, t * P:(t + 1) * P], atn[:, t * P:(t + 1) * P],
                                             w_out[:, a, :], start=True, stop=True)
                            m.then_inc(wo_ok, 1)
                        e.wait_ge(xn_ok, u + 1)
                        for t in range(GT):
                            m = e.transpose(PS[:, 0, t * P:(t + 1) * P], xn[:, t, :], ident[:])
                        m.then_inc(xT_ok, 1)
                        e.wait_ge(xs_ok, u + 1)
                        if f in (0, 2, 3):
                            a2 = {0: 0, 2: 1, 3: 2}[f]
                            for n, (w, bk) in enumerate([(0, 1), (1, 2), (2, 3), (3, 4)]):
                                if f and n % 2:
                                    continue
                                e.matmul(bank(bk), w_qkv[:, a2, w * P:(w + 1) * P], xTs[:], start=True, stop=True)\
                                    .then_inc(proj_ok, 1)
                            for t in range(GT):
                                m = e.matmul(PS[:, 5, t * P:(t + 1) * P], xTs[:, t * P:(t + 1) * P],
                                             w_qkv[:, a2, 4 * P:5 * P], start=True, stop=True)
                            m.then_inc(proj_ok, 1)
                        else:
                            w, ne = (w_rt0[:, 0:NE0 - 1], NE0 - 1) if f == 1 else (w_rt1[:], NE1)
                            for t in range(GT):
                                m = e.matmul(PS[:, 7, t * NE1:t * NE1 + ne], xTs[:, t * P:(t + 1) * P], w,
                                             start=True, stop=True)
                            m.then_inc(lgt_ok, 1)
                            e.wait_ge(gsp_ok, 4 * (f == 4) + g + 1)
                            for t in range(GT):
                                m = e.transpose(bank(1, BF16)[0:ROWS, t * P:(t + 1) * P],
                                                gsp[:, t, :, :].rearrange("p a x -> p (a x)"), identb[:])
                            m.then_inc(gtp_ok, 1)
                            e.wait_ge(gt_ok, 4 * (f == 4) + g + 1)

            def attention(a):
                HB = NH * a
                c = 8 * a // 1

                def scores(n, s, qt, kh):
                    if kh == 0:
                        e.wait_ge(max_done, 8 * (HB + n) + qt + 1)
                    m = e.matmul(bank(2 + 2 * (qt % 2) + kh), Qs[0:ROWS, s, qt * P:(qt + 1) * P],
                                 Ks[0:ROWS, s, kh * GW:(kh + 1) * GW], start=True, stop=True)
                    if kh == 1:
                        m.then_inc(s_done, 1)

                def max_transpose(n, s):
                    e.wait_ge(m_split, HB + n + 1)
                    e.wait_ge(mt_copied, HB + n)
                    e.transpose(bank(7, BF16)[0:PARTS * QT, 0:P], Ms[:, s, :, :].rearrange("p a q -> p (a q)"),
                                identb[:]).then_inc(mt_done, 1)

                def values(n, s, kt):
                    if kt == 0:
                        e.wait_ge(v_ready, HB + n + 1)
                        e.wait_ge(o_copied, (NH + 1) * a + n + 1)
                    for g in range(4):
                        m = e.matmul(PS[32 * g:32 * g + VC, 6, 0:256], Va[:, s, kt, :],
                                     PR[:, kt % 4, g * 256:(g + 1) * 256], start=(kt == 0), stop=(kt == QT - 1))
                    m.then_inc(pv_done, 1)

                def position(i, s, last):
                    n = SLOTS * i + s
                    s2 = (s + 2) % SLOTS
                    lead = not (last and s >= 2)
                    if lead:
                        e.wait_ge(qk_in[s2], 48 * (NH // SLOTS * a + i + (s >= 2) + 1))
                    e.wait_ge(m_in[s], 16 * (NH // SLOTS * a + i + 1))
                    for x in range(16):
                        e.wait_ge(exp_done, 16 * (HB + n) + x + 1)
                        kt, qh = x // 2, x % 2
                        e.matmul(bank(x % 2), Ks[0:ROWS, s, kt * P:(kt + 1) * P],
                                 Qs[0:ROWS, s, qh * GW:(qh + 1) * GW], start=True, stop=True).then_inc(st_done, 1)
                        if x == 6 and not (last and s == 3):
                            max_transpose(n + 1, (s + 1) % SLOTS)
                        if lead:
                            scores(n + 2, s2, x // 2, x % 2)
                        if x % 2 and x >= 3:
                            values(n, s, (x - 3) // 2)
                    e.wait_ge(exp_done, 2 + 16 * (HB + n) + 16)
                    values(n, s, QT - 1)

                if a == 0:
                    e.sem_inc(exp_done, 2)
                    e.sem_inc(pv_done, 4)
                for n in range(2):
                    e.wait_ge(qk_in[n], 48 * (NH // SLOTS * a + 1))
                    for x in range(16):
                        scores(n, n, x // 2, x % 2)
                max_transpose(0, 0)
                with e.Fori(0, NH // SLOTS - 1) as i:
                    for s in range(SLOTS):
                        position(i, s, False)
                for s in range(SLOTS):
                    position(NH // SLOTS - 1, s, True)

            def relative_attention():
                def prep(n, s, p):
                    if p == 0:
                        e.wait_ge(ws_in[s], 16 * (n // 2 + 1) if isinstance(n, int) else 16 * (n[0] + 1))
                        e.wait_ge(qk_in[s], 48 * (16 + 1 + (n // 2 if isinstance(n, int) else n[0])))
                    num = n if isinstance(n, int) else n[1]
                    e.wait_ge(prep_mul, 4 * num + p)
                    e.matmul(bank(6), Ws[0:ROWS, s, (p % 2) * P:(p % 2 + 1) * P],
                             Qs[0:ROWS, s, (p // 2) * GW:(p // 2 + 1) * GW], start=True, stop=True)\
                        .then_inc(prep_ps, 1)

                def scores(n, s, qt):
                    if qt == 0:
                        e.wait_ge(prep_add, 2 * n + 2)
                    e.wait_ge(rexp, 8 * n + qt + 1)
                    for kh in range(2):
                        o = bank(2 * (qt % 2) + kh)
                        e.matmul(o, Qs[0:ROWS, s, qt * P:(qt + 1) * P], Ks[0:ROWS, s, kh * GW:(kh + 1) * GW],
                                 start=True, stop=False)
                        m = e.matmul(o, At[:, s, qt * P:(qt + 1) * P], rel[:, 0, kh * GW:(kh + 1) * GW],
                                     start=False, stop=True)
                    m.then_inc(rs_done, 1)

                def position(i, s, last):
                    n = 2 * i + s
                    end = last and s == 1
                    for qt in range(QT):
                        u = 8 * n + qt
                        e.wait_ge(rexp, 2 + u + 1)
                        e.wait_ge(rev_a, u)
                        e.wait_ge(rev_d, u)
                        for kt in range(QT):
                            m = e.transpose(PS[:, 4 + kt // 4, (kt % 4) * P:(kt % 4 + 1) * P],
                                            PR[:, qt % 2, kt * P:(kt + 1) * P], ident[:])
                        m.then_inc(rt_done, 1)
                        if qt < 6:
                            scores(n, s, qt + 2)
                        elif not end:
                            scores(n + 1, 1 - s, qt - 6)
                        if qt < 4 and not end:
                            prep((i + (s == 1), n + 1), 1 - s, qt)
                        if qt % 4 == 3:
                            half = qt // 4
                            e.wait_ge(rev_a, u + 1)
                            e.wait_ge(rev_d, u + 1)
                            if half == 0:
                                e.wait_ge(ro_copied, n)
                                e.wait_ge(rv_ready, n + 1)
                            for kt in range(QT):
                                for g in range(4):
                                    m = e.matmul(PS[32 * g:32 * g + VC, 7, half * P:(half + 1) * P],
                                                 Va[:, s, kt, :], PT[:, half, kt, g, :],
                                                 start=(kt == 0), stop=(kt == QT - 1))
                            m.then_inc(rpv, 1)

                e.sem_inc(rexp, 2)
                for p in range(4):
                    prep(0, 0, p)
                scores(0, 0, 0)
                scores(0, 0, 1)
                with e.Fori(0, NH // 2 - 1) as i:
                    for s in range(2):
                        position(i, s, False)
                for s in range(2):
                    position(NH // 2 - 1, s, True)

            def zero_acc(k):
                e.wait_ge(acc_zero, k + 1)
                for b in range(4, 8):
                    e.matmul(bank(b), acc[:, 0, 0:P], acc[:, 0, :], start=True, stop=True, skip_group_check=True)

            def spread(x, ring, tg):
                e.matmul(bank(ring), sel[0:ROWS, x, :], GTs[0:ROWS, tg * GW:(tg + 1) * GW], start=True, stop=True)\
                    .then_inc(b_ps, 1)

            def experts0():
                zero_acc(0)

                def down(s, tg):
                    for c, (lo, w) in enumerate(FCH):
                        m = e.matmul(bank(4 + tg), wd[0:w, s, c, :], hh[0:w, tg % 2, c, :],
                                     start=False, stop=True, skip_group_check=True)
                    m.then_inc(dn_ok, 1)

                def unit(i, s, tg):
                    x = 2 * i + s
                    v = NG * x + tg
                    first = s == 0 and tg == 0
                    if tg == 0:
                        e.wait_ge(ew_in[s], 32 * (i + 1))
                    xs = XT[:, tg * GW:(tg + 1) * GW]

                    def up(c, k, bk):
                        lo, w = FCH[c]
                        e.matmul(PS[0:w, bk, :], wg[:, s, k, lo:lo + w], xs if k == 0 else xw[:, tg % 2, :],
                                 start=True, stop=True).then_inc(u_ps if k else g_ps, 1)
                    e.wait_ge(h_ok, 3 * v - (0 if first else 1))
                    spread(x, 0, tg)
                    e.wait_ge(sg_ok, 3 * v)
                    up(0, 0, 1)
                    e.wait_ge(h_ok, 3 * v)
                    up(1, 0, 2)
                    if not first:
                        down(s if tg else 1 - s, (tg - 1) % NG)
                    e.wait_ge(xw_ok, v + 1)
                    up(0, 1, 3)
                    up(1, 1, 0)
                    e.wait_ge(sg_ok, 3 * v + 1)
                    up(2, 0, 1)
                    e.wait_ge(sg_ok, 3 * v + 2)
                    up(2, 1, 2)

                with e.Fori(0, NE0 // 2) as i:
                    for s in range(2):
                        for tg in range(NG):
                            unit(i, s, tg)
                    e.wait_ge(h_ok, 3 * NG * (2 * i + 2))
                    down(1, NG - 1)

            def experts1():
                zero_acc(1)
                V0 = NG * NE0

                def values(s, tg):
                    e.matmul(bank(4 + tg), we[:, s, 1, :], hh[:, tg % 2, 0, :], start=False, stop=True,
                             skip_group_check=True).then_inc(dn_ok, 1)

                def unit(i, s, tg):
                    x = 2 * i + s
                    v = NG * x + tg
                    first = s == 0 and tg == 0
                    if tg == 0:
                        e.wait_ge(ew_in[s], 32 * (NE0 // 2) + 16 * (i + 1))
                    e.wait_ge(h_ok, 3 * V0 + v - (0 if first else 1))
                    e.matmul(bank(2 * (tg % 2)), sel[0:ROWS, x, :], GTs[0:ROWS, tg * GW:(tg + 1) * GW],
                             start=True, stop=True).then_inc(b_ps, 1)
                    e.matmul(bank(2 * (tg % 2) + 1), we[:, s, 0, :], XT[:, tg * GW:(tg + 1) * GW],
                             start=True, stop=True).then_inc(g_ps, 1)
                    if not first:
                        e.wait_ge(h_ok, 3 * V0 + v)
                        values(s if tg else 1 - s, (tg - 1) % NG)

                with e.Fori(0, NE1 // 2) as i:
                    for s in range(2):
                        for tg in range(NG):
                            unit(i, s, tg)
                    e.wait_ge(h_ok, 3 * V0 + NG * (2 * i + 2))
                    values(1, NG - 1)

            def back(k):
                e.wait_ge(acc_ok, 4 * (k + 1))
                for g in range(NG):
                    if g:
                        e.wait_ge(xres, 4 * k + g)
                    for t in range(GT):
                        m = e.transpose(PS[:, 6, t * P:(t + 1) * P], acc[:, g, t * P:(t + 1) * P], ident[:])
                    m.then_inc(wo_ok, 1)

            def front2():
                back(0)
                front(2)

            plan = [lambda: front(0), lambda: attention(0), lambda: front(1), experts0, front2,
                    lambda: attention(1), lambda: front(3), relative_attention, lambda: front(4), experts1]
            for k, run in enumerate(plan[:upto]):
                run()
                meet(e, "pe", k + 1)
            if upto > len(plan):
                back(1)

        @block.vector
        def _(e):
            own = Steps(e, own_dve)
            cell = spare[:]

            def layernorm(src, t0, u, parity):
                own.settle_by(cell)
                for t in range(GT):
                    own(e.bn_stats(st[:, t, :], src(t)))
                own.settle_by(cell)
                for t in range(GT):
                    own(e.bn_aggr(mv[:, t, :], st[:, t, :]))
                own.settle()
                e.tensor_scalar(sd[:, 0, :], mv[:, :, 1], EPS, None, ALU.add).then_inc(var_ok, 1)
                e.wait_ge(sd_ok, parity)
                own(e.reciprocal(sd[:, 1, :], sd[:, 0, :]))
                own.settle()
                for t in range(GT):
                    own(e.tensor_scalar(xn[:, t, :], src(t), mv[:, t, 0:1], sd[:, 1, t:t + 1],
                                        ALU.subtract, ALU.mult))
                own.settle()

            def split(dst, src, res, k):
                own(e.tensor_copy(dst(0), src))
                own.settle()
                own(e.tensor_tensor(res[0], src, dst(0), ALU.subtract))
                own.settle()
                own(e.tensor_copy(dst(1), res[0]))
                own.settle()
                own(e.tensor_tensor(res[1], res[0], dst(1), ALU.subtract))
                own.settle()
                return e.tensor_copy(dst(2), res[1])

            def front(f):
                a = {1: 0, 3: 1, 4: 2}.get(f)
                a2 = {0: 0, 2: 1, 3: 2}.get(f)
                lns = 2 if f in (2, 3) else 1
                per = [2 * (13 + 9), 2 * (2 + 13 + 28), 2 * (13 + 2 + 13 + 6), 2 * (2 + 15 + 13 + 6), 2 * (3 + 13 + 18)][f]
                l0 = 4 * [0, 1, 2, 4, 6][f]
                with own.loop(NB, PER[f]) as b:
                    for half in range(2):
                        g = 2 * b + half
                        u = 4 * f + g
                        xg = X[:, bass.ts(g, GT), :].rearrange("p t d -> p (t d)")
                        sg_ = SRC[:, bass.ts(g, GT), :].rearrange("p t d -> p (t d)")

                        def tile(buf):
                            return lambda t: buf[:, bass.ds(GT * g + t, 1), :].rearrange("p t d -> p (t d)")
                        if a is not None:
                            e.wait_ge(at_in, 16 * ([4, 4, 8][a] * (g + 1) + [0, 16, 32][a]))
                            own(e.reciprocal(atu[:, 1, :], atu[:, 1, :]))
                            own.settle()
                            e.tensor_tensor(atn[:], atu[:, 0, :], atu[:, 1, :], ALU.mult).then_inc(atn_ok, 1)
                            e.wait_ge(wo_ok, 4 * [0, 2, 3][a] + g + 1)
                            own(e.tensor_tensor(xg, xg, bank(6), ALU.add))
                            if a == 2:
                                own(e.tensor_tensor(sg_, sg_, bank(6), ALU.add))
                            own.settle()
                            if a == 1:
                                own(e.tensor_tensor(X[:, bass.ts(g, GT), :], X[:, bass.ts(g, GT), :],
                                                    rows[:, 1, :].unsqueeze(1).broadcast_to([P, GT, P]), ALU.add))
                                own.settle()
                        if f < 4:
                            layernorm(tile(X), None, u, l0 + lns * g + 1)
                        else:
                            layernorm(tile(SRC), None, u, l0 + lns * g + 1)
                        if lns == 2:
                            own(e.tensor_copy(sg_, xn[:].rearrange("p t d -> p (t d)")))
                            own(e.tensor_tensor(xg, xg, xn[:].rearrange("p t d -> p (t d)"), ALU.add))
                            own.settle()
                            layernorm(tile(SRC), None, u, l0 + lns * g + 2)
                        e.sem_inc(xn_ok, 1)
                        if a2 is not None:
                            project(f, a2, b, half)
                        else:
                            route(f, g)

            def project(f, a2, b, half):
                g = 2 * b + half
                pr = 5 * g if f == 0 else 20 + 12 * (a2 - 1) + 3 * g
                tok = slice(half * GW, (half + 1) * GW)
                e.wait_ge(split_k, 4 * a2 + g)
                if f == 0:
                    e.wait_ge(proj_ok, pr + 4)
                    own(e.tensor_tensor(rt[:, 0, :], bank(3), rope[:, 0, tok], ALU.mult))
                    own(e.tensor_tensor(rt[:, 1, :], bank(4), rope[:, 1, tok], ALU.mult))
                    own.settle()
                    e.tensor_tensor(qk[:, 1, :], rt[:, 0, :], rt[:, 1, :], ALU.add).then_inc(kin_ok, 1)
                    e.wait_ge(kin_ok, 4 * a2 + g + 1)
                    own(e.tensor_tensor(rt[:, 0, :], bank(1), rope[:, 0, tok], ALU.mult))
                    own(e.tensor_tensor(rt[:, 1, :], bank(2), rope[:, 1, tok], ALU.mult))
                    own.settle()
                    own(e.tensor_tensor(qk[:, 0, :], rt[:, 0, :], rt[:, 1, :], ALU.add))
                else:
                    e.wait_ge(proj_ok, pr + 2)
                    if f == 2:
                        e.tensor_scalar(qk[:, 1, :], bank(3), cols[:, 3:4], None, ALU.add).then_inc(kin_ok, 1)
                        own(e.tensor_scalar(qk[:, 0, :], bank(1), cols[:, 2:3], None, ALU.add))
                    else:
                        e.tensor_copy(qk[:, 1, :], bank(3)).then_inc(kin_ok, 1)
                        own(e.tensor_scalar(qk[:, 0, :], bank(1), SCALE, None, ALU.mult))
                own.settle()
                e.wait_ge(stk_out, 16 * (24 * a2 + 6 * g))
                split(lambda j: sp[:, 0, j, :], qk[:, 0, :], (rt[:, 0, :], rt[:, 1, :]), None).then_inc(split_q, 1)
                e.wait_ge(proj_ok, pr + (5 if f == 0 else 3))
                for t in range(GT):
                    dst = Vt[:, bass.ts(b, H), half * GT + t, :]
                    src = PS[:, 5, t * P:(t + 1) * P].rearrange("p (h d) -> p h d", h=H)
                    if f == 2:
                        own(e.tensor_tensor(dst, src, rows[:, 0, :].rearrange("p (h d) -> p h d", h=H), ALU.add))
                    else:
                        own(e.tensor_copy(dst, src))
                e.wait_ge(split_q, 4 * a2 + g + 1)
                own.settle()

            def route(f, g):
                m = f == 4
                ne, top = (NE1, 4) if m else (NE0 - 1, 2)
                r = 4 * m + g
                e.wait_ge(lgt_ok, r + 1)
                ps = PS[:, 7, 0:GT * NE1].rearrange("p (t x) -> p t x", t=GT)[:, :, 0:ne]
                val = lg[:, :, 0:ne]

                def each(v, k=ne):
                    return v.unsqueeze(2).broadcast_to([P, GT, k])
                if not m:
                    own(e.tensor_tensor(lg2[:, :, 0:ne], ps, rows[:, 2, 0:ne].unsqueeze(1).broadcast_to([P, GT, ne]),
                                        ALU.add))
                    own.settle()
                    own(e.tensor_reduce(sm[:, 0, :], lg2[:, :, 0:ne], AX.X, ALU.max))
                    own.settle()
                    e.tensor_tensor(val, lg2[:, :, 0:ne], each(sm[:, 0, :]), ALU.subtract).then_inc(ex_in, 1)
                    e.wait_ge(ex_ok, r + 1)
                    own(e.tensor_reduce(sm[:, 0, :], val, AX.X, ALU.add))
                    own.settle()
                    own(e.reciprocal(sm[:, 1, :], sm[:, 0, :]))
                    own.settle()
                    own(e.tensor_tensor(val, val, each(sm[:, 1, :]), ALU.mult))
                    own.settle()
                else:
                    e.sem_inc(ex_in, 1)
                    e.wait_ge(ex_ok, r + 1)
                    own(e.tensor_scalar(val, val, 1.0, None, ALU.add))
                    own.settle()
                    own(e.reciprocal(val, val))
                    own.settle()
                own.settle_by(cell)
                for t in range(GT):
                    own(e.max(m8[:, t, :], lg[:, t, 0:ne + 8]))
                own.settle()
                own(e.tensor_copy(rp[:, :, 0:top], m8[:, :, 0:top]))
                own.settle_by(cell)
                for t in range(GT):
                    own(e.match_replace(lg2[:, t, 0:ne + 8], rp[:, t, :], lg[:, t, 0:ne + 8], 0.0))
                own.settle()
                g0 = gate[:, :, 0:ne] if m else gate[:, :, 1:ne + 1]
                own(e.tensor_tensor(g0, val, lg2[:, :, 0:ne], ALU.subtract))
                own.settle()
                if not m:
                    own(e.tensor_reduce(sm[:, 0, :], g0, AX.X, ALU.add))
                    own.settle()
                    own(e.reciprocal(sm[:, 1, :], sm[:, 0, :]))
                    own.settle()
                    own(e.tensor_tensor(g0, g0, each(sm[:, 1, :]), ALU.mult))
                    own.settle()
                split(lambda j: gsp[:, :, j, :], gate[:], (gres[:, 0], gres[:, 1]), None).then_inc(gsp_ok, 1)
                e.wait_ge(gtp_ok, r + 1)
                e.tensor_copy(GTs[0:ROWS, bass.ts(g, GW)], bank(1, BF16)[0:ROWS, 0:GW]).then_inc(gt_ok, 1)
                e.wait_ge(gt_ok, r + 1)

            PER = [56, 82, 82, 88, 72]

            def attention(a):
                HB = NH * a
                e.memset(PS[:, 6, 0:256], 0.0).then_inc(o_zero, 1)
                if a == 0:
                    e.sem_inc(max_done, 2)

                def row_max(n, s, qt):
                    e.wait_ge(s_done, 8 * (HB + n) + qt + 1)
                    e.tensor_reduce(M[:, s, qt:qt + 1], PS[:, 2 + 2 * (qt % 2):4 + 2 * (qt % 2), :]
                                    .rearrange("p a b -> p (a b)"), AX.X, ALU.max, negate=True).then_inc(max_done, 1)

                def max_copy(n, s):
                    e.wait_ge(mt_done, HB + n + 1)
                    e.tensor_copy(MT[:, s, :], bank(7, BF16)[0:PARTS * QT, 0:P]).then_inc(mt_copied, 1)

                for n in range(2):
                    for qt in range(QT):
                        row_max(n, n, qt)
                max_copy(0, 0)

                def position(i, s, last):
                    n = SLOTS * i + s
                    for qt in range(QT):
                        if qt == 4 and not (last and s == 3):
                            max_copy(n + 1, (s + 1) % SLOTS)
                        if not (last and s >= 2):
                            row_max(n + 2, (s + 2) % SLOTS, qt)
                with e.Fori(0, NH // SLOTS - 1) as i:
                    for s in range(SLOTS):
                        position(i, s, False)
                for s in range(SLOTS):
                    position(NH // SLOTS - 1, s, True)

            def relative_attention():
                def prep(n, s, p):
                    e.wait_ge(prep_ps, 4 * n + p + 1)
                    e.wait_ge(prep_add, 2 * n + p // 2)
                    e.tensor_tensor(tA[:, p % 2, :], bank(6), rel[:, 1 + p % 2, (p // 2) * GW:(p // 2 + 1) * GW],
                                    ALU.mult).then_inc(prep_mul, 1)

                def row_max(n, s, qt):
                    e.wait_ge(rs_done, 8 * n + qt + 1)
                    e.tensor_reduce(M[:, s, qt:qt + 1], PS[:, 2 * (qt % 2):2 * (qt % 2) + 2, :]
                                    .rearrange("p a b -> p (a b)"), AX.X, ALU.max, negate=True).then_inc(rmax, 1)

                def position(i, s, last):
                    n = 2 * i + s
                    end = last and s == 1
                    for qt in range(QT):
                        u = 8 * n + qt
                        if qt < 7:
                            row_max(n, s, qt + 1)
                        elif not end:
                            row_max(n + 1, 1 - s, 0)
                        e.wait_ge(rt_done, u + 1)
                        if qt % 4 == 0:
                            e.wait_ge(rpv, 2 * n + qt // 4)
                        e.tensor_copy(PT[:, qt // 4, 4:8, qt % 4, :], PS[:, 5, :].rearrange("p (k q) -> p k q", k=4))\
                            .then_inc(rev_d, 1)
                        if qt < 4 and not end:
                            prep(n + 1, 1 - s, qt)

                for p in range(4):
                    prep(0, 0, p)
                row_max(0, 0, 0)
                with e.Fori(0, NH // 2 - 1) as i:
                    for s in range(2):
                        position(i, s, False)
                for s in range(2):
                    position(NH // 2 - 1, s, True)

            def zero_acc():
                e.memset(acc[:, 0, :], 0.0).then_inc(acc_zero, 1)

            def experts0():
                zero_acc()
                with e.Fori(0, NE0 // 2) as i:
                    for s in range(2):
                        for tg in range(NG):
                            v = NG * (2 * i + s) + tg
                            e.wait_ge(b_ps, v + 1)
                            e.tensor_tensor(xw[:, tg % 2, :], XT[:, tg * GW:(tg + 1) * GW], bank(0), ALU.mult)\
                                .then_inc(xw_ok, 1)
                            for c, (lo, w) in enumerate(FCH):
                                e.wait_ge(u_ps, 3 * v + c + 1)
                                e.wait_ge(sg_ok, 3 * v + c + 1)
                                e.tensor_tensor(hh[0:w, tg % 2, c, :], PS[0:w, [3, 0, 2][c], :], sg[0:w, c, :],
                                                ALU.mult).then_inc(h_ok, 1)

            def experts1():
                V0 = NG * NE0
                e.memset(acc[:, 0, :], 0.0).then_inc(acc_zero, 1)
                with e.Fori(0, NE1 // 2) as i:
                    for s in range(2):
                        for tg in range(NG):
                            v = NG * (2 * i + s) + tg
                            e.wait_ge(sg_ok, 3 * V0 + v + 1)
                            e.tensor_tensor(hh[:, tg % 2, 0, :], bank(2 * (tg % 2)), sg[:, tg % 2, :], ALU.mult)\
                                .then_inc(h_ok, 1)

            def back(k):
                e.wait_ge(dn_ok, NG * (NE0 + k * NE1))
                for g in range(NG):
                    e.tensor_copy(acc[:, g, :], bank(4 + g)).then_inc(acc_ok, 1)
                for g in range(NG):
                    e.wait_ge(wo_ok, [4, 16][k] + g + 1)
                    xg = X[:, GT * g:GT * g + GT, :].rearrange("p t d -> p (t d)")
                    e.tensor_tensor(xg, xg, bank(6), ALU.add).then_inc(xres, 1)
                e.wait_ge(xres, [4, 8][k])

            def front2():
                back(0)
                front(2)

            def front3():
                w = PT[:, 0, 0:2, 0, :]
                res = [PT[:, 0, 2:4, 0, :], PT[:, 0, 4:6, 0, :]]

                def part(j):
                    return PT[:, 1, j, 0:2, :].rearrange("p a f -> p (a f)").bitcast(BF16)[:, 0:2 * P]\
                        .rearrange("p (a f) -> p a f", a=2)
                e.wait_ge(wp_in, 16)
                split(part, w, res, None).then_inc(wsplit, 1)
                front(3)

            plan = [lambda: front(0), lambda: attention(0), lambda: front(1), experts0, front2,
                    lambda: attention(1), front3, relative_attention, lambda: front(4), experts1]
            e.wait_ge(x_in, 16 * NG)
            e.wait_ge(c_in, 16 * N_CONST)
            own(e.memset(lg[:], -1.0))
            own(e.memset(rp[:], -1.0))
            own(e.memset(gate[:], 0.0))
            own.settle()
            own(e.memset(gate[:, :, 0:1], 1.0))
            own.settle()
            for k, run in enumerate(plan[:upto]):
                run()
                meet(e, "dve", k + 1)
            if upto > len(plan):
                back(1)

        @block.scalar
        def _(e):
            e.wait_ge(c_in, 16 * N_CONST)

            def front(f):
                lns = 2 if f in (2, 3) else 1
                l0 = 4 * [0, 1, 2, 4, 6][f]
                with e.Fori(0, NB) as b:
                    for half in range(2):
                        g = 2 * b + half
                        u = 4 * f + g
                        for k in range(lns):
                            e.wait_ge(var_ok, l0 + lns * g + k + 1)
                            e.activation(sd[:, 0, :], sd[:, 0, :], ACT.Sqrt).then_inc(sd_ok, 1)
                        e.wait_ge(xT_ok, u + 1)
                        if f >= 1:
                            e.wait_ge(xs_used, [0, 0, 4, 4, 4][f] + (g if f in (1, 4) else 0))
                        if f < 2:
                            e.activation(xTs[:], bank(0), ACT.Copy).then_inc(xs_ok, 1)
                        else:
                            c = {2: 0, 3: 4, 4: 6}[f]
                            e.activation(xTs[:], bank(0), ACT.Identity, scale=cols[:, c:c + 1],
                                         bias=cols[:, c + 1:c + 2]).then_inc(xs_ok, 1)
                        if f == 1:
                            e.wait_ge(ex_in, g + 1)
                            e.activation(lg[:, :, 0:NE0 - 1], lg[:, :, 0:NE0 - 1], ACT.Exp).then_inc(ex_ok, 1)
                        if f == 4:
                            e.wait_ge(ex_in, 4 + g + 1)
                            ps = PS[:, 7, 0:GT * NE1].rearrange("p (t x) -> p t x", t=GT)
                            e.activation(lg[:, :, 0:NE1], ps, ACT.Exp, scale=-1.0).then_inc(ex_ok, 1)

            def attention(a):
                HB = NH * a

                def evacuate(k, buf, before):
                    e.wait_ge(pv_done, 4 + 8 * (HB + k))
                    e.wait_ge(o_out[buf], before)
                    e.activation(Ob[:, buf, :], PS[:, 6, 0:256], ACT.Copy).then_inc(o_copied, 1)

                def position(i, s):
                    n = SLOTS * i + s
                    for x in range(16):
                        kt, qh = x // 2, x % 2
                        e.wait_ge(st_done, 16 * (HB + n) + x + 1)
                        if qh == 0:
                            e.wait_ge(pv_done, 8 * (HB + n) + kt + 1)
                        e.activation(PR[:, kt % 4, qh * GW:(qh + 1) * GW], bank(x % 2), ACT.Exp, scale=SCALE)\
                            .then_inc(exp_done, 1)
                        if x == 1:
                            evacuate(n, s % 2, 16 * ((17 - s % 2) * a + 2 * i + s // 2))

                e.wait_ge(o_zero, a + 1)
                with e.Fori(0, NH // SLOTS) as i:
                    for s in range(SLOTS):
                        position(i, s)
                evacuate(NH, 0, 16 * (17 * a + 16))

            def relative_attention():
                def exp(n, s, qt, k):
                    e.wait_ge(rmax, k + 1)
                    e.wait_ge(rt_done, k - 1) if not isinstance(k, int) or k >= 1 else None
                    e.activation(PR[:, qt % 2, :], PS[:, 2 * (qt % 2):2 * (qt % 2) + 2, :]
                                 .rearrange("p a b -> p (a b)"), ACT.Exp, bias=M[:, s, qt:qt + 1]).then_inc(rexp, 1)

                def position(i, s, last):
                    n = 2 * i + s
                    end = last and s == 1
                    for qt in range(QT):
                        u = 8 * n + qt
                        if qt < 7:
                            exp(n, s, qt + 1, u + 1)
                        elif not end:
                            exp(n + 1, 1 - s, 0, u + 1)
                        e.wait_ge(rt_done, u + 1)
                        if qt % 4 == 0:
                            e.wait_ge(rpv, 2 * n + qt // 4)
                        e.activation(PT[:, qt // 4, 0:4, qt % 4, :], PS[:, 4, :].rearrange("p (k q) -> p k q", k=4),
                                     ACT.Copy).then_inc(rev_a, 1)
                    e.wait_ge(rpv, 2 * n + 2)
                    e.wait_ge(o_out[s], 16 * ((17 - s) * 2 + i))
                    e.activation(Ob[:, s, :], PS[:, 7, 0:256], ACT.Copy).then_inc(ro_copied, 1)

                exp(0, 0, 0, 0)
                with e.Fori(0, NH // 2 - 1) as i:
                    for s in range(2):
                        position(i, s, False)
                for s in range(2):
                    position(NH // 2 - 1, s, True)

            def experts0():
                with e.Fori(0, NE0 // 2) as i:
                    for s in range(2):
                        for tg in range(NG):
                            v = NG * (2 * i + s) + tg
                            for c, (lo, w) in enumerate(FCH):
                                e.wait_ge(g_ps, 3 * v + c + 1)
                                e.wait_ge(h_ok, 3 * v)
                                e.activation(sg[0:w, c, :], PS[0:w, [1, 2, 1][c], :], ACT.Silu).then_inc(sg_ok, 1)

            def experts1():
                V0 = NG * NE0
                with e.Fori(0, NE1 // 2) as i:
                    for s in range(2):
                        for tg in range(NG):
                            v = NG * (2 * i + s) + tg
                            e.wait_ge(g_ps, 3 * V0 + v + 1)
                            e.activation(sg[:, tg % 2, :], bank(2 * (tg % 2) + 1), ACT.Relu).then_inc(sg_ok, 1)

            plan = [lambda: front(0), lambda: attention(0), lambda: front(1), experts0, lambda: front(2),
                    lambda: attention(1), lambda: front(3), relative_attention, lambda: front(4), experts1]
            for k, run in enumerate(plan[:upto]):
                run()
                meet(e, "act", k + 1)

        @block.gpsimd
        def _(e):
            own = Steps(e, own_pool)
            own(e.memset(zrow[:], 0.0))
            own(e.memset(nil[:], 0.0))
            own(e.memset(Va[:], 0.0))
            own(e.memset(Ws[:], 0.0))
            own.settle()
            own(e.memset(Ks[64:ROWS], 1.0))
            own(e.memset(Qs[64:ROWS], 0.0))
            own.settle()
            own(e.memset(Va[:, :, :, DH:DH + 1], 1.0))
            own.settle()
            e.wait_ge(c_in, 16 * N_CONST)
            own(e.tensor_copy(identb[:], ident[:]))
            own(e.tensor_copy(sel[0:ROWS], sel0[:].unsqueeze(2).broadcast_to([ROWS, NE1, P])))
            own.settle()

            def copy(dst, src):
                zeros = nil[:, 0:1]
                for _ in range(len(src.shape) - 2):
                    zeros = zeros.unsqueeze(1)
                return e.tensor_tensor(dst, src, zeros.broadcast_to(list(src.shape)), ALU.add)

            def front(f):
                with own.loop(NB, 2 * (4 if f in (0, 2, 3) else 0)) as b:
                    for half in range(2):
                        g = 2 * b + half
                        if f in (0, 2, 3):
                            a2 = {0: 0, 2: 1, 3: 2}[f]
                            e.wait_ge(kin_ok, 4 * a2 + g + 1)
                            e.wait_ge(stk_out, 16 * (24 * a2 + 6 * g))
                            kk = qk[:, 1, :]
                            own(copy(sp[:, 1, 0, :], kk))
                            own.settle()
                            own(e.tensor_tensor(kk, kk, sp[:, 1, 0, :], ALU.subtract))
                            own.settle()
                            own(copy(sp[:, 1, 1, :], kk))
                            own.settle()
                            own(e.tensor_tensor(kk, kk, sp[:, 1, 1, :], ALU.subtract))
                            own.settle()
                            copy(sp[:, 1, 2, :], kk).then_inc(split_k, 1)
                        else:
                            e.wait_ge(xs_ok, 4 * f + g + 1)
                            copy(XT[:, bass.ts(g, GW)], xTs[:]).then_inc(xs_used, 1)
                if f in (1, 4):
                    e.wait_ge(xs_used, [4, 8][f == 4])

            def value_slot(n, s, ready):
                copy(Va[:, s, :, 0:DH], Vt[:, bass.ds(n, 1), :, :].rearrange("p n k d -> p (n k) d"))\
                    .then_inc(ready, 1)

            def attention(a):
                HB = NH * a

                def split_max(n, s):
                    e.wait_ge(max_done, 2 + 8 * (HB + n + 1))
                    own(copy(Ms[:, s, 0, :], M[:, s, :]))
                    own.settle()
                    own(e.tensor_tensor(Mr[:, 0, :], M[:, s, :], Ms[:, s, 0, :], ALU.subtract))
                    own.settle()
                    own(copy(Ms[:, s, 1, :], Mr[:, 0, :]))
                    own.settle()
                    own(e.tensor_tensor(Mr[:, 1, :], Mr[:, 0, :], Ms[:, s, 1, :], ALU.subtract))
                    own.settle()
                    copy(Ms[:, s, 2, :], Mr[:, 1, :]).then_inc(m_split, 1)
                    e.wait_ge(m_split, HB + n + 1)

                for n in range(2):
                    value_slot(n, n, v_ready)
                    split_max(n, n)
                with own.loop(NH // SLOTS - 1, 4 * SLOTS) as i:
                    for s in range(SLOTS):
                        split_max(SLOTS * i + s + 2, (s + 2) % SLOTS)
                        value_slot(SLOTS * i + s + 2, (s + 2) % SLOTS, v_ready)
                for s in range(2):
                    n = NH - SLOTS + s + 2
                    split_max(n, n % SLOTS)
                    value_slot(n, n % SLOTS, v_ready)

            def relative_attention():
                def add(n, s, h):
                    e.wait_ge(prep_mul, 4 * n + 2 * h + 2)
                    e.tensor_tensor(At[:, s, h * GW:(h + 1) * GW], tA[:, 0, :], tA[:, 1, :], ALU.add)\
                        .then_inc(prep_add, 1)

                for n in range(2):
                    value_slot(n, n, rv_ready)
                for h in range(2):
                    add(0, 0, h)
                with e.Fori(0, NH // 2 - 1) as i:
                    for s in range(2):
                        n = 2 * i + s
                        for h in range(2):
                            add(n + 1, 1 - s, h)
                        e.wait_ge(rpv, 2 * n + 2)
                        value_slot(n + 2, s, rv_ready)
                for h in range(2):
                    add(NH - 1, 1, h)

            plan = [lambda: front(0), lambda: attention(0), lambda: front(1), lambda: None, lambda: front(2),
                    lambda: attention(1), lambda: front(3), relative_attention, lambda: front(4), lambda: None]
            for k, run in enumerate(plan[:upto]):
                run()
                meet(e, "pool", k + 1)


SHAPES = {
    "x": ([TT * P, P], F32), "ident": ([P, P], F32), "w_qkv": ([P, 3, 5 * P], F32),
    "rope": ([P, 2, L], F32), "w_out": ([P, 3, P], F32), "cols": ([P, 8], F32), "rows": ([P, 3, P], F32),
    "rel": ([P, 3, L], F32), "w_rt0": ([P, 8], F32), "w_rt1": ([P, NE1], F32), "sel0": ([ROWS, NE1], F32),
    "wpT": ([P, 2 * P], F32),
    "gu": ([NE0, P, 2, FI], F32), "dn": ([NE0, P, 3, P], F32), "kv": ([NE1, P, 2, P], F32),
}


def layout(i):
    i = {k: np.asarray(v) for k, v in i.items()}
    half = DH // 2
    swap = np.arange(P).reshape(H, 2, half)[:, ::-1].reshape(-1)
    w0 = i["L0_attn_Wqkv"]
    q0, k0, v0 = w0[:, 0:P], w0[:, P:2 * P], w0[:, 2 * P:3 * P]
    w1 = i["L1_attn_W_qkv"].T
    q1, k1, v1 = w1[:, 0:P], w1[:, P:2 * P], w1[:, 2 * P:3 * P]
    q2, k2, v2 = i["L1_ffn_wq"], i["L1_ffn_wk"], i["L1_ffn_wv"]
    w_qkv = np.stack([np.concatenate([q0, q0[:, swap], k0, k0[:, swap], v0], 1),
                      np.concatenate([q1, q1, k1, k1, v1], 1),
                      np.concatenate([q2, q2, k2, k2, v2], 1)], 1)
    w_out = np.stack([i["L0_attn_Wo"], i["L1_attn_W_out"].T, i["L1_ffn_wo"]], 1)
    b1 = i["L1_attn_b_qkv"]
    cols = np.stack([i["L1_attn_ln_gamma"], i["L1_attn_ln_beta"], b1[0:P], b1[P:2 * P],
                     i["L1_ffn_ln1_g"], i["L1_ffn_ln1_b"], i["L1_ffn_ln2_g"], i["L1_ffn_ln2_b"]], 1)
    rb = np.zeros(P, np.float32)
    rb[0:NE0 - 1] = i["L0_ffn_rb"]
    rows = np.broadcast_to(np.stack([b1[2 * P:3 * P], i["L1_attn_b_out"], rb])[None], (P, 3, P))
    w_rt0 = np.zeros((P, 8), np.float32)
    w_rt0[:, 0:NE0 - 1] = i["L0_ffn_wr"].T
    gate = np.concatenate([i["L0_ffn_sg"][None], i["L0_ffn_rg"]])
    up = np.concatenate([i["L0_ffn_su"][None], i["L0_ffn_ru"]])
    down = np.concatenate([i["L0_ffn_sd"][None], i["L0_ffn_rd"]])
    gu = np.stack([gate.transpose(0, 2, 1), up.transpose(0, 2, 1)], 2)
    dn = np.zeros((NE0, P, 3, P), np.float32)
    for c, (lo, w) in enumerate(FCH):
        dn[:, 0:w, c, :] = down[:, :, lo:lo + w].transpose(0, 2, 1)
    kv = np.stack([i["L1_ffn_keys"], i["L1_ffn_values"]], 2)
    wpT = i["L1_ffn_wp"].T
    swapped = np.concatenate([np.arange(P // 2, P), np.arange(P // 2)])
    rope, rel = tables()
    return {
        "x": i["L0_attn_x"].reshape(TT * P, P), "ident": np.eye(P, dtype=np.float32),
        "w_qkv": w_qkv, "rope": rope, "w_out": w_out, "cols": cols, "rows": rows, "rel": rel, "w_rt0": w_rt0,
        "w_rt1": i["L1_ffn_sel_w"], "sel0": np.tile(np.eye(NE1, dtype=np.float32), (PARTS, 1)),
        "wpT": np.concatenate([wpT, wpT[:, swapped]], 1),
        "gu": gu, "dn": dn, "kv": kv,
    }


def kernel(**inputs):
    import concourse.bacc as bacc
    from concourse.bass_utils import run_bass_kernel_spmd

    arrays = {f"in_{k}": np.ascontiguousarray(v) for k, v in layout(inputs).items()}
    nc = bacc.Bacc("TRN2", target_bir_lowering=False, num_devices=1)
    A = {}
    for name, (shape, dt) in SHAPES.items():
        assert list(arrays[f"in_{name}"].shape) == shape, (name, arrays[f"in_{name}"].shape)
        A[name] = nc.dram_tensor(f"in_{name}", shape, dt, kind="ExternalInput").ap()
    out = nc.dram_tensor("out", [TT * P, P], F32, kind="ExternalOutput").ap()
    two_layers(nc, A, out)
    r = run_bass_kernel_spmd(nc, [arrays], core_ids=[0])
    return np.asarray(r.results[0]["out"]).reshape(NB, L, P)
```

```python
from contextlib import ExitStack, contextmanager

import numpy as np

import concourse.bass as bass
from concourse import mybir
from concourse.alu_op_type import AluOpType as ALU

F32 = mybir.dt.float32
F32R = mybir.dt.float32r
BF16 = mybir.dt.bfloat16
ACT = mybir.ActivationFunctionType
AX = mybir.AxisListType

P = 128
NB, L = 2, 1024
H, DH = 16, 8
NH = NB * H
TT = NB * L // P
GT, GW = 4, 512
NG = TT // GT
QT = L // P
EPS = 1e-5
SCALE = DH ** -0.5
PARTS = 3
STACK = PARTS * PARTS * DH
ROWS = 96
VC = 32
NE0, FI = 8, 352
FCH = [(0, 128), (128, 128), (256, 96)]
NE1 = 32
SLOTS = 4


def tables():
    t = np.arange(L, dtype=np.float32)
    inv = (1.0 / 10000.0 ** (np.arange(0, DH, 2, dtype=np.float32) / DH)).astype(np.float32)
    ang = (t[:, None] * inv[None, :]).astype(np.float32)
    ang = np.tile(np.concatenate([ang, ang], 1), (1, H)).T.astype(np.float64)
    sign = np.where(np.arange(P) % DH < DH // 2, -1.0, 1.0)[:, None]
    rope = np.stack([np.cos(ang), np.sin(ang) * sign], 1).astype(np.float32)
    finv = (1.0 / 10000.0 ** (np.arange(0, P, 2, dtype=np.float32) / P)).astype(np.float32)
    fang = finv.astype(np.float64)[:, None] * t.astype(np.float64)[None, :]
    s, c = np.sin(fang), np.cos(fang)
    rel = np.stack([np.concatenate([s, c]), np.concatenate([c, c]), np.concatenate([s, -s])], 1)
    return rope, rel.astype(np.float32)


class Steps:

    def __init__(self, eng, sem):
        self.eng, self.sem, self.base, self.k, self.i, self.per = eng, sem, 0, 0, None, 0

    def now(self):
        return self.base + self.k if self.i is None else self.base + self.i * self.per + self.k

    def __call__(self, ins):
        ins.then_inc(self.sem, 1)
        self.k += 1

    def settle(self):
        self.eng.wait_ge(self.sem, self.now())

    @contextmanager
    def loop(self, trips, per):
        self.base, self.k, self.per = self.base + self.k, 0, per
        with self.eng.Fori(0, trips) as i:
            self.i = i
            yield i
        assert self.k == per, (self.k, per)
        self.base, self.k, self.i = self.base + trips * per, 0, None


def two_layers(nc, A, out, upto=99):
    with ExitStack() as ctx:
        def sb(name, shape, dt=F32):
            return ctx.enter_context(nc.sbuf_tensor(name, shape, dt))

        def sem(name):
            return ctx.enter_context(nc.semaphore(name))

        PS = ctx.enter_context(nc.psum_tensor("PS", [P, 8, GW], F32))

        def bank(b, dt=F32):
            return PS[:, b, :] if dt == F32 else PS[:, b, :].bitcast(dt)

        q_stack = nc.dram_tensor("q_stack", [9, NB * P, L], BF16)
        k_stack = nc.dram_tensor("k_stack", [9, NB * P, L], BF16)
        w_stack = nc.dram_tensor("w_stack", [9, NB * P, 2 * P], BF16)
        o_dram = nc.dram_tensor("o_dram", [NH + 1, 4, 32, 256], F32)

        X = sb("X", [P, TT, P])
        SRC = sb("SRC", [P, TT, P])
        XT = sb("XT", [P, TT * P])
        ident = sb("ident", [P, P])
        identb = sb("identb", [P, P], BF16)
        w_qkv = sb("w_qkv", [P, 3, 5 * P])
        w_out = sb("w_out", [P, 3, P])
        rope = sb("rope", [P, 2, L])
        rel = sb("rel", [P, 2, L])
        cols = sb("cols", [P, 8])
        rows = sb("rows", [P, 3, P])
        w_rt0 = sb("w_rt0", [P, 8])
        w_rt1 = sb("w_rt1", [P, NE1])
        Qs = sb("Qs", [P, SLOTS, L], BF16)
        Ks = sb("Ks", [P, SLOTS, L], BF16)
        zrow = sb("zrow", [PARTS, L], BF16)
        Vt = sb("Vt", [P, NH, QT, DH])
        Va = sb("Va", [P, SLOTS, QT, VC])
        M = sb("M", [P, SLOTS, QT])
        Mr = sb("Mr", [P, 2, QT])
        Ms = sb("Ms", [P, SLOTS, PARTS, QT], BF16)
        MT = sb("MT", [PARTS * QT, SLOTS, P], BF16)
        PR = sb("PR", [P, 4, L])
        Ob = sb("Ob", [P, 2, 256])
        Ws = sb("Ws", [P, 2, 2 * P], BF16)
        Ah = sb("Ah", [P, 2, L], F32R)
        Al = sb("Al", [P, 2, L], F32R)
        Eh = sb("Eh", [P, L], F32R)
        El = sb("El", [P, L], F32R)
        BIG = sb("BIG", [P, 2 * QT * 4 * P])
        PT = BIG[:].rearrange("p (a k g q) -> p a k g q", a=2, k=QT, g=4)
        st = sb("st", [P, GT, 6])
        mv = sb("mv", [P, GT, 2])
        sd = sb("sd", [P, 2, GT])
        xn = sb("xn", [P, GT, P])
        xTs = sb("xTs", [P, GW])
        qk = sb("qk", [P, 2, GW])
        rt = sb("rt", [P, 2, GW])
        At, tA = qk, rt
        sp = sb("sp", [P, 2, PARTS, GW], BF16)
        atu = rope[:].rearrange("p a (b t) -> p a b t", b=2)
        atn = sb("atn", [P, 2, GW])
        lg = sb("lg", [P, GT, NE1 + 8])
        lg2 = sb("lg2", [P, GT, NE1 + 8])
        m8 = sb("m8", [P, GT, 8])
        rp = sb("rp", [P, GT, 8])
        sm = sb("sm", [P, 2, GT])
        nil = sb("nil", [P, 1])
        gate = sb("gate", [P, GT, NE1])
        gres = sb("gres", [P, 2, GT, NE1])
        gsp = sb("gsp", [P, GT, PARTS, NE1], BF16)
        GTs = sb("GTs", [P, TT * P], BF16)
        sel0 = sb("sel0", [ROWS, NE1])
        sel = sb("sel", [P, NE1, P], BF16)
        wg = sb("wg", [P, 2, 2, FI])
        wd = sb("wd", [P, 2, 3, P])
        hh = BIG[:, 0:6 * GW].rearrange("p (a c t) -> p a c t", a=2, c=3)
        sg = BIG[:, 6 * GW:9 * GW].rearrange("p (c t) -> p c t", c=3)
        xw = BIG[:, 9 * GW:11 * GW].rearrange("p (a t) -> p a t", a=2)
        we = wg[:, :, :, 0:P]
        acc = PR[:].rearrange("p a (b t) -> p (a b) t", b=2)[:, 0:NG, :]

        x_in = [sem(f"x_in{g}") for g in range(NG)]
        w_in, rope_in, c_in = map(sem, "w_in rope_in c_in".split())
        stage = {e: sem(f"stage_{e}") for e in ("sp", "act", "pool", "pe", "dve")}
        own_dve, own_pool, own_act = sem("own_dve"), sem("own_pool"), sem("own_act")
        at_in = [sem(f"at_in{s}") for s in range(2)]
        atn_ok, wo_ok, var_ok, sd_ok, xn_ok, xT_ok, xs_ok, xs_used = map(
            sem, "atn_ok wo_ok var_ok sd_ok xn_ok xT_ok xs_ok xs_used".split())
        proj_ok, split_k, stk_out, v_ok, xres = map(sem, "proj_ok split_k stk_out v_ok xres".split())
        kin_ok, split_q, lgt_ok, ex_in, ex_ok, gsp_ok, gtp_ok, gt_ok = map(
            sem, "kin_ok split_q lgt_ok ex_in ex_ok gsp_ok gtp_ok gt_ok".split())
        w_out_ok = sem("w_out_ok")
        wp_in, table_in, table_split, wsplit = map(sem, "wp_in table_in table_split wsplit".split())
        qk_in = [sem(f"qk_in{s}") for s in range(SLOTS)]
        m_in = [sem(f"m_in{s}") for s in range(SLOTS)]
        o_out = [sem(f"o_out{s}") for s in range(2)]
        v_ready, s_done, max_done, m_split, mt_done, mt_copied = map(
            sem, "v_ready s_done max_done m_split mt_done mt_copied".split())
        st_done, exp_done, pv_done, o_copied, o_zero = map(
            sem, "st_done exp_done pv_done o_copied o_zero".split())
        ws_in = [sem(f"ws_in{s}") for s in range(2)]
        prep_ps, prep_mul, prep_add, prep_split = map(sem, "prep_ps prep_mul prep_add prep_split".split())
        rs_done, rmax, rexp, rt_done, rev_a, rev_d, rpv = map(
            sem, "rs_done rmax rexp rt_done rev_a rev_d rpv".split())
        ro_copied = sem("ro_copied")
        rv_ready = sem("rv_ready")
        ew_in = [sem(f"ew_in{s}") for s in range(2)]
        acc_zero = sem("acc_zero")
        b_ps, g_ps, u_ps, xw_ok, sg_ok, h_ok, dn_ok, acc_ok = map(
            sem, "b_ps g_ps u_ps xw_ok sg_ok h_ok dn_ok acc_ok".split())
        y_out = sem("y_out")

        block = ctx.enter_context(nc.Block())

        N_CONST = 8

        def meet(eng, me, k):
            if k not in MEETINGS:
                return
            k = MEETINGS.index(k) + 1
            eng.sem_inc(stage[me], 1)
            for other in stage:
                if other != me:
                    eng.wait_ge(stage[other], k)

        MEETINGS = [3, 4, 9, 10]

        STARTS = {"sp": o_out, "pe": [st_done, rt_done, rpv], "act": [sg_ok, rev_a, ro_copied], "dve": [h_ok, rev_d]}

        def start(eng, me):
            for sm_ in STARTS[me]:
                eng.sem_inc(sm_, 1)

        @block.sync
        def _(e):
            start(e, "sp")
            x_t = A["x"].rearrange("(t p) d -> p t d", p=P)
            for g in range(NG):
                e.dma_start(X[:, GT * g:GT * g + GT, :], x_t[:, GT * g:GT * g + GT, :]).then_inc(x_in[g], 16)
                if g == 0:
                    e.dma_start(ident[:], A["ident"]).then_inc(w_in, 16)
                    e.dma_start(w_qkv[:, 0, :], A["w_qkv"][:, 0, :]).then_inc(w_in, 16)
            e.dma_start(rope[:], A["rope"]).then_inc(rope_in, 16)
            loads = [(w_qkv[:, 1:3, :], A["w_qkv"][:, 1:3, :]), (w_out[:], A["w_out"]), (cols[:], A["cols"]), (rows[:], A["rows"]),
                     (rel[:], A["rel"][:, 1:3, :]), (w_rt0[:], A["w_rt0"]), (w_rt1[:], A["w_rt1"]),
                     (sel0[:], A["sel0"])]
            for dst, src in loads:
                e.dma_start(dst, src).then_inc(c_in, 16)
            assert len(loads) == N_CONST

            def stacks_out(f, b, half):
                u = 4 * f + 2 * b + half
                for which, ready, dst in ((0, split_q, q_stack), (1, split_k, k_stack)):
                    e.wait_ge(ready, 4 * QKV.index(f) + 2 * b + half + 1)
                    d = dst[:, bass.ts(b, P), half * GW:(half + 1) * GW]
                    if which == 0:
                        for i in range(PARTS):
                            e.dma_start(d[PARTS * i:PARTS * i + PARTS].rearrange("j p t -> p j t"),
                                        sp[:, 0, i, :].unsqueeze(1).broadcast_to([P, PARTS, GW])).then_inc(stk_out, 16)
                    else:
                        for j in range(PARTS):
                            dj = d.rearrange("(i j) p t -> j p i t", j=PARTS)[j]
                            e.dma_start(dj, sp[:, 1, j, :].unsqueeze(1).broadcast_to([P, PARTS, GW]))\
                                .then_inc(stk_out, 16)

            def attention_in(k, b, half, relative):
                u = 4 * k + 2 * b + half
                e.wait_ge(atn_ok, max(0, u - 1))
                heads = o_dram[1 + H * b:1 + H * b + H]
                if relative:
                    pieces = [(g, slice(half * P, half * P + P)) for g in range(4)]
                else:
                    pieces = [(2 * half + g, slice(0, 256)) for g in range(2)]
                w = GW // len(pieces)
                for n, (g, q) in enumerate(pieces):
                    src = heads[:, g, :, q]
                    e.dma_start(atu[:, half, 0, n * w:(n + 1) * w], src[:, 0:DH, :]).then_inc(at_in[half], 16)
                    e.dma_start(atu[:, half, 1, n * w:(n + 1) * w],
                                src[:, DH:DH + 1, :].broadcast_to([H, DH, w])).then_inc(at_in[half], 16)

            def load_qk(a, n, s):
                e.dma_start(Qs[0:STACK, s, :], q_stack[:, bass.ts(n, DH), :]).then_inc(qk_in[s], 16)
                e.dma_start(Qs[STACK:STACK + PARTS, s, :], zrow[:, :]).then_inc(qk_in[s], 16)
                e.dma_start(Ks[0:STACK, s, :], k_stack[:, bass.ts(n, DH), :]).then_inc(qk_in[s], 16)

            def load_rel(n, s):
                load_qk(2, n, s)
                e.dma_start(Ws[0:STACK, s, :], w_stack[:, bass.ts(n, DH), :]).then_inc(ws_in[s], 16)

            def attention(a):
                def max_rows(n, s):
                    e.wait_ge(mt_copied, NH * a + n + 1)
                    e.dma_start(Qs[STACK:STACK + PARTS, s, :], MT[:, s, :]).then_inc(m_in[s], 16)

                def position(i, s, last):
                    n = SLOTS * i + s
                    if not (last and s >= 1):
                        e.wait_ge(st_done, 1 + 16 * (NH * a + n))
                        load_qk(a, n + 3, (s + 3) % SLOTS)
                    e.wait_ge(o_copied, (NH + 1) * a + n + 1)
                    e.dma_start(o_dram[bass.ds(n, 1)].rearrange("n g c q -> (n g c) q"), Ob[:, s % 2, :])\
                        .then_inc(o_out[s % 2], 16)
                    if not (last and s == 3):
                        max_rows(n + 1, (s + 1) % SLOTS)

                max_rows(0, 0)
                with e.Fori(0, NH // SLOTS - 1) as i:
                    for s in range(SLOTS):
                        position(i, s, False)
                e.wait_ge(o_out[0], 1 + 16 * (17 * a + NH // 2 - 2))
                e.wait_ge(o_out[1], 1 + 16 * (16 * a + NH // 2 - 2))
                for half in range(2):
                    attention_in(a, 0, half, False)
                for s in range(SLOTS):
                    position(NH // SLOTS - 1, s, True)
                e.wait_ge(o_copied, (NH + 1) * (a + 1))
                e.dma_start(o_dram[NH:NH + 1].rearrange("n g c q -> (n g c) q"), Ob[:, 0, :]).then_inc(o_out[0], 16)
                e.wait_ge(o_out[0], 1 + 16 * 17 * (a + 1))
                e.wait_ge(o_out[1], 1 + 16 * 16 * (a + 1))

            def relative_attention():
                def position(i, s, last):
                    n = 2 * i + s
                    e.wait_ge(ro_copied, 1 + n + 1)
                    e.dma_start(o_dram[bass.ds(n + 1, 1)].rearrange("n g c q -> (n g c) q"), Ob[:, s, :])\
                        .then_inc(o_out[s], 16)
                    if not last:
                        load_rel(n + 2, s)

                with e.Fori(0, NH // 2 - 1) as i:
                    for s in range(2):
                        position(i, s, False)
                e.wait_ge(o_out[0], 1 + 16 * (17 * 2 + NH // 2 - 1))
                e.wait_ge(o_out[1], 1 + 16 * (16 * 2 + NH // 2 - 1))
                for half in range(2):
                    attention_in(2, 0, half, True)
                for s in range(2):
                    position(NH // 2 - 1, s, True)
                e.wait_ge(o_out[0], 1 + 16 * (17 * 2 + NH // 2))
                e.wait_ge(o_out[1], 1 + 16 * (16 * 2 + NH // 2))

            def load_expert(k, x, s):
                if k == 0:
                    e.dma_start(wg[:, s, :, :], A["gu"][bass.ds(x, 1)].rearrange("x p a f -> (x p) a f"))\
                        .then_inc(ew_in[s], 16)
                    e.dma_start(wd[:, s, :, :], A["dn"][bass.ds(x, 1)].rearrange("x p c f -> (x p) c f"))\
                        .then_inc(ew_in[s], 16)
                else:
                    e.dma_start(we[:, s, :, :], A["kv"][bass.ds(x, 1)].rearrange("x p a f -> (x p) a f"))\
                        .then_inc(ew_in[s], 16)

            def experts(k):
                with e.Fori(0, [NE0, NE1][k] // 2 - 1) as i:
                    for s in range(2):
                        e.wait_ge(dn_ok, NG * (NE0 * k + 2 * i + s + 1))
                        load_expert(k, 2 * i + s + 2, s)

            QKV = [0, 2, 3]

            def front(f):
                if f == 3:
                    e.dma_start(PR[:, 3, :], A["rel"][:, 0, :]).then_inc(table_in, 16)
                    e.wait_ge(wsplit, 1)
                    for b in range(NB):
                        d = w_stack[:, b * P:(b + 1) * P, :].rearrange("(i j) p t -> j p i t", j=PARTS)
                        for j in range(PARTS):
                            src = PT[:, 1, j, 0:2, :].rearrange("p a f -> p (a f)").bitcast(BF16)[:, 0:2 * P]
                            e.dma_start(d[j], src.unsqueeze(1).broadcast_to([P, PARTS, 2 * P])).then_inc(w_out_ok, 16)
                if f in (1, 4):
                    for s in range(2):
                        load_expert(f // 4, s, s)
                for g in range(NG):
                    if f in (1, 3, 4) and g < 2:
                        attention_in({1: 0, 3: 1, 4: 2}[f], 1, g, f == 4)
                    if f not in QKV:
                        continue
                    stacks_out(f, g // 2, g % 2)
                    if g == 1:
                        e.wait_ge(stk_out, 16 * (24 * QKV.index(f) + 12))
                        if f < 3:
                            for n in range(3):
                                load_qk(QKV.index(f), n, n)
                        else:
                            e.wait_ge(w_out_ok, 16 * 6)
                            load_rel(0, 0)
                            load_rel(1, 1)
                if f in QKV:
                    e.wait_ge(stk_out, 16 * 24 * (QKV.index(f) + 1))

            def attention1():
                e.dma_start(PT[:, 0, 0:2, 0, :], A["wpT"].rearrange("p (a f) -> p a f", a=2)).then_inc(wp_in, 16)
                attention(1)

            plan = [lambda: front(0), lambda: attention(0), lambda: front(1), lambda: experts(0), lambda: front(2),
                    attention1, lambda: front(3), relative_attention, lambda: front(4), lambda: experts(1)]
            for k, run in enumerate(plan[:upto]):
                run()
                meet(e, "sp", k + 1)
            if upto > len(plan):
                e.wait_ge(xres, 8)
            o_t = out.rearrange("(t p) d -> p t d", p=P)
            for g in range(NG):
                e.dma_start(o_t[:, GT * g:GT * g + GT, :], X[:, GT * g:GT * g + GT, :]).then_inc(y_out, 16)
            e.wait_ge(y_out, 16 * NG)

        @block.tensor
        def _(e):
            start(e, "pe")
            e.wait_ge(w_in, 16 * 2)

            def transpose(dst, src):
                return e.transpose(dst, src, ident[:])

            def front(f):
                a = {1: 0, 3: 1, 4: 2}.get(f)
                a2 = {0: 0, 2: 1, 3: 2}.get(f)

                def gates(g):
                    r = 4 * (f == 4) + g
                    e.wait_ge(gsp_ok, r + 1)
                    e.wait_ge(gt_ok, r)
                    for t in range(GT):
                        m = e.transpose(bank(1, BF16)[0:ROWS, t * P:(t + 1) * P],
                                        gsp[:, t, :, :].rearrange("p a x -> p (a x)"), identb[:])
                    m.then_inc(gtp_ok, 1)

                def project_out(g):
                    if a is None or g >= NG:
                        return
                    e.wait_ge(atn_ok, 4 * a + g + 1)
                    if g == 1:
                        e.wait_ge(o_copied if a < 2 else ro_copied, (NH + 1) * (a + 1) if a < 2 else 1 + NH)
                    for t in range(GT):
                        m = e.matmul(PS[:, [4, 6][g % 2], t * P:(t + 1) * P], atn[:, g % 2, t * P:(t + 1) * P],
                                     w_out[:, a, :], start=True, stop=True)
                    m.then_inc(wo_ok, 1)

                project_out(0)
                project_out(1)
                for g in range(NG):
                    u = 4 * f + g
                    e.wait_ge(xn_ok, u + 1)
                    for t in range(GT):
                        m = transpose(PS[:, 0, t * P:(t + 1) * P], xn[:, t, :])
                    m.then_inc(xT_ok, 1)
                    if g:
                        project_out(g + 1)
                    e.wait_ge(xs_ok, u + 1)
                    if a2 is not None:
                        e.wait_ge(v_ok, 4 * a2 + g)
                        for w, bk in ((2, 3), (3, 4), (0, 1), (1, 2)):
                            if f == 0 or w % 2 == 0:
                                e.matmul(bank(bk), w_qkv[:, a2, w * P:(w + 1) * P], xTs[:], start=True, stop=True)\
                                    .then_inc(proj_ok, 1)
                        for t in range(GT):
                            m = e.matmul(PS[:, 5, t * P:(t + 1) * P], xTs[:, t * P:(t + 1) * P],
                                         w_qkv[:, a2, 4 * P:5 * P], start=True, stop=True)
                        m.then_inc(proj_ok, 1)
                    else:
                        w, ne = (w_rt0[:, 0:NE0 - 1], NE0 - 1) if f == 1 else (w_rt1[:], NE1)
                        for t in range(GT):
                            m = e.matmul(PS[:, [7, 2][g % 2], t * NE1:t * NE1 + ne], xTs[:, t * P:(t + 1) * P], w,
                                         start=True, stop=True)
                        m.then_inc(lgt_ok, 1)
                        if g:
                            gates(g - 1)
                if a2 is None:
                    gates(NG - 1)

            def attention(a):
                HB = NH * a
                def scores(n, s, qt, kh):
                    if kh == 0:
                        e.wait_ge(max_done, 8 * (HB + n) + qt + 1)
                    m = e.matmul(bank(2 + 2 * (qt % 2) + kh), Qs[0:ROWS, s, qt * P:(qt + 1) * P],
                                 Ks[0:ROWS, s, kh * GW:(kh + 1) * GW], start=True, stop=True)
                    if kh == 1:
                        m.then_inc(s_done, 1)

                def max_transpose(n, s):
                    e.wait_ge(m_split, HB + n + 1)
                    e.wait_ge(mt_copied, HB + n)
                    e.transpose(bank(7, BF16)[0:PARTS * QT, 0:P], Ms[:, s, :, :].rearrange("p a q -> p (a q)"),
                                identb[:]).then_inc(mt_done, 1)

                def values(n, s, kt):
                    if kt == 0:
                        e.wait_ge(v_ready, HB + n + 1)
                        e.wait_ge(o_copied, (NH + 1) * a + n + 1)
                    for g in range(4):
                        m = e.matmul(PS[32 * g:32 * g + VC, 6, 0:256], Va[:, s, kt, :],
                                     PR[:, kt % 4, g * 256:(g + 1) * 256], start=(kt == 0), stop=(kt == QT - 1))
                    m.then_inc(pv_done, 1)

                def position(i, s, last):
                    n = SLOTS * i + s
                    s2 = (s + 2) % SLOTS
                    lead = not (last and s >= 2)
                    if lead:
                        e.wait_ge(qk_in[s2], 48 * (NH // SLOTS * a + i + (s >= 2) + 1))
                    e.wait_ge(m_in[s], 16 * (NH // SLOTS * a + i + 1))
                    for x in range(16):
                        e.wait_ge(exp_done, 16 * (HB + n) + x + 1)
                        kt, qh = x // 2, x % 2
                        e.matmul(bank(x % 2), Ks[0:ROWS, s, kt * P:(kt + 1) * P],
                                 Qs[0:ROWS, s, qh * GW:(qh + 1) * GW], start=True, stop=True).then_inc(st_done, 1)
                        if x == 6 and not (last and s == 3):
                            max_transpose(n + 1, (s + 1) % SLOTS)
                        if lead:
                            scores(n + 2, s2, x // 2, x % 2)
                        if x % 2 and x >= 3:
                            values(n, s, (x - 3) // 2)
                    e.wait_ge(exp_done, 2 + 16 * (HB + n) + 16)
                    values(n, s, QT - 1)

                if a == 0:
                    e.sem_inc(exp_done, 2)
                    e.sem_inc(pv_done, 4)
                e.wait_ge(v_ok, 4 * (a + 1))
                if a == 0:
                    e.wait_ge(c_in, 16 * N_CONST)
                for n in range(2):
                    e.wait_ge(qk_in[n], 48 * (NH // SLOTS * a + 1))
                    for x in range(16):
                        scores(n, n, x // 2, x % 2)
                max_transpose(0, 0)
                with e.Fori(0, NH // SLOTS - 1) as i:
                    for s in range(SLOTS):
                        position(i, s, False)
                for s in range(SLOTS):
                    position(NH // SLOTS - 1, s, True)

            def relative_attention():
                def prep(n, s, p):
                    if p == 0:
                        e.wait_ge(ws_in[s], 16 * (n // 2 + 1) if isinstance(n, int) else 16 * (n[0] + 1))
                        e.wait_ge(qk_in[s], 48 * (16 + 1 + (n // 2 if isinstance(n, int) else n[0])))
                    num = n if isinstance(n, int) else n[1]
                    e.wait_ge(prep_mul, 4 * num + p)
                    e.matmul(bank(6), Ws[0:ROWS, s, (p % 2) * P:(p % 2 + 1) * P],
                             Qs[0:ROWS, s, (p // 2) * GW:(p // 2 + 1) * GW], start=True, stop=True)\
                        .then_inc(prep_ps, 1)

                def scores(n, s, qt):
                    if qt % 4 == 0:
                        e.wait_ge(prep_split, 2 * n + qt // 4 + 1)
                    e.wait_ge(rexp, 8 * n + qt + 1)
                    for kh in range(2):
                        o = bank(2 * (qt % 2) + kh)
                        e.matmul(o, Qs[0:ROWS, s, qt * P:(qt + 1) * P], Ks[0:ROWS, s, kh * GW:(kh + 1) * GW],
                                 start=True, stop=False)
                        for n_a, a_part, e_part in ((0, Ah, El), (1, Al, Eh), (2, Ah, Eh)):
                            m = e.matmul(o, a_part[:, s, qt * P:(qt + 1) * P], e_part[:, kh * GW:(kh + 1) * GW],
                                         start=False, stop=(n_a == 2))
                    m.then_inc(rs_done, 1)

                def position(i, s, last):
                    n = 2 * i + s
                    end = last and s == 1
                    for qt in range(QT):
                        u = 8 * n + qt
                        e.wait_ge(rexp, 2 + u + 1)
                        e.wait_ge(rev_a, 1 + u)
                        e.wait_ge(rev_d, 1 + u)
                        for kt in range(QT):
                            m = transpose(PS[:, 4 + kt // 4, (kt % 4) * P:(kt % 4 + 1) * P],
                                          PR[:, qt % 2, kt * P:(kt + 1) * P])
                        m.then_inc(rt_done, 1)
                        if 2 <= qt < 6 and not end:
                            prep((i + (s == 1), n + 1), 1 - s, qt - 2)
                        if qt < 6:
                            scores(n, s, qt + 2)
                        elif not end:
                            scores(n + 1, 1 - s, qt - 6)
                        if qt % 4 == 3:
                            half = qt // 4
                            e.wait_ge(rev_a, 1 + u + 1)
                            e.wait_ge(rev_d, 1 + u + 1)
                            if half == 0:
                                e.wait_ge(ro_copied, 1 + n)
                                e.wait_ge(rv_ready, n + 1)
                            for kt in range(QT):
                                for g in range(4):
                                    m = e.matmul(PS[32 * g:32 * g + VC, 7, half * P:(half + 1) * P],
                                                 Va[:, s, kt, :], PT[:, half, kt, g, :],
                                                 start=(kt == 0), stop=(kt == QT - 1))
                            m.then_inc(rpv, 1)

                e.sem_inc(rexp, 2)
                e.wait_ge(v_ok, 12)
                for p in range(4):
                    prep(0, 0, p)
                e.wait_ge(table_split, 1)
                scores(0, 0, 0)
                scores(0, 0, 1)
                with e.Fori(0, NH // 2 - 1) as i:
                    for s in range(2):
                        position(i, s, False)
                for s in range(2):
                    position(NH // 2 - 1, s, True)

            def zero_acc(k):
                e.wait_ge(acc_zero, k + 1)
                for b in range(4, 8):
                    e.matmul(bank(b), acc[:, 0, 0:P], acc[:, 0, :], start=True, stop=True, skip_group_check=True)

            def spread(x, ring, tg):
                e.matmul(bank(ring), sel[0:ROWS, x, :], GTs[0:ROWS, tg * GW:(tg + 1) * GW], start=True, stop=True)\
                    .then_inc(b_ps, 1)

            def experts0():
                zero_acc(0)

                def down(s, tg):
                    for c, (lo, w) in enumerate(FCH):
                        m = e.matmul(bank(4 + tg), wd[0:w, s, c, :], hh[0:w, tg % 2, c, :],
                                     start=False, stop=True, skip_group_check=True)
                    m.then_inc(dn_ok, 1)

                def unit(i, s, tg):
                    x = 2 * i + s
                    v = NG * x + tg
                    first = s == 0 and tg == 0
                    if tg == 0:
                        e.wait_ge(ew_in[s], 32 * (i + 1))
                    xs = XT[:, tg * GW:(tg + 1) * GW]

                    def up(c, k, bk):
                        lo, w = FCH[c]
                        e.matmul(PS[0:w, bk, :], wg[:, s, k, lo:lo + w], xs if k == 0 else xw[:, tg % 2, :],
                                 start=True, stop=True).then_inc(u_ps if k else g_ps, 1)
                    e.wait_ge(h_ok, 1 + 3 * v - (0 if first else 1))
                    spread(x, 0, tg)
                    e.wait_ge(sg_ok, 1 + 3 * v)
                    up(0, 0, 1)
                    e.wait_ge(h_ok, 1 + 3 * v)
                    up(1, 0, 2)
                    if not first:
                        down(s if tg else 1 - s, (tg - 1) % NG)
                    e.wait_ge(xw_ok, v + 1)
                    up(0, 1, 3)
                    up(1, 1, 0)
                    e.wait_ge(sg_ok, 1 + 3 * v + 1)
                    up(2, 0, 1)
                    e.wait_ge(sg_ok, 1 + 3 * v + 2)
                    up(2, 1, 2)

                with e.Fori(0, NE0 // 2) as i:
                    for s in range(2):
                        for tg in range(NG):
                            unit(i, s, tg)
                    e.wait_ge(h_ok, 1 + 3 * NG * (2 * i + 2))
                    down(1, NG - 1)

            def experts1():
                zero_acc(1)
                V0 = NG * NE0

                def values(s, tg):
                    e.matmul(bank(4 + tg), we[:, s, 1, :], hh[:, tg % 2, 0, :], start=False, stop=True,
                             skip_group_check=True).then_inc(dn_ok, 1)

                def unit(i, s, tg):
                    x = 2 * i + s
                    v = NG * x + tg
                    first = s == 0 and tg == 0
                    if tg == 0:
                        e.wait_ge(ew_in[s], 32 * (NE0 // 2) + 16 * (i + 1))
                    e.wait_ge(h_ok, 1 + 3 * V0 + v - (0 if first else 1))
                    e.matmul(bank(2 * (tg % 2)), sel[0:ROWS, x, :], GTs[0:ROWS, tg * GW:(tg + 1) * GW],
                             start=True, stop=True).then_inc(b_ps, 1)
                    e.matmul(bank(2 * (tg % 2) + 1), we[:, s, 0, :], XT[:, tg * GW:(tg + 1) * GW],
                             start=True, stop=True).then_inc(g_ps, 1)
                    if not first:
                        e.wait_ge(h_ok, 1 + 3 * V0 + v)
                        values(s if tg else 1 - s, (tg - 1) % NG)

                with e.Fori(0, NE1 // 2) as i:
                    for s in range(2):
                        for tg in range(NG):
                            unit(i, s, tg)
                    e.wait_ge(h_ok, 1 + 3 * V0 + NG * (2 * i + 2))
                    values(1, NG - 1)

            def back(k):
                e.wait_ge(acc_ok, 4 * (k + 1))
                for g in range(NG):
                    if g:
                        e.wait_ge(xres, 4 * k + g)
                    for t in range(GT):
                        m = transpose(PS[:, 6, t * P:(t + 1) * P], acc[:, g, t * P:(t + 1) * P])
                    m.then_inc(wo_ok, 1)

            def front2():
                back(0)
                front(2)

            plan = [lambda: front(0), lambda: attention(0), lambda: front(1), experts0, front2,
                    lambda: attention(1), lambda: front(3), relative_attention, lambda: front(4), experts1]
            for k, run in enumerate(plan[:upto]):
                run()
                meet(e, "pe", k + 1)
            if upto > len(plan):
                back(1)

        @block.vector
        def _(e):
            start(e, "dve")
            own = Steps(e, own_dve)
            norms = [0]

            def layernorm(src, before, done):
                for t in range(GT):
                    own(e.bn_stats(st[:, t, :], src[:, t, :]))
                own.settle()
                for t in range(GT):
                    own(e.bn_aggr(mv[:, t, :], st[:, t, :]))
                own.settle()
                e.tensor_scalar(sd[:, 0, :], mv[:, :, 1], EPS, None, ALU.add).then_inc(var_ok, 1)
                norms[0] += 1
                e.wait_ge(sd_ok, norms[0])
                own(e.reciprocal(sd[:, 1, :], sd[:, 0, :]))
                e.wait_ge(xT_ok, before)
                own.settle()
                for t in range(GT):
                    ins = e.tensor_scalar(xn[:, t, :], src[:, t, :], mv[:, t, 0:1], sd[:, 1, t:t + 1],
                                          ALU.subtract, ALU.mult)
                    if done is not None and t == GT - 1:
                        ins.then_inc(done, 1)
                    else:
                        own(ins)

            def split(dst, src, res):
                own(e.tensor_copy(dst(0), src))
                own.settle()
                own(e.tensor_tensor(res[0], src, dst(0), ALU.subtract))
                own.settle()
                own(e.tensor_copy(dst(1), res[0]))
                own.settle()
                own(e.tensor_tensor(res[1], res[0], dst(1), ALU.subtract))
                own.settle()
                return e.tensor_copy(dst(2), res[1])

            def front(f):
                a = {1: 0, 3: 1, 4: 2}.get(f)
                a2 = {0: 0, 2: 1, 3: 2}.get(f)

                def heads_in(g):
                    if a is None or g >= NG:
                        return
                    half = g % 2
                    e.wait_ge(at_in[half], 16 * ([4, 4, 8][a] * (g // 2 + 1) + [0, 8, 16][a]))
                    own(e.reciprocal(atu[:, half, 1, :], atu[:, half, 1, :]))
                    own.settle()
                    e.tensor_tensor(atn[:, half, :], atu[:, half, 0, :], atu[:, half, 1, :], ALU.mult)\
                        .then_inc(atn_ok, 1)

                def rows_in(g):
                    u = 4 * f + g
                    xg = X[:, GT * g:GT * g + GT, :]
                    sg_ = SRC[:, GT * g:GT * g + GT, :]
                    if f == 0:
                        e.wait_ge(x_in[g], 16)
                    if a is not None:
                        e.wait_ge(wo_ok, 4 * [0, 2, 3][a] + g + 1)
                        y = PS[:, [4, 6][g % 2], :].rearrange("p (t d) -> p t d", t=GT)
                        own(e.tensor_tensor(xg, xg, y, ALU.add))
                        if a == 2:
                            own(e.tensor_tensor(sg_, sg_, y, ALU.add))
                        own.settle()
                        if a == 1:
                            own(e.tensor_tensor(xg, xg, rows[:, 1, :].unsqueeze(1).broadcast_to([P, GT, P]), ALU.add))
                            own.settle()
                    if f in (2, 3):
                        layernorm(xg, u, None)
                        own.settle()
                        own(e.tensor_copy(sg_, xn[:]))
                        own(e.tensor_tensor(xg, xg, xn[:], ALU.add))
                        own.settle()
                    layernorm(xg if f < 2 else sg_, u, xn_ok)

                def rows_out(g):
                    project(f, a2, g) if a2 is not None else route(f, g)

                heads_in(0)
                heads_in(1)
                rows_in(0)
                for g in range(NG):
                    if g + 1 < NG:
                        rows_in(g + 1)
                    heads_in(g + 2)
                    rows_out(g)

            def project(f, a2, g):
                b, half = g // 2, g % 2
                pr = 5 * g if f == 0 else 20 + 12 * (a2 - 1) + 3 * g
                tok = slice(half * GW, (half + 1) * GW)

                def values():
                    e.wait_ge(proj_ok, pr + (5 if f == 0 else 3))
                    for t in range(GT):
                        dst = Vt[:, H * b:H * b + H, half * GT + t, :]
                        src = PS[:, 5, t * P:(t + 1) * P].rearrange("p (h d) -> p h d", h=H)
                        if f == 2:
                            m = e.tensor_tensor(dst, src, rows[:, 0, :].rearrange("p (h d) -> p h d", h=H), ALU.add)
                        else:
                            m = e.tensor_copy(dst, src)
                        if t < GT - 1:
                            own(m)
                    m.then_inc(v_ok, 1)

                e.wait_ge(split_k, 4 * a2 + g)
                if f == 0:
                    e.wait_ge(rope_in, 16)
                    e.wait_ge(proj_ok, pr + 2)
                    own(e.tensor_tensor(rt[:, 0, :], bank(3), rope[:, 0, tok], ALU.mult))
                    own(e.tensor_tensor(rt[:, 1, :], bank(4), rope[:, 1, tok], ALU.mult))
                    own.settle()
                    e.tensor_tensor(qk[:, 1, :], rt[:, 0, :], rt[:, 1, :], ALU.add).then_inc(kin_ok, 1)
                    e.wait_ge(kin_ok, 4 * a2 + g + 1)
                    e.wait_ge(proj_ok, pr + 4)
                    own(e.tensor_tensor(rt[:, 0, :], bank(1), rope[:, 0, tok], ALU.mult))
                    own(e.tensor_tensor(rt[:, 1, :], bank(2), rope[:, 1, tok], ALU.mult))
                    own.settle()
                    own(e.tensor_tensor(qk[:, 0, :], rt[:, 0, :], rt[:, 1, :], ALU.add))
                else:
                    e.wait_ge(proj_ok, pr + 1)
                    if f == 2:
                        e.tensor_scalar(qk[:, 1, :], bank(3), cols[:, 3:4], None, ALU.add).then_inc(kin_ok, 1)
                        e.wait_ge(proj_ok, pr + 2)
                        own(e.tensor_scalar(qk[:, 0, :], bank(1), cols[:, 2:3], None, ALU.add))
                    else:
                        e.tensor_copy(qk[:, 1, :], bank(3)).then_inc(kin_ok, 1)
                        e.wait_ge(proj_ok, pr + 2)
                        own(e.tensor_scalar(qk[:, 0, :], bank(1), SCALE, None, ALU.mult))
                if g + 1 < NG:
                    values()
                own.settle()
                e.wait_ge(stk_out, 16 * (24 * a2 + 6 * g))
                split(lambda j: sp[:, 0, j, :], qk[:, 0, :], (rt[:, 0, :], rt[:, 1, :])).then_inc(split_q, 1)
                if g + 1 == NG:
                    values()
                e.wait_ge(split_q, 4 * a2 + g + 1)
                own.settle()
                if g + 1 == NG:
                    e.wait_ge(v_ok, 4 * (a2 + 1))

            def route(f, g):
                m = f == 4
                ne, top = (NE1, 4) if m else (NE0 - 1, 2)
                r = 4 * m + g
                e.wait_ge(lgt_ok, r + 1)
                ps = PS[:, [7, 2][g % 2], 0:GT * NE1].rearrange("p (t x) -> p t x", t=GT)[:, :, 0:ne]
                val = lg[:, :, 0:ne]

                def each(v, k=ne):
                    return v.unsqueeze(2).broadcast_to([P, GT, k])
                if not m:
                    own(e.tensor_tensor(lg2[:, :, 0:ne], ps, rows[:, 2, 0:ne].unsqueeze(1).broadcast_to([P, GT, ne]),
                                        ALU.add))
                    own.settle()
                    own(e.tensor_reduce(sm[:, 0, :], lg2[:, :, 0:ne], AX.X, ALU.max))
                    own.settle()
                    e.tensor_tensor(val, lg2[:, :, 0:ne], each(sm[:, 0, :]), ALU.subtract).then_inc(ex_in, 1)
                    e.wait_ge(ex_ok, r + 1)
                    own(e.tensor_reduce(sm[:, 0, :], val, AX.X, ALU.add))
                    own.settle()
                    own(e.reciprocal(sm[:, 1, :], sm[:, 0, :]))
                    own.settle()
                    own(e.tensor_tensor(val, val, each(sm[:, 1, :]), ALU.mult))
                    own.settle()
                else:
                    e.sem_inc(ex_in, 1)
                    e.wait_ge(ex_ok, r + 1)
                    own(e.tensor_scalar(val, val, 1.0, None, ALU.add))
                    own.settle()
                    own(e.reciprocal(val, val))
                    own.settle()
                own.settle()
                for t in range(GT):
                    own(e.max(m8[:, t, :], lg[:, t, 0:ne + 8]))
                own.settle()
                own(e.tensor_copy(rp[:, :, 0:top], m8[:, :, 0:top]))
                own.settle()
                for t in range(GT):
                    own(e.match_replace(lg2[:, t, 0:ne + 8], rp[:, t, :], lg[:, t, 0:ne + 8], 0.0))
                own.settle()
                g0 = gate[:, :, 0:ne] if m else gate[:, :, 1:ne + 1]
                own(e.tensor_tensor(g0, val, lg2[:, :, 0:ne], ALU.subtract))
                own.settle()
                if not m:
                    own(e.tensor_reduce(sm[:, 0, :], g0, AX.X, ALU.add))
                    own.settle()
                    own(e.reciprocal(sm[:, 1, :], sm[:, 0, :]))
                    own.settle()
                    own(e.tensor_tensor(g0, g0, each(sm[:, 1, :]), ALU.mult))
                    own.settle()
                split(lambda j: gsp[:, :, j, :], gate[:], (gres[:, 0], gres[:, 1])).then_inc(gsp_ok, 1)
                e.wait_ge(gtp_ok, r + 1)
                e.tensor_copy(GTs[0:ROWS, g * GW:(g + 1) * GW], bank(1, BF16)[0:ROWS, 0:GW]).then_inc(gt_ok, 1)
                e.wait_ge(gt_ok, r + 1)

            def attention(a):
                HB = NH * a
                e.memset(PS[:, 6, 0:256], 0.0).then_inc(o_zero, 1)
                if a == 0:
                    e.wait_ge(c_in, 16 * N_CONST)
                    e.sem_inc(max_done, 2)

                def row_max(n, s, qt):
                    e.wait_ge(s_done, 8 * (HB + n) + qt + 1)
                    e.tensor_reduce(M[:, s, qt:qt + 1], PS[:, 2 + 2 * (qt % 2):4 + 2 * (qt % 2), :]
                                    .rearrange("p a b -> p (a b)"), AX.X, ALU.max, negate=True).then_inc(max_done, 1)

                def max_copy(n, s):
                    e.wait_ge(mt_done, HB + n + 1)
                    e.tensor_copy(MT[:, s, :], bank(7, BF16)[0:PARTS * QT, 0:P]).then_inc(mt_copied, 1)

                for n in range(2):
                    for qt in range(QT):
                        row_max(n, n, qt)
                max_copy(0, 0)

                def position(i, s, last):
                    n = SLOTS * i + s
                    for qt in range(QT):
                        if qt == 4 and not (last and s == 3):
                            max_copy(n + 1, (s + 1) % SLOTS)
                        if not (last and s >= 2):
                            row_max(n + 2, (s + 2) % SLOTS, qt)
                with e.Fori(0, NH // SLOTS - 1) as i:
                    for s in range(SLOTS):
                        position(i, s, False)
                for s in range(SLOTS):
                    position(NH // SLOTS - 1, s, True)

            def relative_attention():
                def prep(n, s, p):
                    e.wait_ge(prep_ps, 4 * n + p + 1)
                    e.wait_ge(prep_add, 2 * n + p // 2)
                    e.tensor_tensor(tA[:, p % 2, :], bank(6), rel[:, p % 2, (p // 2) * GW:(p // 2 + 1) * GW],
                                    ALU.mult).then_inc(prep_mul, 1)

                def row_max(n, s, qt):
                    e.wait_ge(rs_done, 8 * n + qt + 1)
                    e.tensor_reduce(M[:, s, qt:qt + 1], PS[:, 2 * (qt % 2):2 * (qt % 2) + 2, :]
                                    .rearrange("p a b -> p (a b)"), AX.X, ALU.max, negate=True).then_inc(rmax, 1)

                def position(i, s, last):
                    n = 2 * i + s
                    end = last and s == 1
                    for qt in range(QT):
                        u = 8 * n + qt
                        if qt < 7:
                            row_max(n, s, qt + 1)
                        elif not end:
                            row_max(n + 1, 1 - s, 0)
                        e.wait_ge(rt_done, 1 + u + 1)
                        if qt % 4 == 0:
                            e.wait_ge(rpv, 1 + 2 * n + qt // 4)
                        e.tensor_copy(PT[:, qt // 4, 4:8, qt % 4, :], PS[:, 5, :].rearrange("p (k q) -> p k q", k=4))\
                            .then_inc(rev_d, 1)
                        if 2 <= qt < 6 and not end:
                            prep(n + 1, 1 - s, qt - 2)

                for p in range(4):
                    prep(0, 0, p)
                row_max(0, 0, 0)
                with e.Fori(0, NH // 2 - 1) as i:
                    for s in range(2):
                        position(i, s, False)
                for s in range(2):
                    position(NH // 2 - 1, s, True)

            def zero_acc():
                e.memset(acc[:, 0, :], 0.0).then_inc(acc_zero, 1)

            def experts0():
                zero_acc()
                with e.Fori(0, NE0 // 2) as i:
                    for s in range(2):
                        for tg in range(NG):
                            v = NG * (2 * i + s) + tg
                            e.wait_ge(b_ps, v + 1)
                            e.tensor_tensor(xw[:, tg % 2, :], XT[:, tg * GW:(tg + 1) * GW], bank(0), ALU.mult)\
                                .then_inc(xw_ok, 1)
                            for c, (lo, w) in enumerate(FCH):
                                e.wait_ge(u_ps, 3 * v + c + 1)
                                e.wait_ge(sg_ok, 1 + 3 * v + c + 1)
                                e.tensor_tensor(hh[0:w, tg % 2, c, :], PS[0:w, [3, 0, 2][c], :], sg[0:w, c, :],
                                                ALU.mult).then_inc(h_ok, 1)

            def experts1():
                V0 = NG * NE0
                e.memset(acc[:, 0, :], 0.0).then_inc(acc_zero, 1)
                with e.Fori(0, NE1 // 2) as i:
                    for s in range(2):
                        for tg in range(NG):
                            v = NG * (2 * i + s) + tg
                            e.wait_ge(sg_ok, 1 + 3 * V0 + v + 1)
                            e.tensor_tensor(hh[:, tg % 2, 0, :], bank(2 * (tg % 2)), sg[:, tg % 2, :], ALU.mult)\
                                .then_inc(h_ok, 1)

            def back(k):
                e.wait_ge(dn_ok, NG * (NE0 + k * NE1))
                for g in range(NG):
                    e.tensor_copy(acc[:, g, :], bank(4 + g)).then_inc(acc_ok, 1)
                for g in range(NG):
                    e.wait_ge(wo_ok, [4, 16][k] + g + 1)
                    xg = X[:, GT * g:GT * g + GT, :].rearrange("p t d -> p (t d)")
                    e.tensor_tensor(xg, xg, bank(6), ALU.add).then_inc(xres, 1)
                e.wait_ge(xres, [4, 8][k])

            def front2():
                back(0)
                front(2)

            def front3():
                w = PT[:, 0, 0:2, 0, :]
                res = [PT[:, 0, 2:4, 0, :], PT[:, 0, 4:6, 0, :]]

                def part(j):
                    return PT[:, 1, j, 0:2, :].rearrange("p a f -> p (a f)").bitcast(BF16)[:, 0:2 * P]\
                        .rearrange("p (a f) -> p a f", a=2)
                e.wait_ge(wp_in, 16)
                split(part, w, res).then_inc(wsplit, 1)
                e.wait_ge(table_in, 16)
                own(e.tensor_copy(Eh[:], PR[:, 3, :]))
                own.settle()
                e.tensor_tensor(El[:], PR[:, 3, :], Eh[:].bitcast(F32), ALU.subtract).then_inc(table_split, 1)
                front(3)

            plan = [lambda: front(0), lambda: attention(0), lambda: front(1), experts0, front2,
                    lambda: attention(1), front3, relative_attention, lambda: front(4), experts1]
            own(e.memset(lg[:], -1.0))
            own(e.memset(rp[:], -1.0))
            own(e.memset(gate[:], 0.0))
            own.settle()
            own(e.memset(gate[:, :, 0:1], 1.0))
            own.settle()
            for k, run in enumerate(plan[:upto]):
                run()
                meet(e, "dve", k + 1)
            if upto > len(plan):
                back(1)

        @block.scalar
        def _(e):
            start(e, "act")
            norms = [0]

            def front(f):
                def exp(g):
                    if f == 1:
                        e.wait_ge(ex_in, g + 1)
                        e.activation(lg[:, :, 0:NE0 - 1], lg[:, :, 0:NE0 - 1], ACT.Exp).then_inc(ex_ok, 1)
                    if f == 4:
                        e.wait_ge(ex_in, 4 + g + 1)
                        ps = PS[:, [7, 2][g % 2], 0:GT * NE1].rearrange("p (t x) -> p t x", t=GT)
                        e.activation(lg[:, :, 0:NE1], ps, ACT.Exp, scale=-1.0).then_inc(ex_ok, 1)

                for g in range(NG):
                    for k in range(2 if f in (2, 3) else 1):
                        norms[0] += 1
                        e.wait_ge(var_ok, norms[0])
                        e.activation(sd[:, 0, :], sd[:, 0, :], ACT.Sqrt).then_inc(sd_ok, 1)
                    e.wait_ge(xT_ok, 4 * f + g + 1)
                    if f >= 1:
                        e.wait_ge(xs_used, [0, 0, 4, 4, 4][f] + (g if f in (1, 4) else 0))
                    if f < 2:
                        e.activation(xTs[:], bank(0), ACT.Copy).then_inc(xs_ok, 1)
                    else:
                        c = {2: 0, 3: 4, 4: 6}[f]
                        e.activation(xTs[:], bank(0), ACT.Identity, scale=cols[:, c:c + 1],
                                     bias=cols[:, c + 1:c + 2]).then_inc(xs_ok, 1)
                    if g:
                        exp(g - 1)
                exp(NG - 1)

            def attention(a):
                HB = NH * a

                def evacuate(k, buf, before):
                    e.wait_ge(pv_done, 4 + 8 * (HB + k))
                    e.wait_ge(o_out[buf], 1 + before)
                    e.activation(Ob[:, buf, :], PS[:, 6, 0:256], ACT.Copy).then_inc(o_copied, 1)

                def position(i, s):
                    n = SLOTS * i + s
                    for x in range(16):
                        kt, qh = x // 2, x % 2
                        e.wait_ge(st_done, 1 + 16 * (HB + n) + x + 1)
                        if qh == 0:
                            e.wait_ge(pv_done, 8 * (HB + n) + kt + 1)
                        e.activation(PR[:, kt % 4, qh * GW:(qh + 1) * GW], bank(x % 2), ACT.Exp, scale=SCALE)\
                            .then_inc(exp_done, 1)
                        if x == 1:
                            evacuate(n, s % 2, 16 * ((17 - s % 2) * a + 2 * i + s // 2))

                e.wait_ge(c_in, 16 * N_CONST)
                e.wait_ge(o_zero, a + 1)
                with e.Fori(0, NH // SLOTS) as i:
                    for s in range(SLOTS):
                        position(i, s)
                evacuate(NH, 0, 16 * (17 * a + 16))

            def relative_attention():
                def exp(n, s, qt, k):
                    e.wait_ge(rmax, k + 1)
                    e.wait_ge(rt_done, 1 + k - 1) if not isinstance(k, int) or k >= 1 else None
                    e.activation(PR[:, qt % 2, :], PS[:, 2 * (qt % 2):2 * (qt % 2) + 2, :]
                                 .rearrange("p a b -> p (a b)"), ACT.Exp, bias=M[:, s, qt:qt + 1]).then_inc(rexp, 1)

                def position(i, s, last):
                    n = 2 * i + s
                    end = last and s == 1
                    for qt in range(QT):
                        u = 8 * n + qt
                        e.wait_ge(rt_done, 1 + u + 1)
                        if qt % 4 == 0:
                            e.wait_ge(rpv, 1 + 2 * n + qt // 4)
                        e.activation(PT[:, qt // 4, 0:4, qt % 4, :], PS[:, 4, :].rearrange("p (k q) -> p k q", k=4),
                                     ACT.Copy).then_inc(rev_a, 1)
                        if qt < 7:
                            exp(n, s, qt + 1, u + 1)
                        elif not end:
                            exp(n + 1, 1 - s, 0, u + 1)
                    e.wait_ge(rpv, 1 + 2 * n + 2)
                    e.wait_ge(o_out[s], 1 + 16 * ((17 - s) * 2 + i))
                    e.activation(Ob[:, s, :], PS[:, 7, 0:256], ACT.Copy).then_inc(ro_copied, 1)

                exp(0, 0, 0, 0)
                with e.Fori(0, NH // 2 - 1) as i:
                    for s in range(2):
                        position(i, s, False)
                for s in range(2):
                    position(NH // 2 - 1, s, True)

            def experts0():
                with e.Fori(0, NE0 // 2) as i:
                    for s in range(2):
                        for tg in range(NG):
                            v = NG * (2 * i + s) + tg
                            for c, (lo, w) in enumerate(FCH):
                                e.wait_ge(g_ps, 3 * v + c + 1)
                                e.wait_ge(h_ok, 1 + 3 * v)
                                e.activation(sg[0:w, c, :], PS[0:w, [1, 2, 1][c], :], ACT.Silu).then_inc(sg_ok, 1)

            def experts1():
                V0 = NG * NE0
                with e.Fori(0, NE1 // 2) as i:
                    for s in range(2):
                        for tg in range(NG):
                            v = NG * (2 * i + s) + tg
                            e.wait_ge(g_ps, 3 * V0 + v + 1)
                            e.activation(sg[:, tg % 2, :], bank(2 * (tg % 2) + 1), ACT.Relu).then_inc(sg_ok, 1)

            plan = [lambda: front(0), lambda: attention(0), lambda: front(1), experts0, lambda: front(2),
                    lambda: attention(1), lambda: front(3), relative_attention, lambda: front(4), experts1]
            for k, run in enumerate(plan[:upto]):
                run()
                meet(e, "act", k + 1)

        @block.gpsimd
        def _(e):
            own = Steps(e, own_pool)
            own(e.memset(zrow[:], 0.0))
            own(e.memset(nil[:], 0.0))
            own(e.memset(Va[:], 0.0))
            own(e.memset(Ws[:], 0.0))
            own.settle()
            own(e.memset(Ks[64:ROWS], 1.0))
            own(e.memset(Qs[64:ROWS], 0.0))
            own.settle()
            own(e.memset(Va[:, :, :, DH:DH + 1], 1.0))
            own.settle()
            def copy(dst, src):
                zeros = nil[:, 0:1]
                for _ in range(len(src.shape) - 2):
                    zeros = zeros.unsqueeze(1)
                return e.tensor_tensor(dst, src, zeros.broadcast_to(list(src.shape)), ALU.add)

            def front(f):
                for g in range(NG):
                    if f in (0, 2, 3):
                        a2 = {0: 0, 2: 1, 3: 2}[f]
                        e.wait_ge(kin_ok, 4 * a2 + g + 1)
                        e.wait_ge(stk_out, 16 * (24 * a2 + 6 * g))
                        kk = qk[:, 1, :]
                        own(copy(sp[:, 1, 0, :], kk))
                        own.settle()
                        own(e.tensor_tensor(kk, kk, sp[:, 1, 0, :], ALU.subtract))
                        own.settle()
                        own(copy(sp[:, 1, 1, :], kk))
                        own.settle()
                        own(e.tensor_tensor(kk, kk, sp[:, 1, 1, :], ALU.subtract))
                        own.settle()
                        copy(sp[:, 1, 2, :], kk).then_inc(split_k, 1)
                    else:
                        e.wait_ge(xs_ok, 4 * f + g + 1)
                        copy(XT[:, g * GW:(g + 1) * GW], xTs[:]).then_inc(xs_used, 1)
                if f in (1, 4):
                    e.wait_ge(xs_used, [4, 8][f == 4])

            def value_slot(n, s, ready):
                copy(Va[:, s, :, 0:DH], Vt[:, bass.ds(n, 1), :, :].rearrange("p n k d -> p (n k) d"))\
                    .then_inc(ready, 1)

            def attention(a):
                HB = NH * a

                def split_max(n, s):
                    e.wait_ge(max_done, 2 + 8 * (HB + n + 1))
                    own(copy(Ms[:, s, 0, :], M[:, s, :]))
                    own.settle()
                    own(e.tensor_tensor(Mr[:, 0, :], M[:, s, :], Ms[:, s, 0, :], ALU.subtract))
                    own.settle()
                    own(copy(Ms[:, s, 1, :], Mr[:, 0, :]))
                    own.settle()
                    own(e.tensor_tensor(Mr[:, 1, :], Mr[:, 0, :], Ms[:, s, 1, :], ALU.subtract))
                    own.settle()
                    copy(Ms[:, s, 2, :], Mr[:, 1, :]).then_inc(m_split, 1)
                    e.wait_ge(m_split, HB + n + 1)

                e.wait_ge(v_ok, 4 * a + 4)
                if a == 0:
                    e.wait_ge(c_in, 16 * N_CONST)
                    own(e.tensor_copy(identb[:], ident[:]))
                    own.settle()
                for n in range(2):
                    value_slot(n, n, v_ready)
                    split_max(n, n)
                with own.loop(NH // SLOTS - 1, 4 * SLOTS) as i:
                    for s in range(SLOTS):
                        split_max(SLOTS * i + s + 2, (s + 2) % SLOTS)
                        value_slot(SLOTS * i + s + 2, (s + 2) % SLOTS, v_ready)
                for s in range(2):
                    n = NH - SLOTS + s + 2
                    split_max(n, n % SLOTS)
                    value_slot(n, n % SLOTS, v_ready)
                if a == 0:
                    own(e.tensor_copy(sel[0:ROWS], sel0[:].unsqueeze(2).broadcast_to([ROWS, NE1, P])))
                    own.settle()

            def relative_attention():
                def add(n, s, h):
                    e.wait_ge(prep_mul, 4 * n + 2 * h + 2)
                    half = slice(h * GW, (h + 1) * GW)
                    e.tensor_tensor(At[:, h, :], tA[:, 0, :], tA[:, 1, :], ALU.add).then_inc(prep_add, 1)
                    e.wait_ge(prep_add, 2 * n + h + 1)
                    own(copy(Ah[:, s, half], At[:, h, :]))
                    own.settle()
                    e.tensor_tensor(Al[:, s, half], At[:, h, :], Ah[:, s, half].bitcast(F32), ALU.subtract)\
                        .then_inc(prep_split, 1)

                e.wait_ge(v_ok, 12)
                for n in range(2):
                    value_slot(n, n, rv_ready)
                for h in range(2):
                    add(0, 0, h)
                with own.loop(NH // 2 - 1, 4) as i:
                    for s in range(2):
                        n = 2 * i + s
                        for h in range(2):
                            add(n + 1, 1 - s, h)
                        e.wait_ge(rpv, 1 + 2 * n + 2)
                        value_slot(n + 2, s, rv_ready)
                for h in range(2):
                    add(NH - 1, 1, h)

            plan = [lambda: front(0), lambda: attention(0), lambda: front(1), lambda: None, lambda: front(2),
                    lambda: attention(1), lambda: front(3), relative_attention, lambda: front(4), lambda: None]
            for k, run in enumerate(plan[:upto]):
                run()
                meet(e, "pool", k + 1)


SHAPES = {
    "x": ([TT * P, P], F32), "ident": ([P, P], F32), "w_qkv": ([P, 3, 5 * P], F32),
    "rope": ([P, 2, L], F32), "w_out": ([P, 3, P], F32), "cols": ([P, 8], F32), "rows": ([P, 3, P], F32),
    "rel": ([P, 3, L], F32), "w_rt0": ([P, 8], F32), "w_rt1": ([P, NE1], F32), "sel0": ([ROWS, NE1], F32),
    "wpT": ([P, 2 * P], F32),
    "gu": ([NE0, P, 2, FI], F32), "dn": ([NE0, P, 3, P], F32), "kv": ([NE1, P, 2, P], F32),
}


def layout(i):
    i = {k: np.asarray(v) for k, v in i.items()}
    half = DH // 2
    swap = np.arange(P).reshape(H, 2, half)[:, ::-1].reshape(-1)
    w0 = i["L0_attn_Wqkv"]
    q0, k0, v0 = w0[:, 0:P], w0[:, P:2 * P], w0[:, 2 * P:3 * P]
    w1 = i["L1_attn_W_qkv"].T
    q1, k1, v1 = w1[:, 0:P], w1[:, P:2 * P], w1[:, 2 * P:3 * P]
    q2, k2, v2 = i["L1_ffn_wq"], i["L1_ffn_wk"], i["L1_ffn_wv"]
    w_qkv = np.stack([np.concatenate([q0, q0[:, swap], k0, k0[:, swap], v0], 1),
                      np.concatenate([q1, q1, k1, k1, v1], 1),
                      np.concatenate([q2, q2, k2, k2, v2], 1)], 1)
    w_out = np.stack([i["L0_attn_Wo"], i["L1_attn_W_out"].T, i["L1_ffn_wo"]], 1)
    b1 = i["L1_attn_b_qkv"]
    cols = np.stack([i["L1_attn_ln_gamma"], i["L1_attn_ln_beta"], b1[0:P], b1[P:2 * P],
                     i["L1_ffn_ln1_g"], i["L1_ffn_ln1_b"], i["L1_ffn_ln2_g"], i["L1_ffn_ln2_b"]], 1)
    rb = np.zeros(P, np.float32)
    rb[0:NE0 - 1] = i["L0_ffn_rb"]
    rows = np.broadcast_to(np.stack([b1[2 * P:3 * P], i["L1_attn_b_out"], rb])[None], (P, 3, P))
    w_rt0 = np.zeros((P, 8), np.float32)
    w_rt0[:, 0:NE0 - 1] = i["L0_ffn_wr"].T
    gate = np.concatenate([i["L0_ffn_sg"][None], i["L0_ffn_rg"]])
    up = np.concatenate([i["L0_ffn_su"][None], i["L0_ffn_ru"]])
    down = np.concatenate([i["L0_ffn_sd"][None], i["L0_ffn_rd"]])
    gu = np.stack([gate.transpose(0, 2, 1), up.transpose(0, 2, 1)], 2)
    dn = np.zeros((NE0, P, 3, P), np.float32)
    for c, (lo, w) in enumerate(FCH):
        dn[:, 0:w, c, :] = down[:, :, lo:lo + w].transpose(0, 2, 1)
    kv = np.stack([i["L1_ffn_keys"], i["L1_ffn_values"]], 2)
    wpT = i["L1_ffn_wp"].T
    swapped = np.concatenate([np.arange(P // 2, P), np.arange(P // 2)])
    rope, rel = tables()
    return {
        "x": i["L0_attn_x"].reshape(TT * P, P), "ident": np.eye(P, dtype=np.float32),
        "w_qkv": w_qkv, "rope": rope, "w_out": w_out, "cols": cols, "rows": rows, "rel": rel, "w_rt0": w_rt0,
        "w_rt1": i["L1_ffn_sel_w"], "sel0": np.tile(np.eye(NE1, dtype=np.float32), (PARTS, 1)),
        "wpT": np.concatenate([wpT, wpT[:, swapped]], 1),
        "gu": gu, "dn": dn, "kv": kv,
    }


def kernel(**inputs):
    import concourse.bacc as bacc
    from concourse.bass_utils import run_bass_kernel_spmd

    arrays = {f"in_{k}": np.ascontiguousarray(v) for k, v in layout(inputs).items()}
    nc = bacc.Bacc("TRN2", target_bir_lowering=False, num_devices=1)
    A = {}
    for name, (shape, dt) in SHAPES.items():
        assert list(arrays[f"in_{name}"].shape) == shape, (name, arrays[f"in_{name}"].shape)
        A[name] = nc.dram_tensor(f"in_{name}", shape, dt, kind="ExternalInput").ap()
    out = nc.dram_tensor("out", [TT * P, P], F32, kind="ExternalOutput").ap()
    two_layers(nc, A, out)
    r = run_bass_kernel_spmd(nc, [arrays], core_ids=[0])
    return np.asarray(r.results[0]["out"]).reshape(NB, L, P)
```

```python
from contextlib import ExitStack, contextmanager

import numpy as np

import concourse.bass as bass
from concourse import mybir
from concourse.alu_op_type import AluOpType as ALU

F32 = mybir.dt.float32
F32R = mybir.dt.float32r
BF16 = mybir.dt.bfloat16
ACT = mybir.ActivationFunctionType
AX = mybir.AxisListType

P = 128
NB, L = 2, 1024
H, DH = 16, 8
NH = NB * H
TT = NB * L // P
GT, GW = 4, 512
NG = TT // GT
QT = L // P
EPS = 1e-5
SCALE = DH ** -0.5
PARTS = 3
STACK = PARTS * PARTS * DH
ROWS = 96
VC = 32
NE0, FI = 8, 352
FCH = [(0, 128), (128, 128), (256, 96)]
NE1 = 32
SLOTS = 4


def tables():
    t = np.arange(L, dtype=np.float32)
    inv = (1.0 / 10000.0 ** (np.arange(0, DH, 2, dtype=np.float32) / DH)).astype(np.float32)
    ang = (t[:, None] * inv[None, :]).astype(np.float32)
    ang = np.tile(np.concatenate([ang, ang], 1), (1, H)).T.astype(np.float64)
    sign = np.where(np.arange(P) % DH < DH // 2, -1.0, 1.0)[:, None]
    rope = np.stack([np.cos(ang), np.sin(ang) * sign], 1).astype(np.float32)
    finv = (1.0 / 10000.0 ** (np.arange(0, P, 2, dtype=np.float32) / P)).astype(np.float32)
    fang = finv.astype(np.float64)[:, None] * t.astype(np.float64)[None, :]
    s, c = np.sin(fang), np.cos(fang)
    rel = np.stack([np.concatenate([s, c]), np.concatenate([c, c]), np.concatenate([s, -s])], 1)
    return rope, rel.astype(np.float32)


class Steps:

    def __init__(self, eng, sem):
        self.eng, self.sem, self.base, self.k, self.i, self.per = eng, sem, 0, 0, None, 0

    def now(self):
        return self.base + self.k if self.i is None else self.base + self.i * self.per + self.k

    def __call__(self, ins):
        ins.then_inc(self.sem, 1)
        self.k += 1

    def settle(self):
        self.eng.wait_ge(self.sem, self.now())

    @contextmanager
    def loop(self, trips, per):
        self.base, self.k, self.per = self.base + self.k, 0, per
        with self.eng.Fori(0, trips) as i:
            self.i = i
            yield i
        assert self.k == per, (self.k, per)
        self.base, self.k, self.i = self.base + trips * per, 0, None


def two_layers(nc, A, out):
    with ExitStack() as ctx:
        def sb(name, shape, dt=F32):
            return ctx.enter_context(nc.sbuf_tensor(name, shape, dt))

        def two(name, shape):
            with nc.sbuf_tensor(name + "_r", shape, F32R) as rounded:
                pass
            return sb(name, shape), rounded

        def sem(name):
            return ctx.enter_context(nc.semaphore(name))

        PS = ctx.enter_context(nc.psum_tensor("PS", [P, 8, GW], F32))

        def bank(b, dt=F32):
            return PS[:, b, :] if dt == F32 else PS[:, b, :].bitcast(dt)

        q_stack = nc.dram_tensor("q_stack", [9, NB * P, L], BF16)
        k_stack = nc.dram_tensor("k_stack", [9, NB * P, L], BF16)
        w_stack = nc.dram_tensor("w_stack", [9, NB * P, 2 * P], BF16)
        o_dram = nc.dram_tensor("o_dram", [NH + 1, 4, 32, 256], F32)
        r_dram = nc.dram_tensor("r_dram", [NB, H, 4, 256], F32)

        X = sb("X", [P, TT, P])
        SRC = sb("SRC", [P, TT, P])
        XT = sb("XT", [P, TT * P])
        ident = sb("ident", [P, P])
        identb = sb("identb", [P, P], BF16)
        w_qkv = sb("w_qkv", [P, 3, 5 * P])
        w_out = sb("w_out", [P, 3, P])
        rope, rope_r = two("rope", [P, 2, L])
        rel = sb("rel", [P, 2, L])
        cols = sb("cols", [P, 8])
        rows = sb("rows", [P, 3, P])
        w_rt0 = sb("w_rt0", [P, 8])
        w_rt1 = sb("w_rt1", [P, NE1])
        Qs = sb("Qs", [P, SLOTS, L], BF16)
        Ks = sb("Ks", [P, SLOTS, L], BF16)
        zrow = sb("zrow", [PARTS, L], BF16)
        Vt, Vt_r = two("Vt", [P, NH, QT, DH])
        Va = sb("Va", [P, SLOTS, QT, VC])
        M = sb("M", [P, SLOTS, QT])
        Mr = sb("Mr", [P, 2, QT])
        Ms = sb("Ms", [P, SLOTS, PARTS, QT], BF16)
        MT = sb("MT", [PARTS * QT, SLOTS, P], BF16)
        PR, PR_r = two("PR", [P, 4, L])
        Ob = sb("Ob", [P, 2, 256])
        Ws = sb("Ws", [P, 2, 2 * P], BF16)
        Ah = sb("Ah", [P, 2, L], F32R)
        Al = sb("Al", [P, 2, L], F32R)
        Eh = sb("Eh", [P, L], F32R)
        El = sb("El", [P, L], F32R)
        BIG, BIG_r = two("BIG", [P, 2 * QT * 4 * P])
        PQ = BIG[:].rearrange("p (k q) -> p k q", k=QT)
        PT = BIG[:].rearrange("p (a k g q) -> p a k g q", a=2, k=QT, g=4)
        st = sb("st", [P, GT, 6])
        mv = sb("mv", [P, GT, 2])
        sd = sb("sd", [P, 2, GT])
        xn = sb("xn", [P, GT, P])
        xTs = sb("xTs", [P, GW])
        qk = sb("qk", [P, 2, GW])
        rt = sb("rt", [P, 2, GW])
        At, tA = qk, rt
        kin = [qk[:, 1, :], PR[:, 2, 0:GW]]
        sp = sb("sp", [P, 2, PARTS, GW], BF16)
        rs = sb("rs", [P, NB, P])
        atu = rope[:].rearrange("p a (b t) -> p a b t", b=2)
        atn = sb("atn", [P, 2, GW])
        lg, lg2 = (BIG[:, k * 1024:k * 1024 + TT * (NE1 + 8)].rearrange("p (t x) -> p t x", t=TT) for k in range(2))
        gate = BIG[:, 2048:2048 + TT * NE1].rearrange("p (t x) -> p t x", t=TT)
        gres = BIG[:, 3072:3072 + 2 * TT * NE1].rearrange("p (a t x) -> p a t x", a=2, t=TT)
        m8 = sb("m8", [P, TT, 8])
        rp = sb("rp", [P, TT, 8])
        sm = sb("sm", [P, 2, TT])
        nil = sb("nil", [P, 1])
        gsp = sb("gsp", [P, TT, PARTS, NE1], BF16)
        GTs = sb("GTs", [P, TT * P], BF16)
        sel0 = sb("sel0", [ROWS, NE1])
        sel = sb("sel", [P, NE1, P], BF16)
        wg = sb("wg", [P, 2, 2, FI])
        wd = sb("wd", [P, 2, 3, P])
        h0 = BIG[:, 0:3 * GW].rearrange("p (c t) -> p c t", c=3)
        h0p = BIG_r[:, 3 * GW:15 * GW].rearrange("p (r a c t) -> p r a c t", r=2, a=2, c=3)
        sg = SRC[:].rearrange("p t d -> p (t d)")[:, 0:3 * GW].rearrange("p (c t) -> p c t", c=3)
        xw = rt
        xwp = [t[:].rearrange("p (a t) -> p a t", a=2) for t in (Eh, El)]
        wgp = [t.rearrange("p (r k f) -> p r k f", r=2, k=2) for t in (
            PR_r[:, 2:4, :].rearrange("p a t -> p (a t)")[:, 0:4 * FI],
            Vt_r[:].rearrange("p n k d -> p (n k d)")[:, 0:4 * FI])]
        wdp = rope_r[:].rearrange("p a t -> p (a t)")[:, 0:12 * P]\
            .rearrange("p (a r c f) -> p a r c f", a=2, r=2, c=3)
        we = wg[:, :, :, 0:P]
        XTh, XTl = (t[:].rearrange("p a t -> p (a t)") for t in (Ah, Al))
        wsp = PR_r[:, 2:4, :].rearrange("p a (s k r f) -> p (a s) k r f", s=2, k=2, r=2)
        hf, hhi, hlo = (t[:, 4 * k * GW:4 * (k + 1) * GW].rearrange("p (a t) -> p a t", a=4)
                        for k, t in enumerate((BIG, BIG_r, BIG_r)))
        sg1 = BIG[:, 12 * GW:14 * GW].rearrange("p (a t) -> p a t", a=2)
        acc = PR[:].rearrange("p a (b t) -> p (a b) t", b=2)[:, 0:NG, :]

        x_in = [sem(f"x_in{g}") for g in range(NG)]
        w_in, rope_in, c_in = map(sem, "w_in rope_in c_in".split())
        stage = {e: sem(f"stage_{e}") for e in ("sp", "act", "pool", "pe", "dve")}
        own_dve, own_pool, own_act = sem("own_dve"), sem("own_pool"), sem("own_act")
        rs_in, rs_ok, rs_out, src_ok, xadd_ok = map(sem, "rs_in rs_ok rs_out src_ok xadd_ok".split())
        at_in = [sem(f"at_in{s}") for s in range(2)]
        atn_ok, wo_ok, var_ok, sd_ok, xn_ok, xT_ok, xs_ok, xs_used = map(
            sem, "atn_ok wo_ok var_ok sd_ok xn_ok xT_ok xs_ok xs_used".split())
        proj_ok, split_k, stq_out, stk_out, v_ok, xres = map(
            sem, "proj_ok split_k stq_out stk_out v_ok xres".split())
        qin_ok = sem("qin_ok")
        kin_ok, split_q, lgt_ok, ex_in, ex_ok, gsp_ok, gtp_ok, gt_ok = map(
            sem, "kin_ok split_q lgt_ok ex_in ex_ok gsp_ok gtp_ok gt_ok".split())
        w_out_ok = sem("w_out_ok")
        wp_in, table_in, table_split, wsplit = map(sem, "wp_in table_in table_split wsplit".split())
        qk_in = [sem(f"qk_in{s}") for s in range(SLOTS)]
        m_in = [sem(f"m_in{s}") for s in range(SLOTS)]
        o_out = [sem(f"o_out{s}") for s in range(2)]
        v_ready, s_done, max_done, m_split, mt_done, mt_copied = map(
            sem, "v_ready s_done max_done m_split mt_done mt_copied".split())
        st_done, exp_done, pv_done, o_copied, o_zero = map(
            sem, "st_done exp_done pv_done o_copied o_zero".split())
        ws_in = [sem(f"ws_in{s}") for s in range(2)]
        prep_ps, prep_mul, prep_add, prep_split = map(sem, "prep_ps prep_mul prep_add prep_split".split())
        rs_done, rmax, rexp, rt_done, rev_a, rev_d, rpv = map(
            sem, "rs_done rmax rexp rt_done rev_a rev_d rpv".split())
        ro_copied = sem("ro_copied")
        rv_ready = sem("rv_ready")
        ew_in = [sem(f"ew_in{s}") for s in range(2)]
        acc_zero = sem("acc_zero")
        b_ps, g_ps, u_ps, xw_ok, sg_ok, h_ok, dn_ok, acc_ok = map(
            sem, "b_ps g_ps u_ps xw_ok sg_ok h_ok dn_ok acc_ok".split())
        w0_ok, xhi_ok, xlo_ok, hi_ok, lo_ok = map(sem, "w0_ok xhi_ok xlo_ok hi_ok lo_ok".split())
        key_ps, relu_ok, hf_ok, hhi_ok, hlo_ok, wsp_ok, val_ok = map(
            sem, "key_ps relu_ok hf_ok hhi_ok hlo_ok wsp_ok val_ok".split())
        y_out = sem("y_out")

        block = ctx.enter_context(nc.Block())

        N_CONST = 8

        def meet(eng, me, k):
            if k not in MEETINGS:
                return
            k = MEETINGS.index(k) + 1
            eng.sem_inc(stage[me], 1)
            for other in stage:
                if other != me:
                    eng.wait_ge(stage[other], k)

        LATE = 3
        BACK = [2, 4, 6, 7]
        MEETINGS = [3, 4, 9, 10]

        STARTS = {"sp": o_out, "pe": [st_done, rt_done, rpv], "act": [rev_a, ro_copied], "dve": [rev_d]}

        def start(eng, me):
            for signal in STARTS[me]:
                eng.sem_inc(signal, 1)

        def count(n):
            return max(n, 0) if isinstance(n, int) else n

        @block.sync
        def _(e):
            start(e, "sp")
            x_t = A["x"].rearrange("(t p) d -> p t d", p=P)
            for g in range(NG):
                e.dma_start(X[:, GT * g:GT * g + GT, :], x_t[:, GT * g:GT * g + GT, :]).then_inc(x_in[g], 16)
                if g == 0:
                    e.dma_start(ident[:], A["ident"]).then_inc(w_in, 16)
                    e.dma_start(w_qkv[:, 0, :], A["w_qkv"][:, 0, :]).then_inc(w_in, 16)
            e.dma_start(rope[:], A["rope"]).then_inc(rope_in, 16)
            loads = [(w_qkv[:, 1:3, :], A["w_qkv"][:, 1:3, :]), (w_out[:], A["w_out"]), (cols[:], A["cols"]),
                     (rows[:], A["rows"]), (rel[:], A["rel"][:, 1:3, :]), (w_rt0[:], A["w_rt0"]), (w_rt1[:], A["w_rt1"]),
                     (sel0[:], A["sel0"])]
            for dst, src in loads:
                e.dma_start(dst, src).then_inc(c_in, 16)
            assert len(loads) == N_CONST

            def q_out(a, g):
                b, half = g // 2, g % 2
                e.wait_ge(split_q, 4 * a + g + 1)
                d = q_stack[:, b * P:(b + 1) * P, half * GW:(half + 1) * GW]
                for i in range(PARTS):
                    e.dma_start(d[PARTS * i:PARTS * i + PARTS].rearrange("j p t -> p j t"),
                                sp[:, 0, i, :].unsqueeze(1).broadcast_to([P, PARTS, GW])).then_inc(stq_out, 16)

            def k_out(a, g):
                b, half = g // 2, g % 2
                e.wait_ge(split_k, 4 * a + g + 1)
                d = k_stack[:, b * P:(b + 1) * P, half * GW:(half + 1) * GW].rearrange("(i j) p t -> j p i t", j=PARTS)
                for j in range(PARTS):
                    e.dma_start(d[j], sp[:, 1, j, :].unsqueeze(1).broadcast_to([P, PARTS, GW])).then_inc(stk_out, 16)

            def sums_in(k, b):
                e.dma_start(rs[:, b, :], o_dram[1 + H * b:1 + H * b + H, :, DH, :]
                            .rearrange("h g (a q) -> (h g) a q", a=2)).then_inc(rs_in, 16)

            def sums_out(k, b):
                e.wait_ge(rs_ok, NB * k + b + 1)
                e.dma_start(r_dram[b].rearrange("h g (a q) -> (h g) a q", a=2), rs[:, b, :]).then_inc(rs_out, 16)
                e.wait_ge(rs_out, 16 * (NB * k + b + 1))

            def attention_in(k, b, half):
                u = 4 * k + 2 * b + half
                e.wait_ge(atn_ok, max(0, u - 1))
                heads = o_dram[1 + H * b:1 + H * b + H]
                for n in range(2):
                    g, q = 2 * half + n, slice(n * 256, (n + 1) * 256)
                    e.dma_start(atu[:, half, 0, q], heads[:, g, 0:DH, :]).then_inc(at_in[half], 16)
                    e.dma_start(atu[:, half, 1, q], r_dram[b, :, g, :].unsqueeze(1).broadcast_to([H, DH, 256]))\
                        .then_inc(at_in[half], 16)

            def load_qk(a, n, s):
                e.dma_start(Qs[0:STACK, s, :], q_stack[:, bass.ts(n, DH), :]).then_inc(qk_in[s], 16)
                e.dma_start(Qs[STACK:STACK + PARTS, s, :], zrow[:, :]).then_inc(qk_in[s], 16)
                e.dma_start(Ks[0:STACK, s, :], k_stack[:, bass.ts(n, DH), :]).then_inc(qk_in[s], 16)

            def load_rel(n, s):
                load_qk(2, n, s)
                e.dma_start(Ws[0:STACK, s, :], w_stack[:, bass.ts(n, DH), :]).then_inc(ws_in[s], 16)

            def attention(a):
                def max_rows(n, s):
                    e.wait_ge(mt_copied, NH * a + n + 1)
                    e.dma_start(Qs[STACK:STACK + PARTS, s, :], MT[:, s, :]).then_inc(m_in[s], 16)

                def position(i, s, last):
                    n = SLOTS * i + s
                    if not (last and s >= 1):
                        e.wait_ge(st_done, 1 + 16 * (NH * a + n))
                        load_qk(a, n + 3, (s + 3) % SLOTS)
                    e.wait_ge(o_copied, (NH + 1) * a + n + 1)
                    e.dma_start(o_dram[bass.ds(n, 1)].rearrange("n g c q -> (n g c) q"), Ob[:, s % 2, :])\
                        .then_inc(o_out[s % 2], 16)
                    if not (last and s == 3):
                        max_rows(n + 1, (s + 1) % SLOTS)

                max_rows(0, 0)
                with e.Fori(0, NH // SLOTS - 1) as i:
                    for s in range(SLOTS):
                        position(i, s, False)
                e.wait_ge(o_out[0], 1 + 16 * (17 * a + NH // 2 - 2))
                e.wait_ge(o_out[1], 1 + 16 * (16 * a + NH // 2 - 2))
                sums_in(a, 0)
                for s in range(SLOTS - 1):
                    position(NH // SLOTS - 1, s, True)
                sums_out(a, 0)
                for half in range(2):
                    attention_in(a, 0, half)
                position(NH // SLOTS - 1, SLOTS - 1, True)
                e.wait_ge(o_copied, (NH + 1) * (a + 1))
                e.dma_start(o_dram[NH:NH + 1].rearrange("n g c q -> (n g c) q"), Ob[:, 0, :]).then_inc(o_out[0], 16)
                e.wait_ge(o_out[0], 1 + 16 * 17 * (a + 1))
                e.wait_ge(o_out[1], 1 + 16 * 16 * (a + 1))

            def relative_attention():
                def position(i, s, last):
                    n = 2 * i + s
                    e.wait_ge(ro_copied, 1 + n + 1)
                    e.dma_start(o_dram[bass.ds(n + 1, 1)].rearrange("n g c q -> (n g c) q"), Ob[:, s, :])\
                        .then_inc(o_out[s], 16)
                    if not last:
                        load_rel(n + 2, s)

                with e.Fori(0, NH // 2 - 1) as i:
                    for s in range(2):
                        position(i, s, False)
                e.wait_ge(o_out[0], 1 + 16 * (17 * 2 + NH // 2 - 1))
                e.wait_ge(o_out[1], 1 + 16 * (16 * 2 + NH // 2 - 1))
                sums_in(2, 0)
                position(NH // 2 - 1, 0, True)
                sums_out(2, 0)
                for half in range(2):
                    attention_in(2, 0, half)
                position(NH // 2 - 1, 1, True)
                e.wait_ge(o_out[0], 1 + 16 * (17 * 2 + NH // 2))
                e.wait_ge(o_out[1], 1 + 16 * (16 * 2 + NH // 2))

            def load_expert(k, x, s):
                if k == 0:
                    e.dma_start(wg[:, s, :, :], A["gu"][bass.ds(x, 1)].rearrange("x p a f -> (x p) a f"))\
                        .then_inc(ew_in[s], 16)
                    e.dma_start(wd[:, s, :, :], A["dn"][bass.ds(x, 1)].rearrange("x p c f -> (x p) c f"))\
                        .then_inc(ew_in[s], 16)
                else:
                    e.dma_start(we[:, s, :, :], A["kv"][bass.ds(x, 1)].rearrange("x p a f -> (x p) a f"))\
                        .then_inc(ew_in[s], 16)

            def experts(k):
                with e.Fori(0, [NE0, NE1][k] // 2 - 1) as i:
                    for s in range(2):
                        e.wait_ge([w0_ok, wsp_ok][k], 2 * i + s + 1)
                        load_expert(k, 2 * i + s + 2, s)

            QKV = [0, 2, 3]

            def front(f):
                k = {1: 0, 3: 1, 4: 2}.get(f)
                if k is not None:
                    sums_in(k, 1)
                if f == 3:
                    e.dma_start(PR[:, 3, :], A["rel"][:, 0, :]).then_inc(table_in, 16)
                    e.wait_ge(wsplit, 1)
                    for b in range(NB):
                        d = w_stack[:, b * P:(b + 1) * P, :].rearrange("(i j) p t -> j p i t", j=PARTS)
                        for j in range(PARTS):
                            src = PT[:, 1, j, 0:2, :].rearrange("p a f -> p (a f)").bitcast(BF16)[:, 0:2 * P]
                            e.dma_start(d[j], src.unsqueeze(1).broadcast_to([P, PARTS, 2 * P])).then_inc(w_out_ok, 16)
                if f in (1, 4):
                    for s in range(2):
                        load_expert(f // 4, s, s)
                if k is not None:
                    sums_out(k, 1)
                for g in range(NG):
                    if k is not None and g < 2:
                        attention_in(k, 1, g)
                    if f not in QKV:
                        continue
                    a = QKV.index(f)
                    q_out(a, g)
                    if f == 3:
                        k_out(a, g)
                    if g == 2:
                        e.wait_ge(stq_out, 16 * 3 * (4 * a + 2))
                        e.wait_ge(stk_out, 16 * 3 * (4 * a + 2))
                        if f < 3:
                            for n in range(3):
                                load_qk(a, n, n)
                        else:
                            e.wait_ge(w_out_ok, 16 * 6)
                            load_rel(0, 0)
                            load_rel(1, 1)
                    if f < 3:
                        k_out(a, g)
                if f in QKV:
                    e.wait_ge(stq_out, 16 * 12 * (QKV.index(f) + 1))
                    e.wait_ge(stk_out, 16 * 12 * (QKV.index(f) + 1))

            def attention1():
                e.dma_start(PT[:, 0, 0:2, 0, :], A["wpT"].rearrange("p (a f) -> p a f", a=2)).then_inc(wp_in, 16)
                attention(1)

            plan = [lambda: front(0), lambda: attention(0), lambda: front(1), lambda: experts(0), lambda: front(2),
                    attention1, lambda: front(3), relative_attention, lambda: front(4), lambda: experts(1)]
            for k, run in enumerate(plan):
                run()
                meet(e, "sp", k + 1)
            o_t = out.rearrange("(t p) d -> p t d", p=P)
            for g in range(NG):
                e.wait_ge(xres, 4 + g + 1)
                e.dma_start(o_t[:, GT * g:GT * g + GT, :], X[:, GT * g:GT * g + GT, :]).then_inc(y_out, 16)
            e.wait_ge(y_out, 16 * NG)

        @block.tensor
        def _(e):
            start(e, "pe")
            e.wait_ge(w_in, 16 * 2)

            def products_read(n):
                e.wait_ge(qin_ok, n)
                e.wait_ge(kin_ok, n)
                e.wait_ge(v_ok, n)

            def transpose(dst, src):
                return e.transpose(dst, src, ident[:])

            def front(f):
                a = {1: 0, 3: 1, 4: 2}.get(f)
                a2 = {0: 0, 2: 1, 3: 2}.get(f)

                def gates(g):
                    for t in range(GT):
                        m = e.transpose(bank(g, BF16)[0:ROWS, t * P:(t + 1) * P],
                                        gsp[:, GT * g + t, :, :].rearrange("p a x -> p (a x)"), identb[:])
                    m.then_inc(gtp_ok, 1)

                def project_out(g):
                    if a is None or g >= NG:
                        return
                    e.wait_ge(atn_ok, 4 * a + g + 1)
                    if g == 1:
                        e.wait_ge(o_copied if a < 2 else ro_copied, (NH + 1) * (a + 1) if a < 2 else 1 + NH)
                    for t in range(GT):
                        m = e.matmul(PS[:, [4, 6][g % 2], t * P:(t + 1) * P], atn[:, g % 2, t * P:(t + 1) * P],
                                     w_out[:, a, :], start=True, stop=True)
                    m.then_inc(wo_ok, 1)

                project_out(0)
                project_out(1)
                for g in range(NG):
                    u = 4 * f + g
                    e.wait_ge(xn_ok, u + 1)
                    for t in range(GT):
                        m = transpose(PS[:, 0, t * P:(t + 1) * P], xn[:, t, :])
                    m.then_inc(xT_ok, 1)
                    if g:
                        project_out(g + 1)
                    e.wait_ge(xs_ok, u + 1)
                    if a2 is not None:
                        products_read(4 * a2 + g)
                        for w, bk in ((2, 3), (3, 4), (0, 1), (1, 2)):
                            if f == 0 or w % 2 == 0:
                                e.matmul(bank(bk), w_qkv[:, a2, w * P:(w + 1) * P], xTs[:], start=True, stop=True)\
                                    .then_inc(proj_ok, 1)
                        for t in range(GT):
                            m = e.matmul(PS[:, 5, t * P:(t + 1) * P], xTs[:, t * P:(t + 1) * P],
                                         w_qkv[:, a2, 4 * P:5 * P], start=True, stop=True)
                        m.then_inc(proj_ok, 1)
                    else:
                        w, ne = (w_rt0[:, 0:NE0 - 1], NE0 - 1) if f == 1 else (w_rt1[:], NE1)
                        for t in range(GT):
                            c = (GT * g + t) * NE1
                            m = e.matmul(PS[:, 7, c:c + ne], xTs[:, t * P:(t + 1) * P], w, start=True, stop=True)
                        m.then_inc(lgt_ok, 1)
                if a2 is None:
                    e.wait_ge(gsp_ok, 1 + (f == 4))
                    for g in range(NG):
                        gates(g)

            def attention(a):
                HB = NH * a
                def scores(n, s, qt, kh):
                    if kh == 0:
                        e.wait_ge(max_done, 8 * (HB + n) + qt + 1)
                    m = e.matmul(bank(2 + 2 * (qt % 2) + kh), Qs[0:ROWS, s, qt * P:(qt + 1) * P],
                                 Ks[0:ROWS, s, kh * GW:(kh + 1) * GW], start=True, stop=True)
                    if kh == 1:
                        m.then_inc(s_done, 1)

                def max_transpose(n, s):
                    e.wait_ge(m_split, HB + n + 1)
                    e.wait_ge(mt_copied, HB + n)
                    e.transpose(bank(7, BF16)[0:PARTS * QT, 0:P], Ms[:, s, :, :].rearrange("p a q -> p (a q)"),
                                identb[:]).then_inc(mt_done, 1)

                def values(n, s, kt):
                    if kt == 0:
                        e.wait_ge(v_ready, HB + n + 1)
                        e.wait_ge(o_copied, (NH + 1) * a + n + 1)
                    for g in range(4):
                        m = e.matmul(PS[32 * g:32 * g + VC, 6, 0:256], Va[:, s, kt, :],
                                     PR[:, kt % 4, g * 256:(g + 1) * 256], start=(kt == 0), stop=(kt == QT - 1))
                    m.then_inc(pv_done, 1)

                def position(i, s, last):
                    n = SLOTS * i + s
                    s1, s2 = (s + 1) % SLOTS, (s + 2) % SLOTS
                    e.wait_ge(m_in[s], 16 * (NH // SLOTS * a + i + 1))
                    for x in range(16):
                        if x == 2 * LATE and not (last and s >= 2):
                            e.wait_ge(qk_in[s2], 48 * (NH // SLOTS * a + i + (s >= 2) + 1))
                        e.wait_ge(exp_done, 16 * (HB + n) + x + 1)
                        kt, qh = x // 2, x % 2
                        e.matmul(bank(x % 2), Ks[0:ROWS, s, kt * P:(kt + 1) * P],
                                 Qs[0:ROWS, s, qh * GW:(qh + 1) * GW], start=True, stop=True).then_inc(st_done, 1)
                        if x == 10 and not (last and s == 3):
                            max_transpose(n + 1, s1)
                        if x < 2 * LATE and not (last and s == 3):
                            scores(n + 1, s1, QT - LATE + x // 2, x % 2)
                        if x >= 2 * LATE and not (last and s >= 2):
                            scores(n + 2, s2, x // 2 - LATE, x % 2)
                        if x == 1 and s:
                            values(n - 1, s - 1, QT - 1)
                        if x % 2 and x >= 3:
                            values(n, s, (x - 3) // 2)
                    if s == SLOTS - 1:
                        e.wait_ge(exp_done, 2 + 16 * (HB + n) + 16)
                        values(n, s, QT - 1)

                if a == 0:
                    e.sem_inc(exp_done, 2)
                    e.sem_inc(pv_done, 4)
                products_read(4 * (a + 1))
                if a == 0:
                    e.wait_ge(c_in, 16 * N_CONST)
                for n in range(2):
                    e.wait_ge(qk_in[n], 48 * (NH // SLOTS * a + 1))
                    for x in range(2 * [QT, QT - LATE][n]):
                        scores(n, n, x // 2, x % 2)
                max_transpose(0, 0)
                with e.Fori(0, NH // SLOTS - 1) as i:
                    for s in range(SLOTS):
                        position(i, s, False)
                for s in range(SLOTS):
                    position(NH // SLOTS - 1, s, True)

            def relative_attention():
                def prep(n, k, s, p):
                    if p == 0:
                        e.wait_ge(ws_in[s], 16 * (k + 1))
                        e.wait_ge(qk_in[s], 48 * (2 * NH // SLOTS + k + 1))
                    e.wait_ge(prep_mul, 4 * n + p)
                    e.matmul(bank(6), Ws[0:ROWS, s, (p % 2) * P:(p % 2 + 1) * P],
                             Qs[0:ROWS, s, (p // 2) * GW:(p // 2 + 1) * GW], start=True, stop=True)\
                        .then_inc(prep_ps, 1)

                def scores(n, s, qt):
                    if qt % 4 == 0:
                        e.wait_ge(prep_split, 2 * n + qt // 4 + 1)
                    e.wait_ge(rexp, 8 * n + qt + 1)
                    for kh in range(2):
                        o = bank(2 * (qt % 2) + kh)
                        e.matmul(o, Qs[0:ROWS, s, qt * P:(qt + 1) * P], Ks[0:ROWS, s, kh * GW:(kh + 1) * GW],
                                 start=True, stop=False)
                        for n_a, a_part, e_part in ((0, Ah, El), (1, Al, Eh), (2, Ah, Eh)):
                            m = e.matmul(o, a_part[:, s, qt * P:(qt + 1) * P], e_part[:, kh * GW:(kh + 1) * GW],
                                         start=False, stop=(n_a == 2))
                    m.then_inc(rs_done, 1)

                def position(i, s, last):
                    n = 2 * i + s
                    end = last and s == 1
                    for qt in range(QT):
                        u = 8 * n + qt
                        e.wait_ge(rexp, 2 + u + 1)
                        e.wait_ge(rev_a, 1 + u)
                        e.wait_ge(rev_d, 1 + u)
                        for kt in range(QT):
                            m = transpose(PS[:, 4 + kt // 4, (kt % 4) * P:(kt % 4 + 1) * P],
                                          PR[:, qt % 2, kt * P:(kt + 1) * P])
                        m.then_inc(rt_done, 1)
                        if 2 <= qt < 6 and not end:
                            prep(n + 1, i + (s == 1), 1 - s, qt - 2)
                        if qt < 6:
                            scores(n, s, qt + 2)
                        elif not end:
                            scores(n + 1, 1 - s, qt - 6)
                    e.wait_ge(rev_a, 1 + 8 * n + 8)
                    e.wait_ge(rev_d, 1 + 8 * n + 8)
                    e.wait_ge(ro_copied, 1 + n)
                    e.wait_ge(rv_ready, n + 1)
                    for kt in range(QT):
                        for g in range(4):
                            m = e.matmul(PS[32 * g:32 * g + VC, 7, 0:256], Va[:, s, kt, :],
                                         PQ[:, kt, g * 256:(g + 1) * 256], start=(kt == 0), stop=(kt == QT - 1))
                    m.then_inc(rpv, 1)

                e.sem_inc(rexp, 2)
                products_read(12)
                for p in range(4):
                    prep(0, 0, 0, p)
                e.wait_ge(table_split, 1)
                scores(0, 0, 0)
                scores(0, 0, 1)
                with e.Fori(0, NH // 2 - 1) as i:
                    for s in range(2):
                        position(i, s, False)
                for s in range(2):
                    position(NH // 2 - 1, s, True)

            def zero_acc(k):
                e.wait_ge(acc_zero, k + 1)
                for b in range(4, 8):
                    e.matmul(bank(b), acc[:, 0, 0:P], acc[:, 0, :], start=True, stop=True, skip_group_check=True)

            def spread(x, ring, tg):
                e.matmul(bank(ring), sel[0:ROWS, x, :], GTs[0:ROWS, tg * GW:(tg + 1) * GW], start=True, stop=True)\
                    .then_inc(b_ps, 1)

            def three(out, w, h, start):
                for n, (a, b) in enumerate(((0, 1), (1, 0), (0, 0))):
                    m = e.matmul(out, w[a], h[b], start=start and n == 0, stop=n == 2 or not start,
                                 skip_group_check=not start)
                return m

            def experts0():
                zero_acc(0)
                x_parts = (XTh, XTl)

                def down(v, par, tg, c):
                    lo, w = FCH[c]
                    e.wait_ge(lo_ok, 3 * v + c + 1)
                    m = three(bank(4 + tg), [wdp[0:w, par, r, c, :] for r in range(2)],
                              [h0p[0:w, r, tg % 2, c, :] for r in range(2)], False)
                    if c == 2:
                        m.then_inc(dn_ok, 1)

                def up(place, par, tg, c, k):
                    lo, w = FCH[c]
                    h = [xwp[r][:, tg % 2, :] for r in range(2)] if k else \
                        [x_parts[r][:, tg * GW:(tg + 1) * GW] for r in range(2)]
                    three(PS[0:w, (7 * tg + place) % 4, :], [wgp[par][:, r, k, lo:lo + w] for r in range(2)], h, True)\
                        .then_inc([g_ps, u_ps][k], 1)

                def unit(x, par, tg, first, last):
                    v = NG * x + tg
                    if tg == 0:
                        e.wait_ge(w0_ok, x + 1)
                    e.wait_ge(h_ok, count(3 * v - 2))
                    up(0, par, tg, 0, 0)
                    if not (last and tg == NG - 1):
                        e.wait_ge(h_ok, count(3 * v - 1))
                        y, t2 = (x, tg + 1) if tg < NG - 1 else (x + 1, 0)
                        e.matmul(bank((7 * tg + 1) % 4), sel[0:ROWS, y, :], GTs[0:ROWS, t2 * GW:(t2 + 1) * GW],
                                 start=True, stop=True).then_inc(b_ps, 1)
                    e.wait_ge(sg_ok, count(3 * v))
                    if first and tg == 0:
                        e.wait_ge(xw_ok, 1)
                    up(2, par, tg, 1, 0)
                    par2, tg2 = (par, tg - 1) if tg else (1 - par, NG - 1)
                    before = not (first and tg == 0)
                    if before:
                        down(v - 1, par2, tg2, 0)
                    e.wait_ge(h_ok, count(3 * v))
                    e.wait_ge(xlo_ok, v + 1)
                    up(3, par, tg, 0, 1)
                    if before:
                        down(v - 1, par2, tg2, 1)
                    e.wait_ge(sg_ok, 3 * v + 1)
                    up(4, par, tg, 1, 1)
                    if not (last and tg == NG - 1):
                        e.wait_ge(xw_ok, v + 2)
                    up(5, par, tg, 2, 0)
                    if before:
                        down(v - 1, par2, tg2, 2)
                    e.wait_ge(sg_ok, 3 * v + 2)
                    up(6, par, tg, 2, 1)

                e.matmul(bank(2), sel[0:ROWS, 0, :], GTs[0:ROWS, 0:GW], start=True, stop=True).then_inc(b_ps, 1)
                for tg in range(NG):
                    unit(0, 0, tg, True, False)
                with e.Fori(0, NE0 // 2 - 1) as i:
                    for s in range(2):
                        for tg in range(NG):
                            unit(2 * i + 1 + s, 1 - s, tg, False, False)
                for tg in range(NG):
                    unit(NE0 - 1, 1, tg, False, True)
                for c in range(3):
                    down(NG * NE0 - 1, 1, NG - 1, c)

            def experts1():
                zero_acc(1)

                def values(s, tg):
                    three(bank(4 + tg), [wsp[:, s, 1, r, :] for r in range(2)], (hhi[:, tg, :], hlo[:, tg, :]), False)\
                        .then_inc(val_ok, 1)

                def unit(i, s, tg):
                    x = SLOTS * i + s
                    v = NG * x + tg
                    early = isinstance(v, int) and v < 3
                    if tg == 0:
                        e.wait_ge(wsp_ok, x + 1)
                    if not (isinstance(v, int) and v < 2):
                        e.wait_ge(hf_ok, v - 1)
                    cols_ = slice(tg * GW, (tg + 1) * GW)
                    e.matmul(bank(2 * (tg % 2)), sel[0:ROWS, x, :], GTs[0:ROWS, cols_], start=True, stop=True)
                    three(bank(2 * (tg % 2) + 1), [wsp[:, s, 0, r, :] for r in range(2)],
                          (XTh[:, cols_], XTl[:, cols_]), True).then_inc(key_ps, 1)
                    if not early:
                        e.wait_ge(hlo_ok, v - 2)
                        values(s if tg == 3 else (s - 1) % SLOTS, (tg + 1) % NG)

                for s in range(SLOTS):
                    for tg in range(NG):
                        unit(0, s, tg)
                with e.Fori(0, NE1 // SLOTS - 1) as i:
                    for s in range(SLOTS):
                        for tg in range(NG):
                            unit(i + 1, s, tg)
                for tg in range(1, NG):
                    e.wait_ge(hlo_ok, NG * NE1 - NG + tg + 1)
                    values(SLOTS - 1, tg)

            def back(k):
                for g in range(NG):
                    e.wait_ge(acc_ok, 4 * k + g + 1)
                    for t in range(GT):
                        m = transpose(PS[:, BACK[g], t * P:(t + 1) * P], acc[:, g, t * P:(t + 1) * P])
                    m.then_inc(wo_ok, 1)

            def front2():
                back(0)
                front(2)

            plan = [lambda: front(0), lambda: attention(0), lambda: front(1), experts0, front2,
                    lambda: attention(1), lambda: front(3), relative_attention, lambda: front(4), experts1]
            for k, run in enumerate(plan):
                run()
                meet(e, "pe", k + 1)
            back(1)

        @block.vector
        def _(e):
            start(e, "dve")
            own = Steps(e, own_dve)
            norms = [0]

            def row_sums(k, b):
                e.wait_ge(rs_in, 16 * (NB * k + b + 1))
                e.reciprocal(rs[:, b, :], rs[:, b, :]).then_inc(rs_ok, 1)

            def layernorm(src, dst, before, done):
                for t in range(GT):
                    own(e.bn_stats(st[:, t, :], src[:, t, :]))
                own.settle()
                for t in range(GT):
                    own(e.bn_aggr(mv[:, t, :], st[:, t, :]))
                own.settle()
                e.tensor_scalar(sd[:, 0, :], mv[:, :, 1], EPS, None, ALU.add).then_inc(var_ok, 1)
                norms[0] += 1
                e.wait_ge(sd_ok, norms[0])
                own(e.reciprocal(sd[:, 1, :], sd[:, 0, :]))
                e.wait_ge(xT_ok, before)
                own.settle()
                for t in range(GT):
                    ins = e.tensor_scalar(dst[:, t, :], src[:, t, :], mv[:, t, 0:1], sd[:, 1, t:t + 1],
                                          ALU.subtract, ALU.mult)
                    if t == GT - 1:
                        ins.then_inc(done, 1)
                    else:
                        own(ins)

            def split(dst, src, res):
                own(e.tensor_copy(dst(0), src))
                own.settle()
                own(e.tensor_tensor(res[0], src, dst(0), ALU.subtract))
                own.settle()
                own(e.tensor_copy(dst(1), res[0]))
                own.settle()
                own(e.tensor_tensor(res[1], res[0], dst(1), ALU.subtract))
                own.settle()
                return e.tensor_copy(dst(2), res[1])

            def front(f):
                a = {1: 0, 3: 1, 4: 2}.get(f)
                a2 = {0: 0, 2: 1, 3: 2}.get(f)

                def heads_in(g):
                    if a is None or g >= NG:
                        return
                    half = g % 2
                    e.wait_ge(at_in[half], 16 * 4 * (2 * a + g // 2 + 1))
                    e.tensor_tensor(atn[:, half, :], atu[:, half, 0, :], atu[:, half, 1, :], ALU.mult)\
                        .then_inc(atn_ok, 1)

                def rows_in(g):
                    u = 4 * f + g
                    xg = X[:, GT * g:GT * g + GT, :]
                    sg_ = SRC[:, GT * g:GT * g + GT, :]
                    if f == 0:
                        e.wait_ge(x_in[g], 16)
                    if f == 2:
                        back_in(0, g)
                    if a is not None:
                        e.wait_ge(wo_ok, 4 * [0, 2, 3][a] + g + 1)
                        y = PS[:, [4, 6][g % 2], :].rearrange("p (t d) -> p t d", t=GT)
                        if f > 2:
                            e.wait_ge(xadd_ok, 4 * (f - 3) + g + 1)
                        own(e.tensor_tensor(xg, xg, y, ALU.add))
                        if a == 2:
                            own(e.tensor_tensor(sg_, sg_, y, ALU.add))
                        own.settle()
                    if f in (2, 3):
                        layernorm(xg, sg_, u, src_ok)
                        own.settle()
                        e.wait_ge(src_ok, 4 * (f - 2) + g + 1)
                    layernorm(xg if f < 2 else sg_, xn, u, xn_ok)

                heads_in(0)
                heads_in(1)
                rows_in(0)
                if a is not None:
                    row_sums(a, 1)
                for g in range(NG):
                    if g + 1 < NG:
                        rows_in(g + 1)
                    heads_in(g + 2)
                    if a2 is not None:
                        project(f, a2, g)
                if a2 is None:
                    route(f)

            def project(f, a2, g):
                b, half = g // 2, g % 2
                pr = 5 * g if f == 0 else 20 + 12 * (a2 - 1) + 3 * g
                tok = slice(half * GW, (half + 1) * GW)

                k_in = kin[g % 2]
                if f == 0:
                    e.wait_ge(split_k, 4 * a2 + max(0, g - 1))
                    e.wait_ge(rope_in, 16)
                    e.wait_ge(proj_ok, pr + 2)
                    own(e.tensor_tensor(rt[:, 0, :], bank(3), rope[:, 0, tok], ALU.mult))
                    own(e.tensor_tensor(rt[:, 1, :], bank(4), rope[:, 1, tok], ALU.mult))
                    own.settle()
                    e.tensor_tensor(k_in, rt[:, 0, :], rt[:, 1, :], ALU.add).then_inc(kin_ok, 1)
                    e.wait_ge(kin_ok, 4 * a2 + g + 1)
                    e.wait_ge(proj_ok, pr + 4)
                    own(e.tensor_tensor(rt[:, 0, :], bank(1), rope[:, 0, tok], ALU.mult))
                    own(e.tensor_tensor(rt[:, 1, :], bank(2), rope[:, 1, tok], ALU.mult))
                    own.settle()
                    e.tensor_tensor(qk[:, 0, :], rt[:, 0, :], rt[:, 1, :], ALU.add).then_inc(qin_ok, 1)
                if f == 2:
                    e.wait_ge(proj_ok, pr + 3)
                    for t in range(GT):
                        m = e.tensor_tensor(Vt[:, H * b:H * b + H, half * GT + t, :],
                                            PS[:, 5, t * P:(t + 1) * P].rearrange("p (h d) -> p h d", h=H),
                                            rows[:, 0, :].rearrange("p (h d) -> p h d", h=H), ALU.add)
                        if t < GT - 1:
                            own(m)
                    m.then_inc(v_ok, 1)
                own.settle()
                e.wait_ge(stq_out, 16 * 3 * (4 * a2 + g))
                e.wait_ge(qin_ok, 4 * a2 + g + 1)
                split(lambda j: sp[:, 0, j, :], qk[:, 0, :], (rt[:, 0, :], rt[:, 1, :])).then_inc(split_q, 1)
                e.wait_ge(split_q, 4 * a2 + g + 1)
                own.settle()
                if g + 1 == NG:
                    e.wait_ge(v_ok, 4 * (a2 + 1))

            def route(f):
                m = f == 4
                ne, top = (NE1, 4) if m else (NE0 - 1, 2)
                own(e.memset(lg[:], -1.0))
                own(e.memset(rp[:], -1.0))
                own(e.memset(gate[:], 0.0))
                own.settle()
                own(e.memset(gate[:, :, 0:1], 1.0))
                own.settle()
                e.wait_ge(lgt_ok, NG * (1 + m))
                ps = PS[:, 7, :].rearrange("p (t x) -> p t x", t=TT)[:, :, 0:ne]
                val = lg[:, :, 0:ne]

                def each(v, k=ne):
                    return v.unsqueeze(2).broadcast_to([P, TT, k])
                if not m:
                    own(e.tensor_tensor(lg2[:, :, 0:ne], ps, rows[:, 2, 0:ne].unsqueeze(1).broadcast_to([P, TT, ne]),
                                        ALU.add))
                    own.settle()
                    own(e.tensor_reduce(sm[:, 0, :], lg2[:, :, 0:ne], AX.X, ALU.max))
                    own.settle()
                    e.tensor_tensor(val, lg2[:, :, 0:ne], each(sm[:, 0, :]), ALU.subtract).then_inc(ex_in, 1)
                    e.wait_ge(ex_ok, 1 + m)
                    own(e.tensor_reduce(sm[:, 0, :], val, AX.X, ALU.add))
                    own.settle()
                    own(e.reciprocal(sm[:, 1, :], sm[:, 0, :]))
                    own.settle()
                    own(e.tensor_tensor(val, val, each(sm[:, 1, :]), ALU.mult))
                    own.settle()
                else:
                    e.sem_inc(ex_in, 1)
                    e.wait_ge(ex_ok, 1 + m)
                    own(e.tensor_scalar(val, val, 1.0, None, ALU.add))
                    own.settle()
                    own(e.reciprocal(val, val))
                    own.settle()
                own.settle()
                for t in range(TT):
                    own(e.max(m8[:, t, :], lg[:, t, 0:ne + 8]))
                own.settle()
                own(e.tensor_copy(rp[:, :, 0:top], m8[:, :, 0:top]))
                own.settle()
                for t in range(TT):
                    own(e.match_replace(lg2[:, t, 0:ne + 8], rp[:, t, :], lg[:, t, 0:ne + 8], 0.0))
                own.settle()
                g0 = gate[:, :, 0:ne] if m else gate[:, :, 1:ne + 1]
                own(e.tensor_tensor(g0, val, lg2[:, :, 0:ne], ALU.subtract))
                own.settle()
                if not m:
                    own(e.tensor_reduce(sm[:, 0, :], g0, AX.X, ALU.add))
                    own.settle()
                    own(e.reciprocal(sm[:, 1, :], sm[:, 0, :]))
                    own.settle()
                    own(e.tensor_tensor(g0, g0, each(sm[:, 1, :]), ALU.mult))
                    own.settle()
                split(lambda j: gsp[:, :, j, :], gate[:], (gres[:, 0], gres[:, 1])).then_inc(gsp_ok, 1)
                for g in range(NG):
                    e.wait_ge(gtp_ok, NG * m + g + 1)
                    e.tensor_copy(GTs[0:ROWS, g * GW:(g + 1) * GW], bank(g, BF16)[0:ROWS, 0:GW]).then_inc(gt_ok, 1)
                e.wait_ge(gt_ok, NG * (1 + m))

            def attention(a):
                HB = NH * a
                e.memset(PS[:, 6, 0:256], 0.0).then_inc(o_zero, 1)
                if a == 0:
                    e.wait_ge(c_in, 16 * N_CONST)
                    e.sem_inc(max_done, 2)

                def row_max(n, s, qt):
                    e.wait_ge(s_done, 8 * (HB + n) + qt + 1)
                    e.tensor_reduce(M[:, s, qt:qt + 1], PS[:, 2 + 2 * (qt % 2):4 + 2 * (qt % 2), :]
                                    .rearrange("p a b -> p (a b)"), AX.X, ALU.max, negate=True).then_inc(max_done, 1)

                def max_copy(n, s):
                    e.wait_ge(mt_done, HB + n + 1)
                    e.tensor_copy(MT[:, s, :], bank(7, BF16)[0:PARTS * QT, 0:P]).then_inc(mt_copied, 1)

                for n in range(2):
                    for qt in range([QT, QT - LATE][n]):
                        row_max(n, n, qt)
                max_copy(0, 0)

                def position(i, s, last):
                    n = SLOTS * i + s
                    if not (last and s == 3):
                        for qt in range(QT - LATE, QT):
                            row_max(n + 1, (s + 1) % SLOTS, qt)
                    for qt in range(QT - LATE):
                        if qt == 2 and not (last and s == 3):
                            max_copy(n + 1, (s + 1) % SLOTS)
                        if not (last and s >= 2):
                            row_max(n + 2, (s + 2) % SLOTS, qt)
                with e.Fori(0, NH // SLOTS - 1) as i:
                    for s in range(SLOTS):
                        position(i, s, False)
                for s in range(SLOTS):
                    position(NH // SLOTS - 1, s, True)
                row_sums(a, 0)

            def relative_attention():
                def prep(n, s, p):
                    e.wait_ge(prep_ps, 4 * n + p + 1)
                    e.wait_ge(prep_add, 2 * n + p // 2)
                    e.tensor_tensor(tA[:, p % 2, :], bank(6), rel[:, p % 2, (p // 2) * GW:(p // 2 + 1) * GW],
                                    ALU.mult).then_inc(prep_mul, 1)

                def row_max(n, s, qt):
                    e.wait_ge(rs_done, 8 * n + qt + 1)
                    e.tensor_reduce(M[:, s, qt:qt + 1], PS[:, 2 * (qt % 2):2 * (qt % 2) + 2, :]
                                    .rearrange("p a b -> p (a b)"), AX.X, ALU.max, negate=True).then_inc(rmax, 1)

                def position(i, s, last):
                    n = 2 * i + s
                    end = last and s == 1
                    for qt in range(QT):
                        u = 8 * n + qt
                        if qt < 7:
                            row_max(n, s, qt + 1)
                        elif not end:
                            row_max(n + 1, 1 - s, 0)
                        e.wait_ge(rt_done, 1 + u + 1)
                        if qt == 0:
                            e.wait_ge(rpv, 1 + n)
                        e.tensor_copy(PQ[:, 4:8, qt * P:(qt + 1) * P], PS[:, 5, :].rearrange("p (k q) -> p k q", k=4))\
                            .then_inc(rev_d, 1)
                        if 2 <= qt < 6 and not end:
                            prep(n + 1, 1 - s, qt - 2)

                for p in range(4):
                    prep(0, 0, p)
                row_max(0, 0, 0)
                with e.Fori(0, NH // 2 - 1) as i:
                    for s in range(2):
                        position(i, s, False)
                position(NH // 2 - 1, 0, True)
                row_sums(2, 0)
                position(NH // 2 - 1, 1, True)

            def zero_acc():
                e.memset(acc[:, 0, :], 0.0).then_inc(acc_zero, 1)

            def experts0():
                zero_acc()

                def weights(x, par, k):
                    e.wait_ge(ew_in[par], 32 * (k + 1))
                    e.wait_ge(dn_ok, count(NG * (x - 1)))
                    own(e.tensor_copy(wgp[par][:, 0], wg[:, par]))
                    own(e.tensor_copy(wdp[:, par, 0], wd[:, par]))
                    own.settle()
                    own(e.tensor_tensor(wgp[par][:, 1], wg[:, par], wgp[par][:, 0].bitcast(F32), ALU.subtract))
                    e.tensor_tensor(wdp[:, par, 1], wd[:, par], wdp[:, par, 0].bitcast(F32), ALU.subtract)\
                        .then_inc(w0_ok, 1)

                def gated(v, tg, b):
                    e.wait_ge(b_ps, v + 1)
                    e.wait_ge(xlo_ok, count(v - 1))
                    e.tensor_tensor(xw[:, tg % 2, :], XT[:, tg * GW:(tg + 1) * GW], bank(b), ALU.mult)\
                        .then_inc(xw_ok, 1)

                def unit(x, par, tg, k, last):
                    v = NG * x + tg
                    if not (last and tg == NG - 1):
                        gated(v + 1, (tg + 1) % NG, (7 * tg + 1) % 4)
                    for c, (lo, w) in enumerate(FCH):
                        e.wait_ge(u_ps, 3 * v + c + 1)
                        e.wait_ge(sg_ok, 3 * v + c + 1)
                        e.wait_ge(lo_ok, count(3 * v - 2 + c))
                        e.tensor_tensor(h0[0:w, c, :], PS[0:w, (7 * tg + [3, 4, 6][c]) % 4, :], sg[0:w, c, :],
                                        ALU.mult).then_inc(h_ok, 1)
                        if c == 1 and tg == 1 and not last:
                            weights(x + 1, 1 - par, k)

                weights(0, 0, 0)
                gated(0, 0, 2)
                for tg in range(NG):
                    unit(0, 0, tg, 0, False)
                with own.loop(NE0 // 2 - 1, 6) as i:
                    for s in range(2):
                        for tg in range(NG):
                            unit(2 * i + 1 + s, 1 - s, tg, i + 1, False)
                for tg in range(NG):
                    unit(NE0 - 1, 1, tg, 0, True)

            def experts1():
                e.memset(acc[:, 0, :], 0.0).then_inc(acc_zero, 1)

                def weights(x, s, k):
                    e.wait_ge(ew_in[s % 2], 16 * (NE0 + k + 1))
                    if not (isinstance(x, int) and x < SLOTS):
                        e.wait_ge(val_ok, NG * (x - SLOTS + 1))
                    own(e.tensor_copy(wsp[:, s, :, 0, :], we[:, s % 2]))
                    own.settle()
                    e.tensor_tensor(wsp[:, s, :, 1, :], we[:, s % 2], wsp[:, s, :, 0, :].bitcast(F32), ALU.subtract)\
                        .then_inc(wsp_ok, 1)

                def unit(i, s, tg, last=False):
                    v = NG * (SLOTS * i + s) + tg
                    if tg == 1 and not (last and s == SLOTS - 1):
                        weights(SLOTS * i + s + 1, (s + 1) % SLOTS, 2 * i + (s + 1) // 2)
                    e.wait_ge(relu_ok, v + 1)
                    if not (isinstance(v, int) and v < NG):
                        e.wait_ge(hlo_ok, v - NG + 1)
                    e.tensor_tensor(hf[:, tg, :], bank(2 * (tg % 2)), sg1[:, tg % 2, :], ALU.mult).then_inc(hf_ok, 1)

                weights(0, 0, 0)
                for s in range(SLOTS):
                    for tg in range(NG):
                        unit(0, s, tg)
                with own.loop(NE1 // SLOTS - 2, SLOTS) as i:
                    for s in range(SLOTS):
                        for tg in range(NG):
                            unit(i + 1, s, tg)
                for s in range(SLOTS):
                    for tg in range(NG):
                        unit(NE1 // SLOTS - 1, s, tg, True)

            def back(k):
                e.wait_ge([dn_ok, val_ok][k], NG * [NE0, NE1][k])
                for g in range(NG):
                    e.tensor_copy(acc[:, g, :], bank(4 + g)).then_inc(acc_ok, 1)

            def back_in(k, g):
                e.wait_ge(wo_ok, [4, 16][k] + g + 1)
                xg = X[:, GT * g:GT * g + GT, :].rearrange("p t d -> p (t d)")
                e.tensor_tensor(xg, xg, bank(BACK[g]), ALU.add).then_inc(xres, 1)
                e.wait_ge(xres, 4 * k + g + 1)

            def front2():
                back(0)
                front(2)

            def front3():
                w = PT[:, 0, 0:2, 0, :]
                res = [PT[:, 0, 2:4, 0, :], PT[:, 0, 4:6, 0, :]]

                def part(j):
                    return PT[:, 1, j, 0:2, :].rearrange("p a f -> p (a f)").bitcast(BF16)[:, 0:2 * P]\
                        .rearrange("p (a f) -> p a f", a=2)
                e.wait_ge(wp_in, 16)
                split(part, w, res).then_inc(wsplit, 1)
                front(3)

            plan = [lambda: front(0), lambda: attention(0), lambda: front(1), experts0, front2,
                    lambda: attention(1), front3, relative_attention, lambda: front(4), experts1]
            for k, run in enumerate(plan):
                run()
                meet(e, "dve", k + 1)
            back(1)
            for g in range(NG):
                back_in(1, g)

        @block.scalar
        def _(e):
            start(e, "act")
            norms = [0]

            def front(f):
                a2 = {0: 0, 2: 1, 3: 2}.get(f)

                def projected(g):
                    if a2 is None or g < 0:
                        return
                    b, half = g // 2, g % 2
                    pr = 5 * g if f == 0 else 20 + 12 * (a2 - 1) + 3 * g
                    if f > 0:
                        e.wait_ge(proj_ok, pr + 1)
                        e.wait_ge(split_k, 4 * a2 + max(0, g - 1))
                        if f == 2:
                            e.activation(kin[half], bank(3), ACT.Identity, bias=cols[:, 3:4]).then_inc(kin_ok, 1)
                        else:
                            e.activation(kin[half], bank(3), ACT.Copy).then_inc(kin_ok, 1)
                        e.wait_ge(proj_ok, pr + 2)
                        e.wait_ge(split_q, 4 * a2 + g)
                        if f == 2:
                            e.activation(qk[:, 0, :], bank(1), ACT.Identity, bias=cols[:, 2:3]).then_inc(qin_ok, 1)
                        else:
                            e.activation(qk[:, 0, :], bank(1), ACT.Copy, scale=SCALE).then_inc(qin_ok, 1)
                    if f != 2:
                        e.wait_ge(proj_ok, pr + (5 if f == 0 else 3))
                        e.activation(Vt[:, H * b:H * b + H, half * GT:half * GT + GT, :]
                                     .rearrange("p h t d -> p t h d"),
                                     PS[:, 5, :].rearrange("p (t h d) -> p t h d", t=GT, h=H), ACT.Copy)\
                            .then_inc(v_ok, 1)

                for g in range(NG):
                    for k in range(2 if f in (2, 3) else 1):
                        norms[0] += 1
                        e.wait_ge(var_ok, norms[0])
                        e.activation(sd[:, 0, :], sd[:, 0, :], ACT.Sqrt).then_inc(sd_ok, 1)
                    projected(g - 1)
                    e.wait_ge(xT_ok, 4 * f + g + 1)
                    if f >= 1:
                        e.wait_ge(xs_used, [0, 0, 4, 4, 4][f] + (g if f in (1, 4) else 0))
                    if f < 2:
                        e.activation(xTs[:], bank(0), ACT.Copy).then_inc(xs_ok, 1)
                    else:
                        c = {2: 0, 3: 4, 4: 6}[f]
                        e.activation(xTs[:], bank(0), ACT.Identity, scale=cols[:, c:c + 1],
                                     bias=cols[:, c + 1:c + 2]).then_inc(xs_ok, 1)
                projected(NG - 1)
                if f == 1:
                    e.wait_ge(ex_in, 1)
                    e.activation(lg[:, :, 0:NE0 - 1], lg[:, :, 0:NE0 - 1], ACT.Exp).then_inc(ex_ok, 1)
                if f == 4:
                    e.wait_ge(ex_in, 2)
                    e.activation(lg[:, :, 0:NE1], PS[:, 7, :].rearrange("p (t x) -> p t x", t=TT), ACT.Exp, scale=-1.0)\
                        .then_inc(ex_ok, 1)

            def attention(a):
                HB = NH * a

                def evacuate(k, buf, before):
                    e.wait_ge(pv_done, 4 + 8 * (HB + k))
                    e.wait_ge(o_out[buf], 1 + before)
                    e.activation(Ob[:, buf, :], PS[:, 6, 0:256], ACT.Copy).then_inc(o_copied, 1)

                def position(i, s):
                    n = 2 * SLOTS * i + s
                    for x in range(16):
                        kt, qh = x // 2, x % 2
                        e.wait_ge(st_done, 1 + 16 * (HB + n) + x + 1)
                        if qh == 0:
                            e.wait_ge(pv_done, 8 * (HB + n) + kt + 1)
                        e.activation(PR[:, kt % 4, qh * GW:(qh + 1) * GW], bank(x % 2), ACT.Exp, scale=SCALE)\
                            .then_inc(exp_done, 1)
                        if x == 1:
                            evacuate(n, s % 2, 16 * ((17 - s % 2) * a + SLOTS * i + s // 2))

                e.wait_ge(c_in, 16 * N_CONST)
                e.wait_ge(o_zero, a + 1)
                with e.Fori(0, NH // (2 * SLOTS)) as i:
                    for s in range(2 * SLOTS):
                        position(i, s)
                evacuate(NH, 0, 16 * (17 * a + 16))

            def relative_attention():
                def exp(n, s, qt, k):
                    e.wait_ge(rmax, k + 1)
                    e.wait_ge(rt_done, k)
                    e.activation(PR[:, qt % 2, :], PS[:, 2 * (qt % 2):2 * (qt % 2) + 2, :]
                                 .rearrange("p a b -> p (a b)"), ACT.Exp, bias=M[:, s, qt:qt + 1]).then_inc(rexp, 1)

                def position(i, s, last):
                    n = 2 * i + s
                    end = last and s == 1
                    for qt in range(QT):
                        u = 8 * n + qt
                        e.wait_ge(rt_done, 1 + u + 1)
                        if qt == 0:
                            e.wait_ge(rpv, 1 + n)
                        e.activation(PQ[:, 0:4, qt * P:(qt + 1) * P], PS[:, 4, :].rearrange("p (k q) -> p k q", k=4),
                                     ACT.Copy).then_inc(rev_a, 1)
                        if qt < 7:
                            exp(n, s, qt + 1, u + 1)
                        elif not end:
                            exp(n + 1, 1 - s, 0, u + 1)
                    e.wait_ge(rpv, 1 + n + 1)
                    e.wait_ge(o_out[s], 1 + 16 * ((17 - s) * 2 + i))
                    e.activation(Ob[:, s, :], PS[:, 7, 0:256], ACT.Copy).then_inc(ro_copied, 1)

                exp(0, 0, 0, 0)
                with e.Fori(0, NH // 2 - 1) as i:
                    for s in range(2):
                        position(i, s, False)
                for s in range(2):
                    position(NH // 2 - 1, s, True)

            def experts0():
                def high(v, tg, c):
                    w = FCH[c][1]
                    e.wait_ge(h_ok, 3 * v + c + 1)
                    e.wait_ge(dn_ok, count(v - 1))
                    e.activation(h0p[0:w, 0, tg % 2, c, :], h0[0:w, c, :], ACT.Copy).then_inc(hi_ok, 1)

                def high_x(v, tg):
                    e.wait_ge(xw_ok, v + 1)
                    e.wait_ge(u_ps, count(3 * v - 3))
                    e.activation(xwp[0][:, tg % 2, :], xw[:, tg % 2, :], ACT.Copy).then_inc(xhi_ok, 1)

                def unit(x, tg, first, last):
                    v = NG * x + tg

                    def gate(c):
                        w = FCH[c][1]
                        e.wait_ge(g_ps, 3 * v + c + 1)
                        e.wait_ge(h_ok, count(3 * v - 2 + c))
                        e.activation(sg[0:w, c, :], PS[0:w, (7 * tg + [0, 2, 5][c]) % 4, :], ACT.Silu).then_inc(sg_ok, 1)
                    gate(0)
                    if not (first and tg == 0):
                        high(v - 1, (tg - 1) % NG, 2)
                    gate(1)
                    if not (last and tg == NG - 1):
                        high_x(v + 1, (tg + 1) % NG)
                    high(v, tg, 0)
                    gate(2)
                    high(v, tg, 1)

                high_x(0, 0)
                for tg in range(NG):
                    unit(0, tg, True, False)
                with e.Fori(0, NE0 // 2 - 1) as i:
                    for s in range(2):
                        for tg in range(NG):
                            unit(2 * i + 1 + s, tg, False, False)
                for tg in range(NG):
                    unit(NE0 - 1, tg, False, True)
                high(NG * NE0 - 1, NG - 1, 2)

            def experts1():
                def high(v, tg):
                    e.wait_ge(hf_ok, v + 1)
                    if not (isinstance(v, int) and v < NG):
                        e.wait_ge(val_ok, v - NG + 1)
                    e.activation(hhi[:, tg, :], hf[:, tg, :], ACT.Copy).then_inc(hhi_ok, 1)

                def unit(i, s, tg):
                    v = NG * (SLOTS * i + s) + tg
                    e.wait_ge(key_ps, v + 1)
                    if not (isinstance(v, int) and v < 2):
                        e.wait_ge(hf_ok, v - 1)
                    e.activation(sg1[:, tg % 2, :], bank(2 * (tg % 2) + 1), ACT.Relu).then_inc(relu_ok, 1)
                    if not (isinstance(v, int) and v < 1):
                        high(v - 1, (tg - 1) % NG)

                for s in range(SLOTS):
                    for tg in range(NG):
                        unit(0, s, tg)
                with e.Fori(0, NE1 // SLOTS - 1) as i:
                    for s in range(SLOTS):
                        for tg in range(NG):
                            unit(i + 1, s, tg)
                high(NG * NE1 - 1, NG - 1)

            plan = [lambda: front(0), lambda: attention(0), lambda: front(1), experts0, lambda: front(2),
                    lambda: attention(1), lambda: front(3), relative_attention, lambda: front(4), experts1]
            for k, run in enumerate(plan):
                run()
                meet(e, "act", k + 1)

        @block.gpsimd
        def _(e):
            own = Steps(e, own_pool)
            own(e.memset(zrow[:], 0.0))
            own(e.memset(nil[:], 0.0))
            own(e.memset(Va[:], 0.0))
            own(e.memset(Ws[:], 0.0))
            own.settle()
            own(e.memset(Ks[64:ROWS], 1.0))
            own(e.memset(Qs[64:ROWS], 0.0))
            own.settle()
            own(e.memset(Va[:, :, :, DH:DH + 1], 1.0))
            own.settle()
            def copy(dst, src):
                zeros = nil[:, 0:1]
                for _ in range(len(src.shape) - 2):
                    zeros = zeros.unsqueeze(1)
                return e.tensor_tensor(dst, src, zeros.broadcast_to(list(src.shape)), ALU.add)

            def front(f):
                def residual(g):
                    if f not in (2, 3) or g >= NG:
                        return
                    xg = X[:, GT * g:GT * g + GT, :]
                    e.wait_ge(src_ok, 4 * (f - 2) + g + 1)
                    ins = e.tensor_tensor(xg, xg, SRC[:, GT * g:GT * g + GT, :], ALU.add)
                    if f == 2:
                        own(ins)
                        own.settle()
                        ins = e.tensor_tensor(xg, xg, rows[:, 1, :].unsqueeze(1).broadcast_to([P, GT, P]), ALU.add)
                    ins.then_inc(xadd_ok, 1)

                if f == 3:
                    e.wait_ge(table_in, 16)
                    own(copy(Eh[:], PR[:, 3, :]))
                    own.settle()
                    e.tensor_tensor(El[:], PR[:, 3, :], Eh[:].bitcast(F32), ALU.subtract).then_inc(table_split, 1)
                residual(0)
                for g in range(NG):
                    residual(g + 1)
                    if f in (0, 2, 3):
                        a2 = {0: 0, 2: 1, 3: 2}[f]
                        e.wait_ge(kin_ok, 4 * a2 + g + 1)
                        e.wait_ge(stk_out, 16 * 3 * (4 * a2 + g))
                        kk = kin[g % 2]
                        own(copy(sp[:, 1, 0, :], kk))
                        own.settle()
                        own(e.tensor_tensor(kk, kk, sp[:, 1, 0, :], ALU.subtract))
                        own.settle()
                        own(copy(sp[:, 1, 1, :], kk))
                        own.settle()
                        own(e.tensor_tensor(kk, kk, sp[:, 1, 1, :], ALU.subtract))
                        own.settle()
                        copy(sp[:, 1, 2, :], kk).then_inc(split_k, 1)
                    else:
                        e.wait_ge(xs_ok, 4 * f + g + 1)
                        cols_ = slice(g * GW, (g + 1) * GW)
                        if f == 1:
                            own(copy(XT[:, cols_], xTs[:]))
                        own(copy(XTh[:, cols_], xTs[:]))
                        own.settle()
                        e.tensor_tensor(XTl[:, cols_], xTs[:], XTh[:, cols_].bitcast(F32), ALU.subtract)\
                            .then_inc(xs_used, 1)
                if f in (1, 4):
                    e.wait_ge(xs_used, [4, 8][f == 4])

            def value_slot(n, s, ready):
                copy(Va[:, s, :, 0:DH], Vt[:, bass.ds(n, 1), :, :].rearrange("p n k d -> p (n k) d"))\
                    .then_inc(ready, 1)

            def attention(a):
                HB = NH * a

                def split_max(n, s):
                    e.wait_ge(max_done, 2 + 8 * (HB + n + 1))
                    own(copy(Ms[:, s, 0, :], M[:, s, :]))
                    own.settle()
                    own(e.tensor_tensor(Mr[:, 0, :], M[:, s, :], Ms[:, s, 0, :], ALU.subtract))
                    own.settle()
                    own(copy(Ms[:, s, 1, :], Mr[:, 0, :]))
                    own.settle()
                    own(e.tensor_tensor(Mr[:, 1, :], Mr[:, 0, :], Ms[:, s, 1, :], ALU.subtract))
                    own.settle()
                    copy(Ms[:, s, 2, :], Mr[:, 1, :]).then_inc(m_split, 1)
                    e.wait_ge(m_split, HB + n + 1)

                e.wait_ge(v_ok, 4 * a + 4)
                if a == 0:
                    e.wait_ge(c_in, 16 * N_CONST)
                    own(e.tensor_copy(identb[:], ident[:]))
                    own.settle()
                for n in range(2):
                    value_slot(n, n, v_ready)
                    split_max(n, n)
                with own.loop(NH // SLOTS - 1, 4 * SLOTS) as i:
                    for s in range(SLOTS):
                        split_max(SLOTS * i + s + 2, (s + 2) % SLOTS)
                        value_slot(SLOTS * i + s + 2, (s + 2) % SLOTS, v_ready)
                for s in range(2):
                    n = NH - SLOTS + s + 2
                    split_max(n, n % SLOTS)
                    value_slot(n, n % SLOTS, v_ready)
                if a == 0:
                    own(e.tensor_copy(sel[0:ROWS], sel0[:].unsqueeze(2).broadcast_to([ROWS, NE1, P])))
                    own.settle()

            def relative_attention():
                def add(n, s, h):
                    e.wait_ge(prep_mul, 4 * n + 2 * h + 2)
                    half = slice(h * GW, (h + 1) * GW)
                    e.tensor_tensor(At[:, h, :], tA[:, 0, :], tA[:, 1, :], ALU.add).then_inc(prep_add, 1)
                    e.wait_ge(prep_add, 2 * n + h + 1)
                    own(copy(Ah[:, s, half], At[:, h, :]))
                    own.settle()
                    e.tensor_tensor(Al[:, s, half], At[:, h, :], Ah[:, s, half].bitcast(F32), ALU.subtract)\
                        .then_inc(prep_split, 1)

                e.wait_ge(v_ok, 12)
                for n in range(2):
                    value_slot(n, n, rv_ready)
                for h in range(2):
                    add(0, 0, h)
                with own.loop(NH // 2 - 1, 4) as i:
                    for s in range(2):
                        n = 2 * i + s
                        for h in range(2):
                            add(n + 1, 1 - s, h)
                        e.wait_ge(rpv, 1 + n + 1)
                        value_slot(n + 2, s, rv_ready)
                for h in range(2):
                    add(NH - 1, 1, h)

            def experts0():
                def low(v, tg, c):
                    w = FCH[c][1]
                    e.wait_ge(hi_ok, 3 * v + c + 1)
                    e.tensor_tensor(h0p[0:w, 1, tg % 2, c, :], h0[0:w, c, :], h0p[0:w, 0, tg % 2, c, :].bitcast(F32),
                                    ALU.subtract).then_inc(lo_ok, 1)

                def low_x(v, tg):
                    e.wait_ge(xhi_ok, v + 1)
                    e.tensor_tensor(xwp[1][:, tg % 2, :], xw[:, tg % 2, :], xwp[0][:, tg % 2, :].bitcast(F32),
                                    ALU.subtract).then_inc(xlo_ok, 1)

                def unit(x, tg, first, last):
                    v = NG * x + tg
                    if not (first and tg == 0):
                        low(v - 1, (tg - 1) % NG, 2)
                    if not (last and tg == NG - 1):
                        low_x(v + 1, (tg + 1) % NG)
                    low(v, tg, 0)
                    low(v, tg, 1)

                low_x(0, 0)
                for tg in range(NG):
                    unit(0, tg, True, False)
                with e.Fori(0, NE0 // 2 - 1) as i:
                    for s in range(2):
                        for tg in range(NG):
                            unit(2 * i + 1 + s, tg, False, False)
                for tg in range(NG):
                    unit(NE0 - 1, tg, False, True)
                low(NG * NE0 - 1, NG - 1, 2)

            def experts1():
                with e.Fori(0, NE1 // SLOTS) as i:
                    for s in range(SLOTS):
                        for tg in range(NG):
                            e.wait_ge(hhi_ok, NG * (SLOTS * i + s) + tg + 1)
                            e.tensor_tensor(hlo[:, tg, :], hf[:, tg, :], hhi[:, tg, :].bitcast(F32), ALU.subtract)\
                                .then_inc(hlo_ok, 1)

            plan = [lambda: front(0), lambda: attention(0), lambda: front(1), experts0, lambda: front(2),
                    lambda: attention(1), lambda: front(3), relative_attention, lambda: front(4), experts1]
            for k, run in enumerate(plan):
                run()
                meet(e, "pool", k + 1)


SHAPES = {
    "x": ([TT * P, P], F32), "ident": ([P, P], F32), "w_qkv": ([P, 3, 5 * P], F32),
    "rope": ([P, 2, L], F32), "w_out": ([P, 3, P], F32), "cols": ([P, 8], F32), "rows": ([P, 3, P], F32),
    "rel": ([P, 3, L], F32), "w_rt0": ([P, 8], F32), "w_rt1": ([P, NE1], F32), "sel0": ([ROWS, NE1], F32),
    "wpT": ([P, 2 * P], F32),
    "gu": ([NE0, P, 2, FI], F32), "dn": ([NE0, P, 3, P], F32), "kv": ([NE1, P, 2, P], F32),
}


def layout(i):
    i = {k: np.asarray(v) for k, v in i.items()}
    half = DH // 2
    swap = np.arange(P).reshape(H, 2, half)[:, ::-1].reshape(-1)
    w0 = i["L0_attn_Wqkv"]
    q0, k0, v0 = w0[:, 0:P], w0[:, P:2 * P], w0[:, 2 * P:3 * P]
    w1 = i["L1_attn_W_qkv"].T
    q1, k1, v1 = w1[:, 0:P], w1[:, P:2 * P], w1[:, 2 * P:3 * P]
    q2, k2, v2 = i["L1_ffn_wq"], i["L1_ffn_wk"], i["L1_ffn_wv"]
    w_qkv = np.stack([np.concatenate([q0, q0[:, swap], k0, k0[:, swap], v0], 1),
                      np.concatenate([q1, q1, k1, k1, v1], 1),
                      np.concatenate([q2, q2, k2, k2, v2], 1)], 1)
    w_out = np.stack([i["L0_attn_Wo"], i["L1_attn_W_out"].T, i["L1_ffn_wo"]], 1)
    b1 = i["L1_attn_b_qkv"]
    cols = np.stack([i["L1_attn_ln_gamma"], i["L1_attn_ln_beta"], b1[0:P], b1[P:2 * P],
                     i["L1_ffn_ln1_g"], i["L1_ffn_ln1_b"], i["L1_ffn_ln2_g"], i["L1_ffn_ln2_b"]], 1)
    rb = np.zeros(P, np.float32)
    rb[0:NE0 - 1] = i["L0_ffn_rb"]
    rows = np.broadcast_to(np.stack([b1[2 * P:3 * P], i["L1_attn_b_out"], rb])[None], (P, 3, P))
    w_rt0 = np.zeros((P, 8), np.float32)
    w_rt0[:, 0:NE0 - 1] = i["L0_ffn_wr"].T
    gate = np.concatenate([i["L0_ffn_sg"][None], i["L0_ffn_rg"]])
    up = np.concatenate([i["L0_ffn_su"][None], i["L0_ffn_ru"]])
    down = np.concatenate([i["L0_ffn_sd"][None], i["L0_ffn_rd"]])
    gu = np.stack([gate.transpose(0, 2, 1), up.transpose(0, 2, 1)], 2)
    dn = np.zeros((NE0, P, 3, P), np.float32)
    for c, (lo, w) in enumerate(FCH):
        dn[:, 0:w, c, :] = down[:, :, lo:lo + w].transpose(0, 2, 1)
    kv = np.stack([i["L1_ffn_keys"], i["L1_ffn_values"]], 2)
    wpT = i["L1_ffn_wp"].T
    swapped = np.concatenate([np.arange(P // 2, P), np.arange(P // 2)])
    rope, rel = tables()
    return {
        "x": i["L0_attn_x"].reshape(TT * P, P), "ident": np.eye(P, dtype=np.float32),
        "w_qkv": w_qkv, "rope": rope, "w_out": w_out, "cols": cols, "rows": rows, "rel": rel, "w_rt0": w_rt0,
        "w_rt1": i["L1_ffn_sel_w"], "sel0": np.tile(np.eye(NE1, dtype=np.float32), (PARTS, 1)),
        "wpT": np.concatenate([wpT, wpT[:, swapped]], 1),
        "gu": gu, "dn": dn, "kv": kv,
    }


def kernel(**inputs):
    import concourse.bacc as bacc
    from concourse.bass_utils import run_bass_kernel_spmd

    arrays = {f"in_{k}": np.ascontiguousarray(v) for k, v in layout(inputs).items()}
    nc = bacc.Bacc("TRN2", target_bir_lowering=False, num_devices=1)
    A = {}
    for name, (shape, dt) in SHAPES.items():
        assert list(arrays[f"in_{name}"].shape) == shape, (name, arrays[f"in_{name}"].shape)
        A[name] = nc.dram_tensor(f"in_{name}", shape, dt, kind="ExternalInput").ap()
    out = nc.dram_tensor("out", [TT * P, P], F32, kind="ExternalOutput").ap()
    two_layers(nc, A, out)
    r = run_bass_kernel_spmd(nc, [arrays], core_ids=[0])
    return np.asarray(r.results[0]["out"]).reshape(NB, L, P)
```
